# Optimizing a Trainium2 kernel written in Bass

```python
import numpy as np
import jax
import jax.numpy as jnp

def _softmax(x, axis=-1):
    return jax.nn.softmax(x, axis=axis)

def _gelu(x):
    return jax.nn.gelu(x, approximate=True)

def _silu(x):
    return jax.nn.silu(x)

def _sigmoid(x):
    return jax.nn.sigmoid(x)

def _layernorm(x, axis=-1, eps=1e-05):
    m = jnp.mean(x, axis=axis, keepdims=True)
    v = jnp.var(x, axis=axis, keepdims=True)
    return (x - m) / jnp.sqrt(v + eps)

def _scatter_add(tgt, idx, src, axis=0):
    return tgt.at[idx].add(src)

def _segment_sum(src, seg, n):
    return jax.ops.segment_sum(src, seg, n)
kernel_name = 'mk_gnn_preln_d4_gnn_r64_25ff53'

def setup_inputs(seed: int=0):
    np.random.seed(seed)
    _w = jnp.asarray

    def _rec_inputs():
        import jax
        import jax.numpy as jnp
        _gk = jax.random.key(seed)
        x = -0.000202 + 1 * jax.random.normal(jax.random.fold_in(_gk, 1), (100000, 64), jnp.float32)
        src = jax.random.randint(jax.random.fold_in(_gk, 2), (50000,), 0, 100000, jnp.int32)
        dst = jax.random.randint(jax.random.fold_in(_gk, 3), (50000,), 0, 100000, jnp.int32)
        _o = jnp.argsort(dst, stable=True)
        src = src[_o]
        dst = dst[_o]
        edge_attr_32 = 0.000216709 + 1.00012 * jax.random.normal(jax.random.fold_in(_gk, 12), (50000, 32), jnp.float32)
        edge_weight = jax.random.uniform(jax.random.fold_in(_gk, 14), (50000,), jnp.float32, 0.0, 1)
        return (x, src, dst, edge_attr_32, edge_weight)
    x, src, dst, edge_attr_32, edge_weight = _rec_inputs()

    def _L0_gnn_setup():
        import jax, jax.numpy as jnp
        import numpy as np
        N_NODES = 100000

        def _spmm(edge_index, edge_weight, x):
            dst, src = (edge_index[0], edge_index[1])
            msgs = edge_weight[:, None] * x[src]
            return jax.ops.segment_sum(msgs, dst, num_segments=N_NODES)
        key = jax.random.key(seed)
        k1, k2, k3, k4 = jax.random.split(key, 4)
        N, E, D = (N_NODES, 50000, 64)
        features = jax.random.normal(k1, (N, D), dtype=jnp.float32)
        edge_weight = jax.random.uniform(k2, (E,), dtype=jnp.float32)
        dst = jax.random.randint(k3, (E,), 0, N)
        src = jax.random.randint(k4, (E,), 0, N)
        edge_index = jnp.stack([dst, src]).astype(jnp.int64)
        return {'features': features, 'edge_weight': edge_weight, 'edge_index': edge_index, 'degree': 2}
    _L0_gnn_all = _L0_gnn_setup()
    _L0_gnn_in = {k: v for k, v in _L0_gnn_all.items() if k in ()}
    del _L0_gnn_all

    def _L1_gnn_setup():
        import jax, jax.numpy as jnp
        import numpy as np
        N = 100000
        M = 25000
        IN_C = 64
        OUT_C = 64
        key = jax.random.key(seed)
        k1, k2, k3 = jax.random.split(key, 3)
        x = jax.random.normal(k1, (N, IN_C), dtype=jnp.float32)
        edge_index = jax.random.randint(k2, (2, M), 0, N, dtype=jnp.int64)
        limit = np.sqrt(6.0 / (IN_C + OUT_C))
        W = jax.random.uniform(k3, (IN_C, OUT_C), dtype=jnp.float32, minval=-limit, maxval=limit)
        b = jnp.zeros((OUT_C,), dtype=jnp.float32)
        return {'x': x, 'edge_index': edge_index, 'W': W, 'b': b}
    _L1_gnn_all = _L1_gnn_setup()
    _L1_gnn_in = {k: v for k, v in _L1_gnn_all.items() if k in ('W', 'b')}
    del _L1_gnn_all

    def _L2_gnn_setup():
        import jax, jax.numpy as jnp
        import numpy as np
        N_NODES = 100000
        N_EDGES = 25000
        DIM = 64
        key = jax.random.key(seed)
        k1, k2, k3, k4 = jax.random.split(key, 4)
        x = jax.random.normal(k1, (N_NODES, DIM), dtype=jnp.float32)
        edge_index = jax.random.randint(k2, (2, N_EDGES), 0, N_NODES, dtype=jnp.int64)
        W1 = jax.random.normal(k3, (DIM, DIM), dtype=jnp.float32) * 0.05
        b1 = jnp.zeros((DIM,), dtype=jnp.float32)
        W2 = jax.random.normal(k4, (DIM, DIM), dtype=jnp.float32) * 0.05
        b2 = jnp.zeros((DIM,), dtype=jnp.float32)
        return {'x': x, 'edge_index': edge_index, 'W1': W1, 'b1': b1, 'W2': W2, 'b2': b2}
    _L2_gnn_all = _L2_gnn_setup()
    _L2_gnn_in = {k: v for k, v in _L2_gnn_all.items() if k in ('W1', 'b1', 'W2', 'b2')}
    del _L2_gnn_all

    def _L3_gnn_setup():
        import jax, jax.numpy as jnp
        import numpy as np
        N_NODES = 50000
        N_EDGES = 12500
        D_NODE = 64
        D_EDGE = 32
        D_HID = 128

        def _mlp(x, W1, b1, W2, b2):
            return jax.nn.relu(x @ W1 + b1) @ W2 + b2
        key = jax.random.key(seed)
        ks = jax.random.split(key, 12)
        inp = {'nodes': jax.random.normal(ks[0], (N_NODES, D_NODE), dtype=jnp.float32), 'row': jax.random.randint(ks[1], (N_EDGES,), 0, N_NODES, dtype=jnp.int32), 'col': jax.random.randint(ks[2], (N_EDGES,), 0, N_NODES, dtype=jnp.int32), 'edge_features': jax.random.normal(ks[3], (N_EDGES, D_EDGE), dtype=jnp.float32)}
        d_in_msg = 2 * D_NODE + D_EDGE
        inp['mW1'] = jax.random.normal(ks[4], (d_in_msg, D_HID), dtype=jnp.float32) / np.sqrt(d_in_msg)
        inp['mb1'] = jnp.zeros((D_HID,), dtype=jnp.float32)
        inp['mW2'] = jax.random.normal(ks[5], (D_HID, D_NODE), dtype=jnp.float32) / np.sqrt(D_HID)
        inp['mb2'] = jnp.zeros((D_NODE,), dtype=jnp.float32)
        d_in_upd = 2 * D_NODE
        inp['uW1'] = jax.random.normal(ks[6], (d_in_upd, D_HID), dtype=jnp.float32) / np.sqrt(d_in_upd)
        inp['ub1'] = jnp.zeros((D_HID,), dtype=jnp.float32)
        inp['uW2'] = jax.random.normal(ks[7], (D_HID, D_NODE), dtype=jnp.float32) / np.sqrt(D_HID)
        inp['ub2'] = jnp.zeros((D_NODE,), dtype=jnp.float32)
        return inp
    _L3_gnn_all = _L3_gnn_setup()
    _L3_gnn_in = {k: v for k, v in _L3_gnn_all.items() if k in ('mW1', 'mb1', 'mW2', 'mb2', 'uW1', 'ub1', 'uW2', 'ub2')}
    del _L3_gnn_all
    return {'x': x, 'src': src, 'dst': dst, 'edge_attr_32': edge_attr_32, 'edge_weight': edge_weight, 'L1_gnn_W': _L1_gnn_in['W'], 'L1_gnn_b': _L1_gnn_in['b'], 'L2_gnn_W1': _L2_gnn_in['W1'], 'L2_gnn_b1': _L2_gnn_in['b1'], 'L2_gnn_W2': _L2_gnn_in['W2'], 'L2_gnn_b2': _L2_gnn_in['b2'], 'L3_gnn_mW1': _L3_gnn_in['mW1'], 'L3_gnn_mb1': _L3_gnn_in['mb1'], 'L3_gnn_mW2': _L3_gnn_in['mW2'], 'L3_gnn_mb2': _L3_gnn_in['mb2'], 'L3_gnn_uW1': _L3_gnn_in['uW1'], 'L3_gnn_ub1': _L3_gnn_in['ub1'], 'L3_gnn_uW2': _L3_gnn_in['uW2'], 'L3_gnn_ub2': _L3_gnn_in['ub2']}

def reference(x, src, dst, edge_attr_32, edge_weight, L1_gnn_W, L1_gnn_b, L2_gnn_W1, L2_gnn_b1, L2_gnn_W2, L2_gnn_b2, L3_gnn_mW1, L3_gnn_mb1, L3_gnn_mW2, L3_gnn_mb2, L3_gnn_uW1, L3_gnn_ub1, L3_gnn_uW2, L3_gnn_ub2):
    import jax
    import jax.numpy as jnp

    def _L0_gnn_ref(features, edge_weight, edge_index, degree):
        import jax, jax.numpy as jnp
        import numpy as np
        N_NODES = 100000

        def _spmm(edge_index, edge_weight, x):
            dst, src = (edge_index[0], edge_index[1])
            msgs = edge_weight[:, None] * x[src]
            return jax.ops.segment_sum(msgs, dst, num_segments=N_NODES)
        x = features
        for _ in range(degree):
            x = _spmm(edge_index, edge_weight, x)
        return x

    def _L1_gnn_ref(x, edge_index, W, b):
        import jax, jax.numpy as jnp
        import numpy as np
        N = 100000
        M = 25000
        IN_C = 64
        OUT_C = 64
        h = x @ W
        n = x.shape[0]
        row, col = (edge_index[0], edge_index[1])
        loop = jnp.arange(n, dtype=edge_index.dtype)
        row = jnp.concatenate([row, loop])
        col = jnp.concatenate([col, loop])
        w = jnp.ones(row.shape[0], dtype=h.dtype)
        deg = jax.ops.segment_sum(w, col, num_segments=n)
        deg_inv_sqrt = deg ** (-0.5)
        deg_inv_sqrt = jnp.where(jnp.isinf(deg_inv_sqrt), 0.0, deg_inv_sqrt)
        norm = deg_inv_sqrt[row] * w * deg_inv_sqrt[col]
        msgs = norm[:, None] * h[row]
        out = jax.ops.segment_sum(msgs, col, num_segments=n)
        return out + b

    def _L2_gnn_ref(x, edge_index, W1, b1, W2, b2):
        import jax, jax.numpy as jnp
        import numpy as np
        N_NODES = 100000
        N_EDGES = 25000
        DIM = 64
        src = edge_index[0]
        dst = edge_index[1]
        agg = jax.ops.segment_sum(x[src], dst, num_segments=x.shape[0])
        h = x + agg
        h = jax.nn.relu(h @ W1.T + b1)
        out = h @ W2.T + b2
        return out

    def _L3_gnn_ref(nodes, row, col, edge_features, mW1, mb1, mW2, mb2, uW1, ub1, uW2, ub2):
        import jax, jax.numpy as jnp
        import numpy as np
        N_NODES = 50000
        N_EDGES = 12500
        D_NODE = 64
        D_EDGE = 32
        D_HID = 128

        def _mlp(x, W1, b1, W2, b2):
            return jax.nn.relu(x @ W1 + b1) @ W2 + b2
        msg_in = jnp.concatenate([nodes[row], nodes[col], edge_features], axis=-1)
        messages = _mlp(msg_in, mW1, mb1, mW2, mb2)
        aggregated = jax.ops.segment_sum(messages, col, num_segments=nodes.shape[0])
        upd_in = jnp.concatenate([nodes, aggregated], axis=-1)
        return _mlp(upd_in, uW1, ub1, uW2, ub2)
    edge_index = jnp.stack([src, dst])
    h = jnp.maximum(_layernorm(x, axis=-1), 0.0)
    x = x + _L0_gnn_ref(h, edge_weight, edge_index, 2)
    h = jnp.maximum(_layernorm(x, axis=-1), 0.0)
    x = x + _L1_gnn_ref(h, edge_index, L1_gnn_W, L1_gnn_b)
    h = jnp.maximum(_layernorm(x, axis=-1), 0.0)
    x = x + _L2_gnn_ref(h, edge_index, L2_gnn_W1, L2_gnn_b1, L2_gnn_W2, L2_gnn_b2)
    h = jnp.maximum(_layernorm(x, axis=-1), 0.0)
    x = x + _L3_gnn_ref(h, src, dst, edge_attr_32, L3_gnn_mW1, L3_gnn_mb1, L3_gnn_mW2, L3_gnn_mb2, L3_gnn_uW1, L3_gnn_ub1, L3_gnn_uW2, L3_gnn_ub2)
    return x

_drawn_inputs = setup_inputs


def setup_inputs(seed=0):
    import zlib

    import numpy as np

    out = dict(_drawn_inputs(seed))
    spreads = {'L1_gnn_b': (0.0, 0.1),
     'L2_gnn_b1': (0.0, 0.37),
     'L2_gnn_b2': (0.0, 0.1),
     'L3_gnn_mb1': (0.0, 0.361),
     'L3_gnn_mb2': (0.0, 0.1),
     'L3_gnn_ub1': (0.0, 0.1),
     'L3_gnn_ub2': (0.0, 0.1)}
    factors = {}
    for name, (base, spread) in spreads.items():
        noise = np.random.default_rng([zlib.crc32(name.encode()), seed]).standard_normal(out[name].shape)
        drawn = base * np.exp(spread * noise) if base else spread * noise
        out[name] = jnp.asarray(drawn.astype(out[name].dtype))
    for name, factor in factors.items():
        out[name] = (out[name] * factor).astype(out[name].dtype)
    return out
```

```python
from contextlib import ExitStack

import concourse.bass as bass
from concourse import mybir

P = 128
N = 100000
E = 50000
D = 64
DE = 32
DH = 128
EC = -(-E // P)
T = EC + 1
ELAST = E - (P - 1) * EC
G = 14
U = T // G
STEPS = U // 2
NU = -(-N // (P * G))
DSTEPS = NU // 2
W = G * D
HB = G // 2
HC = 208
ROWS = P * T
BIG = float(1 << 20)
EPS = 1e-5
assert G == 14 and T % (2 * G) == 0 and NU % 2 == 0 and W % P == 0

F32 = mybir.dt.float32
I32 = mybir.dt.int32
ALU = mybir.AluOpType
ACT = mybir.ActivationFunctionType
X = mybir.AxisListType.X


class Signal:

    def __init__(self, sem, keys):
        self.sem, self.keys, self.next = sem, list(keys), 0

    def at(self, i, key):
        return self.sem, i * len(self.keys) + self.keys.index(key) + 1

    def raise_by(self, instruction, key):
        assert self.keys[self.next % len(self.keys)] == key, (key, self.keys, self.next)
        self.next += 1
        instruction.then_inc(self.sem, 1)

    def raise_now(self, engine, key):
        assert self.keys[self.next % len(self.keys)] == key, (key, self.keys, self.next)
        self.next += 1
        engine.sem_inc(self.sem, 1)


class Settled:

    def __init__(self, engine, passed):
        self.engine, self.passed = engine, passed

    def wait_ge(self, sem, value):
        self.engine.wait_ge(sem, value)
        if not isinstance(value, int):
            self.engine.sem_inc(self.passed, 1)


class Own:

    def __init__(self, engine, sem):
        self.engine, self.sem, self.per, self.k, self.i = engine, sem, 0, 0, 0

    def step(self, i):
        assert not self.per or self.k == self.per
        self.per, self.i, self.k = self.k, i, 0

    def did(self, instruction):
        instruction.then_inc(self.sem, 1)
        self.k += 1
        return self.sem, self.i * self.per + self.k

    def wait(self, *marks):
        for sem, value in marks:
            self.engine.wait_ge(sem, value)


def steps(engine, n, body, last_apart=False):
    body(0, True)
    with engine.Fori(1, n - last_apart) as i:
        body(i, False)
    if last_apart:
        body(n - 1, False)


def gnn(nc, x, src, dst, edge_attr, edge_weight, W1g, b1g, W2a, b2a, W2b, b2b, mW1, mb1, mW2, mb2, uW1, ub1,
        uW2, ub2, out):
    ctx = ExitStack()
    with ctx:
        def sb(name, shape, dt=F32):
            return ctx.enter_context(nc.sbuf_tensor(name, shape, dt))

        def sem(name):
            return ctx.enter_context(nc.semaphore(name))

        def dram(name, shape):
            return nc.dram_tensor(name, shape, F32, kind="Internal").ap()

        tables = [dram(f"table{k}", [ROWS + P, D]) for k in range(2)]
        hop = dram("hop", [N + 2 * P, D])
        x1 = dram("x1", [N + 2 * P, D])
        suffix = dram("suffix", [ROWS, D])
        node_map = dram("node_map", [N, 2])
        xs1, xs2 = (dram(f"xs{k}", [P, T * D]) for k in (1, 2))
        ms1, hs2 = dram("ms1", [P, T * D]), dram("hs2", [P, T * D])

        def rows(t):
            return t[0:ROWS, :].rearrange("(p c) d -> p (c d)", p=P)

        zeros = sb("zeros", [P, G * DE])
        ident = sb("ident", [P, P])
        upper = sb("upper", [P, P])
        ones = sb("ones", [P, P])
        row0 = sb("row0", [P, P])
        eps = sb("eps", [P, 1])
        one = sb("one", [P, 1])
        wg = sb("wg", [P, P])
        w2a = sb("w2a", [P, P])
        w2b = sb("w2b", [P, P])
        m1 = sb("m1", [P, DH])
        m1e = sb("m1e", [P, 4, DH])
        m2 = sb("m2", [P, D])
        u1 = sb("u1", [P, DH])
        u1s = sb("u1s", [P, 2, DH])
        u2 = sb("u2", [P, D])
        bias = sb("bias", [P, 4, 512])
        bcol = sb("bcol", [P, 3])
        BG, B2, BM, BU = range(4)

        dst_i, src_i = (sb(n, [P, T], I32) for n in ("dst_i", "src_i"))
        dst_f = sb("dst_f", [P, T])
        wt = sb("wt", [P, T])
        same = sb("same", [P, T])
        more = sb("more", [P, T])
        last = sb("last", [P, T])
        cont = sb("cont", [P, T])
        flag = sb("flag", [P, T])
        tmp = sb("tmp", [P, T])
        cnt = sb("cnt", [P, T])
        map_idx = sb("map_idx", [P, T], I32)
        out_idx = sb("out_idx", [P, T], I32)
        dstc_i = sb("dstc_i", [P, T], I32)
        ptr_i = sb("ptr_i", [P, T], I32)
        rowno = sb("rowno", [P, T])
        map_rows = sb("map_rows", [P, T, 2])
        src_map = map_rows
        dis_s = sb("dis_s", [P, T])
        dis_d = sb("dis_d", [P, T])
        kn_i = sb("kn_i", [P, 1], I32)
        small = sb("small", [P, 24])
        head_i, tail_i, brd_i = (sb(n, [P, 1], I32) for n in ("head_i", "tail_i", "brd_i"))
        diag = sb("diag", [P, 2, P])
        kf = sb("kf", [P, 2, P])
        mh, mt1, mt2 = (sb(n, [P, P]) for n in ("mh", "mt1", "mt2"))

        def pair(name, shape, dt=F32):
            return [sb(f"{name}{b}", shape, dt) for b in range(2)]

        unit = [P, G, D]
        xin, hin, xw, h, vt, zz, ga = (pair(n, unit) for n in ("xin", "hin", "xw", "h", "vt", "zz", "ga"))
        acc = pair("acc", unit)
        us = pair("us", unit)
        wide = pair("wide", [P, 4, G, D])
        a3, a4, gx, xd = ([wide[b][:, k] for b in range(2)] for k in range(4))
        equal = [t[:, :, :, :].rearrange("p k g d -> p (k g d)").rearrange("p (g m) -> p g m", g=G) for t in wide]
        lower = sb("lower", [P, 2, 2 * P])
        kslot, krow = pair("kslot", [P, G]), pair("krow", [G, P])
        dups = pair("dups", [P, G])
        kidx = sb("kidx", [P, T], I32)
        key = sb("key", [P, T])
        spare = sb("spare", [P, T])
        x3 = pair("x3", unit)
        xc, sq, st = pair("xc", unit), pair("sq", unit), pair("st", [P, 4, G])
        cc = pair("cc", [P, G, 3 * D])
        pick = cc[0][0:G, :, :].rearrange("p g d -> p (g d)")[:, 0:G * P].rearrange("p (g m) -> p g m", g=G)
        ef = pair("ef", [P, G, DE])
        eft = pair("eft", [P, 512])
        isl, isl2, osl = (pair(n, [P, G], I32) for n in ("isl", "isl2", "osl"))
        msl = pair("msl", [P, G, 2])
        hsum = sb("hsum", [P, D])
        fix = sb("fix", [P, 2 * D])
        brd = sb("brd", [P, 3 * D])
        bz = sb("bz", [P, 2 * P])

        nxt_f, prv_f = (xc[b][:, :, :].rearrange("p g d -> p (g d)")[:, 0:T] for b in range(2))
        nxt_i, prv_i = (sq[b][:, :, :].rearrange("p g d -> p (g d)")[:, 0:T].bitcast(I32) for b in range(2))

        tp = [ctx.enter_context(nc.psum_tensor(f"tp{b}", [P, 1024], F32)) for b in range(2)]
        mm = [ctx.enter_context(nc.psum_tensor(f"mm{b}", [P, 1024], F32)) for b in range(2)]

        def flat(t, n=W):
            return (t if isinstance(t, bass.AP) else t[:, :, :]).rearrange("p g d -> p (g d)")[:, 0:n]

        def cols(ap, c, n=G):
            return ap[:, bass.ds(c, n)].unsqueeze(2).broadcast_to([P, n, D])

        def stat(q, k):
            return st[q][:, k, :].unsqueeze(2).broadcast_to([P, G, D])

        s_const = sem("constants_ready")
        s_zero = sem("zeros_ready")
        s_pad = sem("padding_written")
        s_edges = sem("edges_loaded")
        s_weights = sem("weights_loaded")
        s_cleared = sem("map_and_zero_rows_cleared")
        s_rowno = sem("row_numbers_ready")
        s_prep = sem("dve_prep_done")
        s_diag = sem("diagonals_ready")
        s_kfp = sem("key_rows_in_psum")
        s_mats = sem("span_matrices_ready")
        s_cc = sem("count_carries_in_psum")
        s_mapin = sem("map_rows_ready")
        s_maps = [sem(f"map_scattered{b}") for b in range(2)]
        s_slot = sem("pool_slot_copied")
        s_mapg = [sem(f"map_gathered{b}") for b in range(2)]
        s_mapv = sem("source_map_ready")
        s_ptr = sem("pointers_ready")
        s_deg = sem("degrees_ready")
        s_root = sem("degree_roots_ready")
        s_dense = [sem(f"dense_rows_stored{b}") for b in range(2)]
        s_phase = sem("dve_phase_done")
        s_head = sem("head_sums_gathered")
        s_span = sem("span_sums_in_psum")
        s_fix = sem("span_sums_ready")
        s_fixed = sem("table_complete")
        s_final = sem("final_scattered")
        s_hop_init = sem("hop_cleared")
        s_x1_init = sem("x1_started")
        HALF = [range(0, 8), range(8, G)]
        s_own = sem("dve_prep_own")
        s_fixpart = sem("first_node_sums_ready")
        s_saved = sem("last_nodes_saved")
        WEIGHTS = 12 + 4 + 4 * (512 // D) + 4

        B2K = [0, 1]

        def per_unit(*names):
            return [(n, b) for n in names for b in B2K]

        class Phase:

            def __init__(self, name, lns, rows_,
                         turned=None, copied=None, product=None, hidden=None, second=None,
                         taken=None, message=None, slot=None, krow=None, picked=None,
                         compared=None, merged=None, sums=None, ga_free=None, gx_free=None,
                         in_free=None, xin_free=None, state_ready=None, acc_ready=None,
                         out_ready=None, o_ready=None):
                def signal(kind, keys):
                    return Signal(sem(f"{name}_{kind}"), keys) if keys else None

                ln = [(n, q) for n, qs in lns for q in qs]
                self.dve = sem(name + "_dve_own")
                self.centred, self.squared = signal("centred", ln), signal("squared", ln)
                self.variance, self.deviation = signal("variance", ln), signal("deviation", ln)
                self.rows = signal("rows_ready", rows_)
                self.turned = signal("turned", turned)
                self.copied = signal("copied", copied)
                self.product = signal("product", product)
                self.hidden = signal("hidden", hidden)
                self.second = signal("second", second)
                self.taken = signal("taken", taken)
                self.message = signal("message", message)
                self.slot = signal("slot", slot)
                self.krow = signal("krow", krow)
                self.picked = signal("picked", picked)
                self.compared = signal("compared", compared)
                self.merged = signal("merged", merged)
                self.sums = signal("sums", sums)
                self.ga_free = signal("ga_free", ga_free)
                self.gx_free = signal("gx_free", gx_free)
                self.in_free = signal("in_free", in_free)
                self.xin_free = signal("xin_free", xin_free)
                self.state_ready = signal("state_ready", state_ready)
                self.acc_ready = signal("acc_ready", acc_ready)
                self.out_ready = signal("out_ready", out_ready)
                self.o_ready = signal("o_ready", o_ready)

        dn = Phase("dense", [("l1", B2K), ("l2", B2K), ("l3", B2K)], per_unit("h1", "h2", "h3"),
                   turned=per_unit("h1", "h2", "h3"), copied=per_unit("h1", "h2", "h3"),
                   product=per_unit("h1", "h2", "even", "odd"),
                   hidden=per_unit("h2", "even", "odd"), second=per_unit("h2", "even", "odd"),
                   taken=per_unit("x2", "x3", "even", "odd"),
                   xin_free=per_unit("x"), out_ready=per_unit("o"))
        dn_load = [sem(f"dense_loaded{b}") for b in range(2)]

        hops = []
        for k in range(2):
            f = Phase(f"hop{k}", [("l", B2K)] if k == 0 else [], per_unit("m"),
                      slot=per_unit("k"), turned=per_unit("k"), krow=per_unit("k"),
                      picked=[("k", b, j) for b in B2K for j in B2K], compared=[("k", b, j) for b in B2K for j in B2K],
                      merged=per_unit("m"), sums=per_unit("m"))
            f.got = [sem(f"hop{k}_gathered{b}") for b in B2K]
            f.added = sem(f"hop{k}_added")
            hops.append(f)

        sp_ = []
        for k in range(2):
            v = per_unit("v") if k == 1 else None
            f = Phase(f"s{k}", [("l", B2K)], v, turned=v, copied=v, product=v, taken=v,
                      ga_free=per_unit("g"), in_free=per_unit("x") if k == 1 else None,
                      state_ready=per_unit("x"), acc_ready=per_unit("a"))
            f.got = [sem(f"s{k}_gathered{b}") for b in B2K]
            f.load = [sem(f"s{k}_loaded{b}") for b in B2K] if k == 1 else None
            f.stored = [sem(f"s{k}_sums_stored{b}") for b in B2K]
            f.kept = [sem(f"s{k}_state_stored{b}") for b in B2K]
            sp_.append(f)

        T_TURNED = per_unit("ef", "us", "vd", "ud", "m0", "m1", "u0", "u1")
        T_MLP = per_unit("us", "ud", "m0", "m1", "u0", "u1")
        tt = Phase("t", [("d1", B2K), ("d2", B2K), ("s3", B2K), ("d3", B2K)],
                   per_unit("us", "vd", "ud", "h3", "agg"),
                   turned=T_TURNED, copied=T_TURNED,
                   product=per_unit("us", "vd", "ud", "m0", "m1", "u0", "u1"),
                   hidden=T_MLP, second=T_MLP, message=per_unit("m0", "m1"),
                   taken=per_unit("us", "vd", "ud", "u0", "u1"),
                   in_free=per_unit("x"), gx_free=per_unit("g"), ga_free=per_unit("g"), o_ready=per_unit("o"))
        tt.load = [sem(f"t_loaded{b}") for b in range(2)]
        tt.got_a = [sem(f"t_sums_gathered{b}") for b in range(2)]
        tt.got_x = [sem(f"t_nodes_gathered{b}") for b in range(2)]
        tt.kept = [sem(f"t_suffix_stored{b}") for b in range(2)]
        tt.written = [sem(f"t_rows_written{b}") for b in range(2)]
        s_border = sem("border_dve_steps")
        s_bpe = sem("border_products")

        block = ctx.enter_context(nc.Block())

        def drow(i, b):
            if isinstance(i, int):
                return min((2 * i + b) * P * G, N - P * G)
            return (2 * i + b) * (P * G)

        def ecol(i, b):
            return (2 * i + b) * G

        def tcol(i, b):
            return (U - 1 - b) * G - 2 * G * i

        @block.sync
        def _(sp):
            after = Settled(sp, sem("sp_waits_passed"))
            n = (P - 1) * EC
            after.wait_ge(s_pad, 7)
            for t, s in ((dst_i, dst), (src_i, src), (wt, edge_weight)):
                sp.dma_start(t[0:P - 1, 0:EC], s[0:n].rearrange("(p c) -> p c", c=EC)).then_inc(s_edges, 16)
                sp.dma_start(t[P - 1:P, 0:ELAST], s[n:E].rearrange("(p c) -> p c", p=1)).then_inc(s_edges, 16)
            sp.dma_start(nxt_i[0:P - 1, 0:EC], dst[1:n + 1].rearrange("(p c) -> p c", c=EC)).then_inc(s_edges, 16)
            sp.dma_start(nxt_i[P - 1:P, 0:ELAST - 1], dst[n + 1:E].rearrange("(p c) -> p c", p=1)).then_inc(s_edges, 16)
            sp.dma_start(prv_i[0:1, 1:EC], dst[0:EC - 1].rearrange("(p c) -> p c", p=1)).then_inc(s_edges, 16)
            sp.dma_start(prv_i[1:P - 1, 0:EC], dst[EC - 1:n - 1].rearrange("(p c) -> p c", c=EC)).then_inc(s_edges, 16)
            sp.dma_start(prv_i[P - 1:P, 0:ELAST], dst[n - 1:E - 1].rearrange("(p c) -> p c", p=1)).then_inc(s_edges, 16)
            with nc.allow_non_contiguous_dma(reason="126 single keys"):
                sp.dma_start(kn_i[0:P - 2, :], dst[EC:n].rearrange("(p c) -> p c", c=EC)[:, EC - 1:EC]).then_inc(s_edges, 16)
            after.wait_ge(s_zero, 1)
            cleared = node_map.rearrange("(p a) b -> p (a b)", p=125)
            for j in range(4):
                w = 2 * N // 125 // 4
                sp.dma_start(cleared[:, j * w:j * w + w], zeros[0:125, 0:w]).then_inc(s_cleared, 16)
            cleared = hop.rearrange("a b -> (a b)").rearrange("(p k w) -> p k w", p=P, k=HC)
            w = (N + 2 * P) * D // P // HC
            sp.dma_start(cleared, zeros[:, 0:w].unsqueeze(1).broadcast_to([P, HC, w])).then_inc(s_hop_init, 16)
            for j in range(4):
                at = slice(j * N // 4, (j + 1) * N // 4)
                sp.dma_start(x1[at, :], x[at, :]).then_inc(s_x1_init, 16)
            sp.dma_start(x1[N:N + 2 * P, :].rearrange("(p a) d -> p (a d)", p=P), zeros[:, 0:2 * D]).then_inc(s_x1_init, 16)
            for t in tables:
                sp.dma_start(t[ROWS:ROWS + P, :], zeros[:, 0:D]).then_inc(s_cleared, 16)
            after.wait_ge(s_const, 1)
            lo, hi = slice(0, D), slice(D, P)
            for o, s in ((wg[lo, 0:D], W1g), (wg[hi, D:P], W1g), (w2a[lo, 0:D], W2a), (w2a[hi, D:P], W2a),
                         (w2b[lo, 0:D], W2b), (w2b[hi, D:P], W2b), (m1[:, :], mW1[0:P, :]), (m2[:, :], mW2),
                         (u1[:, :], uW1), (u1s[lo, 0, :], uW1[0:D, :]), (u1s[hi, 1, :], uW1[0:D, :]),
                         (u2[:, :], uW2)):
                sp.dma_start(o, s).then_inc(s_weights, 16)
            for j in range(4):
                sp.dma_start(m1e[DE * j:DE * j + DE, j, :], mW1[P:P + DE, :]).then_inc(s_weights, 16)
            for j, v in enumerate((b1g, b2b, mb2, ub2)):
                for r in range(512 // D):
                    sp.dma_start(bias[0:1, j, r * D:r * D + D], v.rearrange("(p d) -> p d", p=1)).then_inc(s_weights, 16)
            with nc.allow_non_contiguous_dma(reason="bias columns"):
                for o, v in ((bcol[lo, 0:1], b2a), (bcol[hi, 0:1], b2a), (bcol[:, 1:2], mb1), (bcol[:, 2:3], ub1)):
                    sp.dma_start(o, v.rearrange("(d p) -> d p", p=1)).then_inc(s_weights, 16)

            def node_rows(t, i, b):
                return t[bass.ds(drow(i, b), P * G), :].rearrange("(p g) d -> p g d", g=G)

            def dense_load(i, b):
                sp.dma_start(xin[b][:, :, :], node_rows(x1, i, b)).then_inc(dn_load[b], 16)

            def dense(i, first, more_steps=True):
                for b in B2K:
                    if more_steps:
                        after.wait_ge(*dn.xin_free.at(i, ("x", b)))
                        dense_load(i + 1, b)
                for b in B2K:
                    after.wait_ge(*dn.out_ready.at(i, ("o", b)))
                    if not more_steps and b == 1:
                        after.wait_ge(s_dense[0], 16 * DSTEPS)
                    sp.dma_start(node_rows(out, i, b), acc[b][:, :, :]).then_inc(s_dense[b], 16)

            for k, f in enumerate(sp_):
                def load(i, b):
                    for t, s in ((xin, xs1), (hin, ms1)):
                        sp.dma_start(flat(t[b]), s[:, bass.ds(ecol(i, b) * D, W)]).then_inc(f.load[b], 16)

                def body(i, more_steps=True):
                    for b in B2K:
                        if more_steps and k == 1:
                            after.wait_ge(*f.in_free.at(i, ("x", b)))
                            load(i + 1, b)
                    for b in B2K:
                        at = bass.ds(ecol(i, b) * D, W)
                        after.wait_ge(*f.state_ready.at(i, ("x", b)))
                        state, rest = ((ga, xs1), (h, ms1)) if k == 0 else ((xw, xs2), (h, hs2))
                        for t, s in (state, rest):
                            sp.dma_start(s[:, at], flat(t[b])).then_inc(f.kept[b], 16)
                        after.wait_ge(*f.acc_ready.at(i, ("a", b)))
                        sp.dma_start(rows(tables[k])[:, at], flat(acc[b])).then_inc(f.stored[b], 16)

                if k == 1:
                    for b in B2K:
                        after.wait_ge(sp_[0].kept[b], 16 * STEPS * 2)
                        load(0, b)
                body(0)
                with sp.Fori(1, STEPS - 1) as i:
                    body(i)
                body(STEPS - 1, False)

            after.wait_ge(s_phase, 2)
            for b in B2K:
                dense_load(0, b)
            dense(0, True)
            with sp.Fori(1, DSTEPS - 2) as i:
                dense(i, False)
            dense(DSTEPS - 2, False)
            dense(DSTEPS - 1, False, False)

            def t_load(i, b):
                at = bass.ds(tcol(i, b) * D, W)
                for t, s in ((xin, xs2), (hin, hs2), (a3, rows(tables[0])), (a4, rows(tables[1]))):
                    sp.dma_start(flat(t[b]), s[:, at]).then_inc(tt.load[b], 16)
                n = (P - 1) * EC
                c = tcol(i, b)
                first = isinstance(i, int) and i == 0 and b == 0
                w = G - 1 if first else G
                sp.dma_start(ef[b][0:P - 1, 0:w, :],
                             edge_attr[0:n, :].rearrange("(p c) d -> p (c d)", c=EC)[:, bass.ds(c * DE, w * DE)]
                             .rearrange("p (c d) -> p c d", d=DE)).then_inc(tt.load[b], 16)
                tail(i, b, c)

            def tail(i, b, c):
                n = (P - 1) * EC
                left = ELAST - c if isinstance(c, int) else G
                w = max(0, min(G, left))
                if w:
                    sp.dma_start(ef[b][P - 1:P, 0:w, :],
                                 edge_attr[n:E, :].rearrange("(p c) d -> p (c d)", p=1)[:, bass.ds(c * DE, w * DE)]
                                 .rearrange("p (c d) -> p c d", d=DE)).then_inc(tt.load[b], 16)
                else:
                    sp.dma_start(ef[b][P - 1:P, :, :],
                                 zeros[P - 1:P, 0:G * DE].rearrange("p (c d) -> p c d", d=DE)).then_inc(tt.load[b], 16)

            def t_body(i, more_steps=True):
                for b in B2K:
                    if more_steps:
                        after.wait_ge(*tt.in_free.at(i, ("x", b)))
                        t_load(i + 1, b)
                for b in B2K:
                    after.wait_ge(*tt.rows.at(i, ("agg", b)))
                    sp.dma_start(rows(suffix)[:, bass.ds(tcol(i, b) * D, W)].rearrange("p (g d) -> p g d", d=D),
                                 cc[b][:, :, 2 * D:3 * D]).then_inc(tt.kept[b], 16)

            after.wait_ge(s_phase, 3)
            after.wait_ge(s_fixed, 2 * 32)
            for b in B2K:
                after.wait_ge(sp_[1].kept[b], 16 * STEPS * 2)
            for b in B2K:
                t_load(0, b)
            apart = 2
            for i in range(apart):
                t_body(i)
            with sp.Fori(apart, STEPS - 1) as i:
                t_body(i)
            t_body(STEPS - 1, False)
            for b in B2K:
                after.wait_ge(s_dense[b], 16 * DSTEPS)
                after.wait_ge(tt.kept[b], 16 * STEPS)
                after.wait_ge(tt.written[b], 16 * G * STEPS)
            after.wait_ge(s_final, 16)

        @block.gpsimd
        def _(pool):
            after = Settled(pool, sem("pool_waits_passed"))
            nc.gpsimd.memset(zeros[:, :], 0.0).then_inc(s_zero, 1)
            for t, v in ((dst_i, N), (nxt_i, N), (prv_i, -1), (src_i, 0), (kn_i, N)):
                nc.gpsimd.memset(t[:, :], v).then_inc(s_pad, 1)
            nc.gpsimd.memset(wt[:, :], 0.0).then_inc(s_pad, 1)
            nc.gpsimd.memset(ef[0][:, :, :], 0.0).then_inc(s_pad, 1)
            nc.gpsimd.memset(ones[:, :], 1.0).then_inc(s_rowno, 1)
            nc.gpsimd.iota(rowno[:, :], pattern=[[1, T]], base=0, channel_multiplier=T,
                           allow_small_or_imprecise_dtypes=True).then_inc(s_rowno, 1)
            after.wait_ge(s_rowno, 1)
            nc.gpsimd.affine_select(out=ident[:, :], in_=ones[:, :], pattern=[[-1, P]], base=0, channel_multiplier=1,
                                    compare_op=ALU.is_equal, fill=0.0).then_inc(s_rowno, 1)
            nc.gpsimd.affine_select(out=upper[:, :], in_=ones[:, :], pattern=[[1, P]], base=0, channel_multiplier=-1,
                                    compare_op=ALU.is_gt, fill=0.0).then_inc(s_rowno, 1)
            nc.gpsimd.affine_select(out=row0[:, :], in_=ones[:, :], pattern=[[0, P]], base=0, channel_multiplier=1,
                                    compare_op=ALU.is_equal, fill=0.0).then_inc(s_rowno, 1)
            for j in range(2):
                nc.gpsimd.affine_select(out=lower[:, j, 0:P], in_=ones[:, :], pattern=[[-1, P]], base=j * P,
                                        channel_multiplier=1, compare_op=ALU.is_gt, fill=0.0).then_inc(s_rowno, 1)
                nc.gpsimd.affine_select(out=lower[:, j, P:2 * P], in_=ones[:, :], pattern=[[-1, P]], base=(j - 1) * P,
                                        channel_multiplier=1, compare_op=ALU.is_gt, fill=0.0).then_inc(s_rowno, 1)
            nc.gpsimd.memset(pick[:, :, :], 1.0).then_inc(s_rowno, 1)
            after.wait_ge(s_rowno, 10)
            nc.gpsimd.affine_select(out=pick[:, :, :], in_=pick[:, :, :], pattern=[[-1, G], [0, P]], base=0,
                                    channel_multiplier=1, compare_op=ALU.is_equal, fill=0.0).then_inc(s_rowno, 1)
            nc.gpsimd.iota(spare[:, :], pattern=[[0, T // 2], [P, 2]], base=N, channel_multiplier=1,
                           allow_small_or_imprecise_dtypes=True).then_inc(s_rowno, 1)
            nodes_max = pool.to_reg(N - 1)
            rows_max = pool.to_reg(ROWS + P - 1)

            def slot_copy(o, i_):
                return nc.gpsimd.tensor_copy(o, i_).then_inc(s_slot, 1)

            after.wait_ge(s_mapin, 1)
            after.wait_ge(s_cleared, 6 * 16)

            def map_scatter(i, first):
                for b in B2K:
                    if not first:
                        after.wait_ge(s_maps[b], 16 * G * i)
                    slot_copy(isl[b][:, :], map_idx[:, bass.ds(ecol(i, b), G)])
                    slot_copy(msl[b][:, :, :], map_rows[:, bass.ds(ecol(i, b), G), :])
                    after.wait_ge(s_slot, 4 * i + 2 * b + 2)
                    for g in range(G):
                        nc.gpsimd.indirect_dma_start(
                            node_map, bass.IndirectOffsetOnAxis(isl[b][:, g:g + 1], 0), msl[b][:, g, :], None,
                            bounds_check=nodes_max, oob_is_err=False).then_inc(s_maps[b], 16)

            steps(pool, STEPS, map_scatter)
            base = 4 * STEPS
            for b in B2K:
                after.wait_ge(s_maps[b], 16 * G * STEPS)

            def map_gather(i, first):
                for b in B2K:
                    if not first:
                        after.wait_ge(s_mapg[b], 16 * G * i)
                        nc.gpsimd.tensor_copy(src_map[:, bass.ds(ecol(i - 1, b), G), :], msl[b][:, :, :]).then_inc(s_mapv, 1)
                        after.wait_ge(s_mapv, 2 * (i - 1) + b + 1)
                    slot_copy(isl[b][:, :], src_i[:, bass.ds(ecol(i, b), G)])
                    after.wait_ge(s_slot, base + 2 * i + b + 1)
                    for g in range(G):
                        nc.gpsimd.indirect_dma_start(
                            msl[b][:, g, :], None, node_map, bass.IndirectOffsetOnAxis(isl[b][:, g:g + 1], 0),
                            bounds_check=nodes_max, oob_is_err=False).then_inc(s_mapg[b], 16)

            steps(pool, STEPS, map_gather)
            base += 2 * STEPS
            for b in B2K:
                after.wait_ge(s_mapg[b], 16 * G * STEPS)
                nc.gpsimd.tensor_copy(src_map[:, ecol(STEPS - 1, b):ecol(STEPS - 1, b) + G, :], msl[b][:, :, :]).then_inc(s_mapv, 1)

            def gather(o, table, idx, limit, s, columns=range(G)):
                for g in columns:
                    nc.gpsimd.indirect_dma_start(
                        o[:, g, :], None, table, bass.IndirectOffsetOnAxis(idx[:, g:g + 1], 0),
                        bounds_check=limit, oob_is_err=False).then_inc(s, 16)

            spare_max = pool.to_reg(N + 2 * P - 1)
            for k, f in enumerate(hops):
                table, sums = (x, hop) if k == 0 else (hop, x1)
                after.wait_ge(*((s_hop_init, 16) if k == 0 else (s_x1_init, 5 * 16)))
                for b in B2K:
                    slot_copy(isl[b][:, :], dstc_i[:, b * G:b * G + G])
                    after.wait_ge(s_slot, base + b + 1)
                    gather(ga[b], table, isl[b], nodes_max, f.got[b])
                base += 2

                def body(i, more_steps=True):
                    for b in B2K:
                        after.wait_ge(*f.sums.at(i, ("m", b)))
                        slot_copy(osl[b][:, :], kidx[:, bass.ds(ecol(i, b), G)])
                        if more_steps:
                            slot_copy(isl[b][:, :], dstc_i[:, bass.ds(ecol(i + 1, b), G)])
                        after.wait_ge(s_slot, base + 4 * i + 2 * b + 2 if more_steps else base + 4 * i + b + 1)
                        for q in range(HB):
                            if not (isinstance(i, int) and i == 0 and b == 0 and q == 0):
                                after.wait_ge(f.added, 32 * ((2 * i + b) * HB + q))
                            for g in (2 * q, 2 * q + 1):
                                nc.gpsimd.indirect_dma_start(
                                    sums, bass.IndirectOffsetOnAxis(osl[b][:, g:g + 1], 0), acc[b][:, g, :], None,
                                    bounds_check=spare_max, oob_is_err=True, compute_op=ALU.add).then_inc(f.added, 16)
                            if more_steps:
                                gather(ga[b], table, isl[b], nodes_max, f.got[b], (2 * q, 2 * q + 1))

                body(0)
                with pool.Fori(1, STEPS - 1) as i:
                    body(i)
                body(STEPS - 1, False)
                base += 4 * STEPS - 2
                after.wait_ge(f.added, 16 * G * U)

            for k, f in enumerate(sp_):
                if k == 0:
                    table, index, limit = x1, src_i, nodes_max
                else:
                    table, index, limit = tables[k - 1], ptr_i, rows_max
                    after.wait_ge(s_ptr, 1)
                    for b in B2K:
                        after.wait_ge(sp_[0].kept[b], 2 * 16 * STEPS)

                def body(i, first):
                    for b in B2K:
                        if not first:
                            after.wait_ge(*f.ga_free.at(i - 1, ("g", b)))
                            if k == 0:
                                after.wait_ge(f.kept[b], 2 * 16 * i)
                        slot_copy(isl[b][:, :], index[:, bass.ds(ecol(i, b), G)])
                        after.wait_ge(s_slot, base + 2 * i + b + 1)
                        gather(ga[b], table, isl[b], limit, f.got[b])

                steps(pool, STEPS, body)
                base += 2 * STEPS
                for b in B2K:
                    after.wait_ge(f.stored[b], 16 * STEPS)
                if k == 0:
                    after.wait_ge(s_prep, 1)
                nc.gpsimd.indirect_dma_start(hsum[:, :], None, tables[k], bass.IndirectOffsetOnAxis(head_i[:, :], 0),
                                             bounds_check=rows_max, oob_is_err=False).then_inc(s_head, 16)
                after.wait_ge(s_fix, k + 1)
                nc.gpsimd.indirect_dma_start(tables[k], bass.IndirectOffsetOnAxis(head_i[:, :], 0), fix[:, 0:D], None,
                                             bounds_check=rows_max, oob_is_err=False).then_inc(s_fixed, 16)
                pool.dma_start(rows(tables[k])[:, EC * D:T * D], fix[:, D:2 * D]).then_inc(s_fixed, 16)
                after.wait_ge(s_fixed, 32 * (k + 1))

            def t_gather(i, first):
                for b in B2K:
                    if not first:
                        after.wait_ge(*tt.ga_free.at(i - 1, ("g", b)))
                        after.wait_ge(*tt.gx_free.at(i - 1, ("g", b)))
                    slot_copy(isl[b][:, :], ptr_i[:, bass.ds(tcol(i, b), G)])
                    slot_copy(isl2[b][:, :], dstc_i[:, bass.ds(tcol(i, b), G)])
                    if first:
                        after.wait_ge(s_slot, base + 2 * b + 2)
                    else:
                        after.wait_ge(s_slot, base + 6 * (i - 1) + 4 + 2 * b + 2)
                    gather(gx[b], x1, isl2[b], nodes_max, tt.got_x[b])
                    gather(ga[b], tables[1], isl[b], rows_max, tt.got_a[b])

            def t_scatter(i, first=False, more_steps=True):
                for b in B2K:
                    after.wait_ge(*tt.o_ready.at(i, ("o", b)))
                    if not first:
                        after.wait_ge(tt.written[b], 16 * G * i)
                    slot_copy(osl[b][:, :], out_idx[:, bass.ds(tcol(i, b), G)])
                    after.wait_ge(s_slot, base + 6 * i + 4 + (4 if more_steps else 0) + b + 1)
                    for g in range(G):
                        nc.gpsimd.indirect_dma_start(
                            out, bass.IndirectOffsetOnAxis(osl[b][:, g:g + 1], 0), acc[b][:, g, :], None,
                            bounds_check=nodes_max, oob_is_err=False).then_inc(tt.written[b], 16)

            for b in B2K:
                after.wait_ge(s_dense[b], 16 * DSTEPS)
            t_gather(0, True)
            t_gather(1, False)
            t_scatter(0, True)
            with pool.Fori(1, STEPS - 1) as i:
                t_gather(i + 1, False)
                t_scatter(i)
            t_scatter(STEPS - 1, more_steps=False)
            for b in B2K:
                after.wait_ge(tt.kept[b], 16 * STEPS)
            nc.gpsimd.indirect_dma_start(hsum[:, :], None, suffix, bass.IndirectOffsetOnAxis(tail_i[:, :], 0),
                                         bounds_check=rows_max, oob_is_err=False).then_inc(s_head, 16)
            after.wait_ge(s_border, 5)
            nc.gpsimd.indirect_dma_start(out, bass.IndirectOffsetOnAxis(brd_i[:, :], 0), fix[:, 0:D], None,
                                         bounds_check=nodes_max, oob_is_err=False).then_inc(s_final, 16)


        @block.tensor
        def _(pe):
            def turn(b, blocks, signal, key):
                for j, blk in enumerate(blocks):
                    w = blk.shape[1]
                    t = nc.tensor.transpose(tp[b][0:w, j * P:j * P + P], blk, ident[:, :])
                signal.raise_by(t, key)

            def product(o, weights, b, extra=None, signal=None, key=None):
                for c in range(0, W, 512):
                    n = min(512, W - c)
                    t = nc.tensor.matmul(o[:, c:c + n], weights, flat(vt[b])[:, c:c + n], start=True, stop=extra is None)
                    if extra is not None:
                        for j in range(c // P, (c + n) // P):
                            g = extra + j
                            t = nc.tensor.matmul(o[:, j * P:j * P + P], m1e[:, g % 4, :],
                                                 eft[b][:, (g // 4) * P:(g // 4) * P + P],
                                                 start=False, stop=j == (c + n) // P - 1)
                signal.raise_by(t, key)

            def by_row(o, src_, weights, k, signal, key):
                w = weights.shape[1]
                for c in range(0, HB * w, 512):
                    n = min(512, HB * w - c)
                    nc.tensor.matmul(o[:, c:c + n], row0[:, :], bias[:, k, 0:n], start=True, stop=False)
                    for j in range(c // w, (c + n) // w):
                        t = nc.tensor.matmul(o[:, j * w:j * w + w], src_[:, j * P:j * P + P], weights,
                                             start=False, stop=j == (c + n) // w - 1)
                signal.raise_by(t, key)

            pe.wait_ge(s_diag, 2)
            nc.tensor.matmul(tp[0][:, 0:P], ones[:, :], diag[:, 0, :], start=True, stop=True)
            nc.tensor.matmul(tp[0][:, P:2 * P], ones[:, :], diag[:, 1, :], start=True, stop=True).then_inc(s_kfp, 1)
            pe.wait_ge(s_mats, 1)
            nc.tensor.matmul(tp[1][:, 0:1], mh[:, :], small[:, 5:6], start=True, stop=True)
            nc.tensor.matmul(tp[1][:, 1:2], mt1[:, :], small[:, 5:6], start=True, stop=False)
            nc.tensor.matmul(tp[1][:, 1:2], mt2[:, :], small[:, 4:5], start=False, stop=True).then_inc(s_cc, 1)
            pe.wait_ge(s_weights, WEIGHTS * 16)
            pe.wait_ge(s_prep, 1)

            def span(k, tails, heads):
                nc.tensor.matmul(tp[0][:, 0:D], mh[:, :], tails, start=True, stop=True)
                nc.tensor.matmul(tp[0][:, D:2 * D], mt1[:, :], tails, start=True, stop=False)
                nc.tensor.matmul(tp[0][:, D:2 * D], mt2[:, :], heads, start=False, stop=True).then_inc(s_span, 1)

            for k, f in enumerate(hops):
                def body(i, first):
                    for b in B2K:
                        pe.wait_ge(*f.slot.at(i, ("k", b)))
                        f.turned.raise_by(nc.tensor.transpose(tp[b][0:G, W:W + P], kslot[b][:, :], ident[:, :]), ("k", b))
                    for b in B2K:
                        pe.wait_ge(*f.krow.at(i, ("k", b)))
                        for j, columns in enumerate(HALF):
                            if b == 1:
                                pe.wait_ge(*f.compared.at(i, ("k", 0, j)))
                            elif not first:
                                pe.wait_ge(*f.compared.at(i - 1, ("k", 1, j)))
                            for g in columns:
                                t = nc.tensor.matmul(mm[j][:, (g - columns[0]) * P:(g - columns[0] + 1) * P], pick[:, g, :],
                                                     krow[b][:, :], start=True, stop=True)
                            f.picked.raise_by(t, ("k", b, j))
                    for b in B2K:
                        pe.wait_ge(*f.compared.at(i, ("k", b, 1)))
                        pe.wait_ge(*f.rows.at(i, ("m", b)))
                        if not first:
                            pe.wait_ge(*f.sums.at(i - 1, ("m", b)))
                        for g in range(G):
                            for n in range(2):
                                o = g - g % 2 + n
                                t = nc.tensor.matmul(tp[b][:, g * D:g * D + D], equal[b][:, o, (g % 2) * P:(g % 2) * P + P],
                                                     us[b][:, o, :], start=n == 0, stop=n == 1)
                        f.merged.raise_by(t, ("m", b))

                steps(pe, STEPS, body)

            for k, f in enumerate(sp_):
                def body(i, first):
                    for b in B2K:
                        pe.wait_ge(*f.rows.at(i, ("v", b)))
                        turn(b, [flat(us[b])[:, j * P:j * P + P] for j in range(HB)], f.turned, ("v", b))
                    for b in B2K:
                        if not first:
                            pe.wait_ge(*f.taken.at(i - 1, ("v", b)))
                        pe.wait_ge(*f.copied.at(i, ("v", b)))
                        by_row(mm[b], flat(vt[b]), wg[:, :], BG, f.product, ("v", b))

                if k == 1:
                    steps(pe, STEPS, body)
                pe.wait_ge(*f.acc_ready.at(STEPS - 1, ("a", 1)))
                pe.wait_ge(s_head, 16 * (k + 1))
                span(k, acc[1][:, EC - 1 - T + G, :], hsum[:, :])

            def dense(i, first):
                def rows_turned(n):
                    for b in B2K:
                        pe.wait_ge(*dn.rows.at(i, (n, b)))
                        turn(b, [flat(h[b])[:, j * P:j * P + P] for j in range(HB)], dn.turned, (n, b))

                if not first:
                    for b in B2K:
                        pe.wait_ge(*dn.taken.at(i - 1, ("odd", b)))
                rows_turned("h1")
                for b in B2K:
                    pe.wait_ge(*dn.copied.at(i, ("h1", b)))
                    by_row(mm[b], flat(vt[b]), wg[:, :], BG, dn.product, ("h1", b))
                rows_turned("h2")
                for b in B2K:
                    pe.wait_ge(*dn.copied.at(i, ("h2", b)))
                    pe.wait_ge(*dn.taken.at(i, ("x2", b)))
                    product(mm[b], w2a[:, :], b, None, dn.product, ("h2", b))
                for b in B2K:
                    pe.wait_ge(*dn.hidden.at(i, ("h2", b)))
                    by_row(tp[b], flat(zz[b]), w2b[:, :], B2, dn.second, ("h2", b))
                rows_turned("h3")
                for n, s in (("even", 0), ("odd", 1)):
                    for b in B2K:
                        if n == "even":
                            pe.wait_ge(*dn.copied.at(i, ("h3", b)))
                        else:
                            pe.wait_ge(*dn.hidden.at(i, ("even", b)))
                        product(mm[b], u1s[:, s, :], b, None, dn.product, (n, b))
                    for b in B2K:
                        pe.wait_ge(*dn.hidden.at(i, (n, b)))
                        by_row(tp[b][:, 512 * s:512 * s + 512], flat(zz[b]), u2[:, :], BU, dn.second, (n, b))

            steps(pe, DSTEPS, dense)

            def turn_job(i, n, blocks_of, *waits):
                for b in B2K:
                    for w in waits:
                        pe.wait_ge(*w(b))
                    turn(b, blocks_of(b), tt.turned, (n, b))

            def blocks7(t):
                return lambda b: [flat(t[b])[:, j * P:j * P + P] for j in range(HB)]

            def last_pass(i, first):
                if not first:
                    for b in B2K:
                        pe.wait_ge(*tt.taken.at(i - 1, ("u1", b)))
                for b in B2K:
                    pe.wait_ge(*tt.rows.at(i, ("us", b)))
                    e = ef[b][:, :, :].rearrange("p g d -> p (g d)")
                    turn(b, [e[:, c:min(c + P, G * DE)] for c in range(0, G * DE, P)], tt.turned, ("ef", b))
                turn_job(i, "us", blocks7(us), lambda b: tt.copied.at(i, ("ef", b)))
                for b in B2K:
                    pe.wait_ge(*tt.copied.at(i, ("us", b)))
                    product(mm[b], w2a[:, :], b, None, tt.product, ("us", b))
                for b in B2K:
                    pe.wait_ge(*tt.hidden.at(i, ("us", b)))
                    by_row(tp[b], flat(zz[b]), w2b[:, :], B2, tt.second, ("us", b))
                turn_job(i, "vd", blocks7(xw), lambda b: tt.rows.at(i, ("vd", b)), lambda b: tt.taken.at(i, ("us", b)))
                for b in B2K:
                    pe.wait_ge(*tt.copied.at(i, ("vd", b)))
                    by_row(mm[b], flat(vt[b]), wg[:, :], BG, tt.product, ("vd", b))
                turn_job(i, "ud", blocks7(h), lambda b: tt.rows.at(i, ("ud", b)))
                for b in B2K:
                    pe.wait_ge(*tt.copied.at(i, ("ud", b)))
                    pe.wait_ge(*tt.taken.at(i, ("vd", b)))
                    product(mm[b], w2a[:, :], b, None, tt.product, ("ud", b))
                for b in B2K:
                    pe.wait_ge(*tt.hidden.at(i, ("ud", b)))
                    by_row(tp[b], flat(zz[b]), w2b[:, :], B2, tt.second, ("ud", b))
                for part, c0, weights1, weights2, k in (("m", 0, m1, m2, BM), ("u", D, u1, u2, BU)):
                    for half in range(2):
                        n = f"{part}{half}"
                        before = {"m0": lambda b: tt.taken.at(i, ("ud", b)), "m1": lambda b: tt.message.at(i, ("m0", b)),
                                  "u0": lambda b: tt.message.at(i, ("m1", b)), "u1": lambda b: tt.taken.at(i, ("u0", b))}[n]
                        turn_job(i, n, lambda b: [cc[b][:, half * HB + j, c0:c0 + P] for j in range(HB)],
                                 lambda b: tt.rows.at(i, ("h3" if part == "m" else "agg", b)), before)
                        for b in B2K:
                            pe.wait_ge(*tt.copied.at(i, (n, b)))
                            product(mm[b], weights1[:, :], b, half * HB if part == "m" else None, tt.product, (n, b))
                        for b in B2K:
                            pe.wait_ge(*tt.hidden.at(i, (n, b)))
                            by_row(tp[b], flat(zz[b]), weights2[:, :], k, tt.second, (n, b))

            steps(pe, STEPS, last_pass)
            pe.wait_ge(s_head, 16 * 3)
            pe.wait_ge(*tt.taken.at(STEPS - 1, ("u1", 0)))
            span(2, hsum[:, :], cc[1][:, 0, 2 * D:3 * D])
            pe.wait_ge(s_border, 1)
            nc.tensor.transpose(tp[0][:, 0:P], brd[:, D:3 * D], ident[:, :]).then_inc(s_bpe, 1)
            pe.wait_ge(s_border, 2)
            nc.tensor.matmul(mm[0][:, 0:P], u1[:, :], bz[:, 0:P], start=True, stop=True).then_inc(s_bpe, 1)
            pe.wait_ge(s_border, 4)
            nc.tensor.matmul(tp[1][:, 0:D], row0[:, :], bias[:, BU, 0:D], start=True, stop=False)
            nc.tensor.matmul(tp[1][:, 0:D], bz[:, P:2 * P], u2[:, :], start=False, stop=True).then_inc(s_bpe, 1)

        @block.scalar
        def _(act):
            def ln_squares(f, i, lanes, n):
                for q in lanes:
                    act.wait_ge(*f.centred.at(i, (n, q)))
                    f.squared.raise_by(nc.scalar.activation(sq[q][:, :, :], xc[q][:, :, :], ACT.Square), (n, q))

            def ln_stds(f, i, lanes, n):
                for q in lanes:
                    act.wait_ge(*f.variance.at(i, (n, q)))
                    f.deviation.raise_by(nc.scalar.activation(st[q][:, 2, :], st[q][:, 1, :], ACT.Sqrt, bias=eps[:, 0:1],
                                                        scale=1.0 / D), (n, q))

            def copy(f, i, n, after=None):
                for b in B2K:
                    act.wait_ge(*f.turned.at(i, (n, b)))
                    f.copied.raise_by(nc.scalar.copy(flat(vt[b]), tp[b][:, 0:W]), (n, b))

            def relu(f, i, n, k):
                for b in B2K:
                    act.wait_ge(*f.product.at(i, (n, b)))
                    f.hidden.raise_by(nc.scalar.activation(flat(zz[b]), mm[b][:, 0:W], ACT.Relu, bias=bcol[:, k:k + 1]),
                                      (n, b))

            act.wait_ge(s_weights, WEIGHTS * 16)
            act.wait_ge(s_const, 1)

            def dense(i, first):
                ln_squares(dn, i, B2K, "l1")
                ln_stds(dn, i, B2K, "l1")
                copy(dn, i, "h1")
                ln_squares(dn, i, B2K, "l2")
                ln_stds(dn, i, B2K, "l2")
                copy(dn, i, "h2")
                relu(dn, i, "h2", 0)
                ln_squares(dn, i, B2K, "l3")
                ln_stds(dn, i, B2K, "l3")
                copy(dn, i, "h3")
                relu(dn, i, "even", 2)
                for b in B2K:
                    act.wait_ge(*dn.second.at(i, ("even", b)))
                relu(dn, i, "odd", 2)

            for k, f in enumerate(hops):
                def body(i, first):
                    for b in B2K:
                        if not first:
                            act.wait_ge(*f.turned.at(i - 1, ("k", b)))
                        if first and k == 1:
                            act.wait_ge(*hops[0].turned.at(STEPS - 1, ("k", b)))
                        f.slot.raise_by(nc.scalar.copy(kslot[b][:, :], key[:, bass.ds(ecol(i, b), G)]), ("k", b))
                    for b in B2K:
                        act.wait_ge(*f.turned.at(i, ("k", b)))
                        if not first:
                            act.wait_ge(*f.picked.at(i - 1, ("k", b, 1)))
                        if first and k == 1:
                            act.wait_ge(*hops[0].picked.at(STEPS - 1, ("k", b, 1)))
                        f.krow.raise_by(nc.scalar.copy(krow[b][:, :], tp[b][0:G, W:W + P]), ("k", b))
                    if k == 0:
                        ln_squares(f, i, B2K, "l")
                        ln_stds(f, i, B2K, "l")
                    for b in B2K:
                        act.wait_ge(*f.merged.at(i, ("m", b)))
                        if not first:
                            act.wait_ge(f.added, 16 * G * (2 * i - 1 + b))
                        if first and k == 1:
                            act.wait_ge(hops[0].added, 16 * G * U)
                        f.sums.raise_by(nc.scalar.copy(flat(acc[b]), tp[b][:, 0:W]), ("m", b))

                act.wait_ge(s_prep, 1)
                steps(act, STEPS, body)

            act.wait_ge(s_deg, 2)
            nc.scalar.activation(dis_s[:, :], tmp[:, :], ACT.Sqrt, bias=one[:, 0:1]).then_inc(s_root, 1)
            nc.scalar.activation(dis_d[:, :], cnt[:, :], ACT.Sqrt, bias=one[:, 0:1]).then_inc(s_root, 1)

            for k, f in enumerate(sp_):
                def body(i, first):
                    if k == 1:
                        copy(f, i, "v")
                    ln_squares(f, i, B2K, "l")
                    ln_stds(f, i, B2K, "l")

                steps(act, STEPS, body)

            steps(act, DSTEPS, dense)

            def last_pass(i, first):
                for b in B2K:
                    act.wait_ge(*tt.turned.at(i, ("ef", b)))
                    if not first:
                        act.wait_ge(*tt.product.at(i - 1, ("m1", b)))
                    nc.scalar.copy(eft[b][:, 0:3 * P], tp[b][:, 0:3 * P])
                    tt.copied.raise_by(nc.scalar.copy(eft[b][0:D, 3 * P:4 * P], tp[b][0:D, 3 * P:4 * P]), ("ef", b))
                copy(tt, i, "us")
                ln_squares(tt, i, B2K, "d1")
                ln_stds(tt, i, B2K, "d1")
                relu(tt, i, "us", 0)
                copy(tt, i, "vd")
                ln_squares(tt, i, B2K, "d2")
                ln_stds(tt, i, B2K, "d2")
                copy(tt, i, "ud")
                ln_squares(tt, i, B2K, "s3")
                ln_stds(tt, i, B2K, "s3")
                relu(tt, i, "ud", 0)
                ln_squares(tt, i, B2K, "d3")
                ln_stds(tt, i, B2K, "d3")
                for half in range(2):
                    copy(tt, i, f"m{half}")
                    relu(tt, i, f"m{half}", 1)
                    for b in B2K:
                        act.wait_ge(*tt.second.at(i, (f"m{half}", b)))
                        o = us[b][:, half * HB:half * HB + HB, :].rearrange("p g d -> p (g d)")
                        tt.message.raise_by(nc.scalar.copy(o, tp[b][:, 0:HB * D]), (f"m{half}", b))
                for half in range(2):
                    copy(tt, i, f"u{half}")
                    relu(tt, i, f"u{half}", 2)

            steps(act, STEPS, last_pass)

        @block.vector
        def _(dve):
            V = nc.vector
            dve_passed = sem("dve_waits_passed")

            prep = [0]

            def link(ins):
                prep[0] += 1
                ins.then_inc(s_own, 1)
                dve.wait_ge(s_own, prep[0])

            for t in (wg, w2a, w2b, bias, u1s, m1e, *eft):
                link(V.memset(t[:, :] if len(t.shape) == 2 else t[:, :, :], 0.0))
            link(V.memset(eps[:, :], EPS))
            V.memset(one[:, :], 1.0).then_inc(s_const, 1)
            dve.wait_ge(s_const, 1)
            dve.wait_ge(s_edges, 12 * 16)
            dve.wait_ge(s_rowno, 12)
            K, F, KN, TLEN, HLEN, TCNT, CARRY, BCNT, FNK, S0, S1 = (small[:, j:j + 1] for j in range(11))
            link(V.tensor_copy(dst_f[:, :], dst_i[:, :]))
            link(V.tensor_copy(nxt_f[:, :], nxt_i[:, :]))
            link(V.tensor_copy(prv_f[:, :], prv_i[:, :]))
            link(V.tensor_copy(K, dst_f[:, EC - 1:EC]))
            link(V.tensor_copy(F, dst_f[:, 0:1]))
            link(V.tensor_copy(KN, kn_i[:, :]))
            link(V.tensor_copy(dst_f[:, EC:T], K))
            link(V.tensor_tensor(flag[:, :], prv_f[:, :], dst_f[:, :], ALU.is_equal))
            link(V.tensor_copy(same[:, :], flag[:, :]))
            link(V.memset(same[:, 0:1], 0.0))
            link(V.tensor_tensor(more[:, :], nxt_f[:, :], dst_f[:, :], ALU.is_equal))
            link(V.memset(more[:, EC:T], 0.0))
            link(V.tensor_scalar(last[:, :], more[:, :], -1.0, 1.0, ALU.mult, ALU.add))
            link(V.tensor_copy(cont[:, :], more[:, :]))
            link(V.memset(cont[:, EC - 1:EC], 0.0))
            link(V.scalar_tensor_tensor(tmp[:, :], more[:, :], BIG, dst_f[:, :], ALU.mult, ALU.add))
            link(V.memset(tmp[:, EC:T], BIG))
            link(V.tensor_copy(map_idx[:, :], tmp[:, :]))
            link(V.tensor_scalar(tmp[:, :], dst_f[:, :], K, None, ALU.is_equal))
            link(V.tensor_reduce(TLEN, tmp[:, 0:EC], X, ALU.add))
            link(V.tensor_tensor(tmp[:, :], tmp[:, :], flag[:, :], ALU.max))
            link(V.scalar_tensor_tensor(tmp[:, :], tmp[:, :], BIG, dst_f[:, :], ALU.mult, ALU.add))
            link(V.tensor_copy(out_idx[:, :], tmp[:, :]))
            link(V.tensor_scalar(tmp[:, :], dst_f[:, :], float(N - 1), None, ALU.min))
            link(V.tensor_copy(dstc_i[:, :], tmp[:, :]))
            link(V.tensor_scalar(flag[:, :], dst_f[:, :], F, None, ALU.is_equal))
            link(V.memset(flag[:, EC:T], 0.0))
            link(V.tensor_reduce(HLEN, flag[:, 0:EC], X, ALU.add))
            link(V.scalar_tensor_tensor(S0, HLEN, -1.0, rowno[:, 0:1], ALU.add, ALU.add))
            link(V.tensor_copy(head_i[:, :], S0))
            link(V.scalar_tensor_tensor(S0, TLEN, -1.0, rowno[:, EC:T], ALU.mult, ALU.add))
            link(V.tensor_copy(tail_i[:, :], S0))
            link(V.tensor_tensor(S0, K, KN, ALU.is_equal))
            link(V.scalar_tensor_tensor(S1, S0, BIG, K, ALU.mult, ALU.add))
            link(V.tensor_copy(brd_i[:, :], S1))
            link(V.memset(tmp[:, :], 1.0))
            link(V.tensor_tensor_scan(cnt[:, :], same[:, :], tmp[:, :], 0.0, ALU.mult, ALU.add))
            link(V.tensor_copy(TCNT, cnt[:, EC - 1:EC]))
            link(V.tensor_copy(key[:, :], src_i[:, :]))
            link(V.scalar_tensor_tensor(tmp[:, :], dst_f[:, :], float(N), spare[:, :], ALU.is_equal, ALU.mult))
            link(V.tensor_copy(tmp[:, EC:T], spare[:, EC:T]))
            link(V.tensor_tensor(key[:, :], key[:, :], tmp[:, :], ALU.add))
            for j, border in ((0, K), (1, F)):
                V.tensor_scalar(diag[:, j, :], ident[:, :], border, None, ALU.mult).then_inc(s_diag, 1)
            dve.wait_ge(s_kfp, 1)
            link(V.tensor_copy(kf[:, :, :].rearrange("p a b -> p (a b)"), tp[0][:, 0:2 * P]))
            link(V.tensor_tensor(FNK, F, K, ALU.not_equal))
            link(V.scalar_tensor_tensor(mh[:, :], kf[:, 1, :], K, upper[:, :], ALU.is_equal, ALU.mult))
            link(V.tensor_scalar(mt1[:, :], kf[:, 0, :], K, None, ALU.is_equal))
            link(V.tensor_scalar(mt2[:, :], kf[:, 0, :], F, FNK, ALU.is_equal, ALU.mult))
            dve.sem_inc(s_mats, 1)
            dve.wait_ge(s_cc, 1)
            link(V.tensor_copy(small[:, 6:8], tp[1][:, 0:2]))
            link(V.scalar_tensor_tensor(cnt[:, :], flag[:, :], CARRY, cnt[:, :], ALU.mult, ALU.add))
            link(V.tensor_copy(cnt[:, EC:T], BCNT))
            link(V.tensor_copy(map_rows[:, :, 0], rowno[:, :]))
            V.tensor_copy(map_rows[:, :, 1], cnt[:, :]).then_inc(s_mapin, 1)
            dve.sem_inc(s_prep, 1)

            def layer_norm(own, f, i, n, lanes, xs, hs, ready, scale=None, free=None, final=None):
                marks = {}
                for q in lanes:
                    own.wait(*ready[q])
                    marks[q] = own.did(V.tensor_reduce(st[q][:, 0, :], xs[q], X, ALU.add))
                for q in lanes:
                    own.wait(marks[q])
                    f.centred.raise_by(V.scalar_tensor_tensor(xc[q][:, :, :], stat(q, 0), -1.0 / D, xs[q],
                                                              ALU.mult, ALU.add), (n, q))
                    if free is not None:
                        free(q)
                for q in lanes:
                    dve.wait_ge(*f.squared.at(i, (n, q)))
                    f.variance.raise_by(V.tensor_reduce(st[q][:, 1, :], sq[q][:, :, :], X, ALU.add), (n, q))
                for q in lanes:
                    dve.wait_ge(*f.deviation.at(i, (n, q)))
                    marks[q] = own.did(V.reciprocal(st[q][:, 3, :], st[q][:, 2, :]))
                if scale is not None:
                    for q in lanes:
                        own.wait(marks[q])
                        dve.sem_inc(dve_passed)
                        marks[q] = own.did(V.tensor_tensor(st[q][:, 3, :], st[q][:, 3, :], scale(q), ALU.mult))
                done = {}
                for q in lanes:
                    own.wait(marks[q])
                    ins = V.scalar_tensor_tensor(hs[q], xc[q][:, :, :], 0.0, stat(q, 3), ALU.max, ALU.mult)
                    done[q] = final(q, ins) if final else own.did(ins)
                return done

            def full(t):
                return t if isinstance(t, bass.AP) else t[:, :, :]

            for k, f in enumerate(hops):
                own = Own(dve, f.dve)

                def body(i, first):
                    own.step(i)
                    def msg_ready(q, ins):
                        f.rows.raise_by(ins, ("m", q))

                    if not first:
                        for b in B2K:
                            dve.wait_ge(*f.merged.at(i - 1, ("m", b)))
                    elif k == 1:
                        for b in B2K:
                            dve.wait_ge(*hops[0].merged.at(STEPS - 1, ("m", b)))
                    count = {}
                    for b in B2K:
                        for j, columns in enumerate(HALF):
                            dve.wait_ge(*f.picked.at(i, ("k", b, j)))
                            for g in columns:
                                o = g - g % 2 - columns[0]
                                keys, mine = mm[j][:, o * P:o * P + 2 * P], kslot[b][:, g:g + 1]
                                if k == 0:
                                    w = P * (1 + g % 2)
                                    count[b] = own.did(V.scalar_tensor_tensor(
                                        equal[b][:, g, 0:w], keys[:, 0:w], mine, lower[:, g % 2, 0:w], ALU.is_equal,
                                        ALU.mult, accum_out=dups[b][:, g:g + 1]))
                                    own.wait(count[b])
                                ins = V.tensor_scalar(equal[b][:, g, :], keys, mine, None, ALU.is_equal)
                                if g == columns[-1]:
                                    f.compared.raise_by(ins, ("k", b, j))
                    if k == 0:
                        for b in B2K:
                            mine = key[:, bass.ds(ecol(i, b), G)]
                            d0 = own.did(V.tensor_scalar(dups[b][:, :], dups[b][:, :], 1.0, None, ALU.min))
                            d1 = own.did(V.scalar_tensor_tensor(st[b][:, 0, :], mine, -1.0, spare[:, 0:G], ALU.mult, ALU.add))
                            own.wait(d0, d1)
                            own.wait(own.did(V.tensor_tensor(st[b][:, 0, :], st[b][:, 0, :], dups[b][:, :], ALU.mult)))
                            own.wait(own.did(V.tensor_tensor(kidx[:, bass.ds(ecol(i, b), G)], st[b][:, 0, :], mine, ALU.add)))
                        layer_norm(own, f, i, "l", B2K, [full(ga[b]) for b in B2K], [full(us[b]) for b in B2K],
                                   [[(f.got[b], 16 * G * (i + 1))] for b in B2K],
                                   scale=lambda q: wt[:, bass.ds(ecol(i, q), G)], final=msg_ready)
                    else:
                        for b in B2K:
                            dve.wait_ge(f.got[b], 16 * G * (i + 1))
                            msg_ready(b, V.tensor_tensor(full(us[b]), full(ga[b]), cols(wt, ecol(i, b)), ALU.mult))

                steps(dve, STEPS, body)


            base = prep[0]
            dve.wait_ge(s_mapv, 2 * STEPS)
            link(V.tensor_scalar(flag[:, :], src_map[:, :, 1], 0.0, None, ALU.is_equal))
            link(V.tensor_copy(tmp[:, :], rowno[:, 0:1].broadcast_to([P, T])))
            link(V.tensor_scalar(tmp[:, :], tmp[:, :], 1.0 / T, float(ROWS), ALU.mult, ALU.add))
            link(V.tensor_tensor(tmp[:, :], tmp[:, :], flag[:, :], ALU.mult))
            link(V.tensor_tensor(tmp[:, :], tmp[:, :], src_map[:, :, 0], ALU.add))
            link(V.tensor_copy(ptr_i[:, :], tmp[:, :]))
            dve.sem_inc(s_ptr, 1)
            V.tensor_copy(tmp[:, :], src_map[:, :, 1]).then_inc(s_deg, 1)
            dve.wait_ge(s_deg, 1)
            dve.sem_inc(s_deg, 1)
            dve.wait_ge(s_root, 2)
            link(V.reciprocal(dis_s[:, :], dis_s[:, :]))
            link(V.reciprocal(dis_d[:, :], dis_d[:, :]))
            dve.sem_inc(s_phase, 1)

            def running(own, i, b, o, prev, first_at, msg, factor, col, ready, order, final=None):
                mark = None
                for n, g in enumerate(order):
                    if mark is None:
                        own.wait(*ready)
                    else:
                        own.wait(mark)
                    if prev is None:
                        ins = V.tensor_copy(o(g), msg(g))
                    else:
                        ins = V.scalar_tensor_tensor(o(g), prev, factor[:, bass.ds(col + g, 1)], msg(g), ALU.mult, ALU.add)
                    prev = o(g)
                    if final is not None and n == G - 1:
                        final(ins)
                    else:
                        mark = own.did(ins)

            for k, f in enumerate(sp_):
                own = Own(dve, f.dve)

                def body(i, first):
                    own.step(i)
                    ready = {}
                    if not first:
                        dve.wait_ge(*f.acc_ready.at(i - 1, ("a", 1)))
                        for b in B2K:
                            dve.wait_ge(f.kept[b], 16 * 2 * i)
                    got = {b: (f.got[b], 16 * G * (i + 1)) for b in B2K}
                    if k == 0:
                        ready = layer_norm(own, f, i, "l", B2K, [full(ga[b]) for b in B2K], [full(h[b]) for b in B2K],
                                           [[got[b]] for b in B2K], scale=lambda q: dis_s[:, bass.ds(ecol(i, q), G)])
                        for b in B2K:
                            own.wait(ready[b])
                            f.ga_free.raise_now(dve, ("g", b))
                    else:
                        for b in B2K:
                            own.wait(got[b], (f.load[b], 32 * (i + 1)))
                            ready[b] = own.did(V.tensor_tensor(full(us[b]), full(hin[b]), full(ga[b]), ALU.add))
                        for b in B2K:
                            own.wait(ready[b])
                            f.ga_free.raise_now(dve, ("g", b))
                            f.rows.raise_by(V.tensor_tensor(full(us[b]), full(us[b]), cols(dis_s, ecol(i, b)), ALU.mult), ("v", b))
                        for b in B2K:
                            dve.wait_ge(*f.product.at(i, ("v", b)))
                            f.taken.raise_by(V.tensor_tensor(flat(xw[b]), flat(xin[b]), mm[b][:, 0:W], ALU.add), ("v", b))
                        for b in B2K:
                            dve.wait_ge(*f.taken.at(i, ("v", b)))
                            f.in_free.raise_now(dve, ("x", b))
                        ready = layer_norm(own, f, i, "l", B2K, [full(xw[b]) for b in B2K], [full(h[b]) for b in B2K],
                                           [[] for b in B2K])
                    for b in B2K:
                        own.wait(ready[b])
                        f.state_ready.raise_now(dve, ("x", b))
                    for b in B2K:
                        if not first:
                            dve.wait_ge(f.stored[b], 16 * i)
                        prev = None if first and b == 0 else acc[1 - b][:, G - 1, :]
                        carry = [] if b == 0 else [f.acc_ready.at(i, ("a", 0))]
                        if b == 0 and not first:
                            carry = [f.acc_ready.at(i - 1, ("a", 1))]
                        running(own, i, b, lambda g: acc[b][:, g, :], prev, 0, lambda g: h[b][:, g, :], same, ecol(i, b),
                                [ready[b]] + carry, range(G),
                                final=lambda ins: f.acc_ready.raise_by(ins, ("a", b)))

                if k == 1:
                    for b in B2K:
                        dve.wait_ge(sp_[0].stored[b], 16 * STEPS)
                        dve.wait_ge(sp_[0].kept[b], 16 * 2 * STEPS)
                steps(dve, STEPS, body)
                dve.wait_ge(s_span, k + 1)
                V.tensor_tensor(fix[:, 0:D], tp[0][:, 0:D], hsum[:, :], ALU.add).then_inc(s_fixpart, 1)
                dve.wait_ge(s_fixpart, k + 1)
                V.tensor_copy(fix[:, D:2 * D], tp[0][:, D:2 * D]).then_inc(s_fix, 1)
                dve.wait_ge(s_fix, k + 1)
                dve.sem_inc(s_phase, 1)

            own = Own(dve, dn.dve)
            for b in B2K:
                dve.wait_ge(sp_[1].stored[b], 16 * STEPS)
                dve.wait_ge(sp_[1].kept[b], 16 * 2 * STEPS)

            def dense(i, first):
                own.step(i)

                def rows_ready(n):
                    def done(q, ins):
                        dn.rows.raise_by(ins, (n, q))
                        return dn.rows.at(i, (n, q))
                    return done

                layer_norm(own, dn, i, "l1", B2K, [full(xin[b]) for b in B2K], [full(h[b]) for b in B2K],
                           [[(dn_load[b], 16 * (i + 1))] for b in B2K], final=rows_ready("h1"))
                marks = {}
                for b in B2K:
                    dve.wait_ge(*dn.product.at(i, ("h1", b)))
                    dn.taken.raise_by(V.tensor_tensor(flat(xw[b]), flat(xin[b]), mm[b][:, 0:W], ALU.add), ("x2", b))
                for b in B2K:
                    dve.wait_ge(*dn.taken.at(i, ("x2", b)))
                    dn.xin_free.raise_now(dve, ("x", b))
                layer_norm(own, dn, i, "l2", B2K, [full(xw[b]) for b in B2K], [full(h[b]) for b in B2K],
                           [[] for b in B2K], final=rows_ready("h2"))
                for b in B2K:
                    dve.wait_ge(*dn.second.at(i, ("h2", b)))
                    dn.taken.raise_by(V.tensor_tensor(flat(xw[b]), flat(xw[b]), tp[b][:, 0:W], ALU.add), ("x3", b))
                layer_norm(own, dn, i, "l3", B2K, [full(xw[b]) for b in B2K], [full(h[b]) for b in B2K],
                           [[dn.taken.at(i, ("x3", b))] for b in B2K], final=rows_ready("h3"))
                for n, s in (("even", 0), ("odd", 1)):
                    for b in B2K:
                        dve.wait_ge(*dn.second.at(i, (n, b)))
                        if not first and n == "even":
                            dve.wait_ge(s_dense[b], 16 * i)
                        dn.taken.raise_by(V.tensor_tensor(
                            acc[b][:, s:G:2, :], xw[b][:, s:G:2, :],
                            tp[b][:, 512 * s:512 * s + HB * D].rearrange("p (g d) -> p g d", d=D), ALU.add), (n, b))
                for b in B2K:
                    dve.wait_ge(*dn.taken.at(i, ("odd", b)))
                    dn.out_ready.raise_now(dve, ("o", b))

            steps(dve, DSTEPS, dense)
            dve.sem_inc(s_phase, 1)

            own = Own(dve, tt.dve)

            def last_pass(i, first):
                own.step(i)
                both = range(G - 1, -1, -1)

                def did(signal, key, ins):
                    signal.raise_by(ins, key)
                    return signal.at(i, key)

                loaded = {b: (tt.load[b], 16 * 6 * (i + 1)) for b in B2K}
                got_a = {b: (tt.got_a[b], 16 * G * (i + 1)) for b in B2K}
                got_x = {b: (tt.got_x[b], 16 * G * (i + 1)) for b in B2K}
                ddis = lambda b: dis_d[:, bass.ds(tcol(i, b), G)]
                for b in B2K:
                    own.wait(loaded[b], got_a[b])
                    did(tt.rows, ("us", b), V.tensor_tensor(full(us[b]), full(hin[b]), full(ga[b]), ALU.add))
                xm = {}
                for b in B2K:
                    own.wait(tt.rows.at(i, ("us", b)))
                    tt.ga_free.raise_now(dve, ("g", b))
                hd = layer_norm(own, tt, i, "d1", B2K, [full(gx[b]) for b in B2K], [full(xw[b]) for b in B2K],
                                [[got_x[b]] for b in B2K], scale=ddis)
                for b in B2K:
                    own.wait(hd[b])
                    hd[b] = own.did(V.tensor_tensor(full(xw[b]), full(xw[b]), full(a3[b]), ALU.add))
                for b in B2K:
                    own.wait(hd[b])
                    did(tt.rows, ("vd", b), V.tensor_tensor(full(xw[b]), full(xw[b]), cols(dis_d, tcol(i, b)), ALU.mult))
                xs = {}
                for b in B2K:
                    dve.wait_ge(*tt.second.at(i, ("us", b)))
                    xs[b] = did(tt.taken, ("us", b),
                                V.tensor_tensor(flat(us[b]), flat(xin[b]), tp[b][:, 0:W], ALU.add))
                for b in B2K:
                    dve.wait_ge(*tt.product.at(i, ("vd", b)))
                    xm[b] = did(tt.taken, ("vd", b), V.tensor_tensor(flat(xd[b]), flat(gx[b]), mm[b][:, 0:W], ALU.add))
                for b in B2K:
                    own.wait(xm[b])
                    tt.gx_free.raise_now(dve, ("g", b))
                hd = layer_norm(own, tt, i, "d2", B2K, [full(xd[b]) for b in B2K], [full(h[b]) for b in B2K],
                                [[xm[b]] for b in B2K])
                for b in B2K:
                    own.wait(hd[b])
                    did(tt.rows, ("ud", b), V.tensor_tensor(full(h[b]), full(h[b]), full(a4[b]), ALU.add))
                for b in B2K:
                    own.wait(tt.rows.at(i, ("ud", b)))
                    tt.in_free.raise_now(dve, ("x", b))
                h3s = layer_norm(own, tt, i, "s3", B2K, [full(us[b]) for b in B2K],
                                 [cc[b][:, :, 0:D] for b in B2K], [[xs[b]] for b in B2K])
                for b in B2K:
                    dve.wait_ge(*tt.second.at(i, ("ud", b)))
                    xm[b] = did(tt.taken, ("ud", b), V.tensor_tensor(flat(xd[b]), flat(xd[b]), tp[b][:, 0:W], ALU.add))
                for b in B2K:
                    own.wait(xm[b])
                    xm[b] = own.did(V.tensor_tensor(full(xd[b]), full(xd[b]), cols(last, tcol(i, b)), ALU.mult))
                ends = {}
                for b in B2K:
                    prev = None if first and b == 0 else x3[1 - b][:, 0, :]
                    mark = []
                    if b == 1:
                        mark = [ends[0]]
                    running(own, i, b, lambda g: x3[b][:, g, :], prev, 0, lambda g: xd[b][:, g, :], more, tcol(i, b),
                            [xm[b]] + mark, both)
                    ends[b] = (own.sem, own.i * own.per + own.k)
                layer_norm(own, tt, i, "d3", B2K, [full(x3[b]) for b in B2K], [cc[b][:, :, D:2 * D] for b in B2K],
                           [[ends[b]] for b in B2K], final=lambda q, ins: did(tt.rows, ("h3", q), ins))
                for b in B2K:
                    if not first:
                        dve.wait_ge(tt.kept[b], 16 * i)
                    prev = None if first and b == 0 else cc[1 - b][:, 0, 2 * D:3 * D]
                    mark = [tt.message.at(i, ("m1", b))] + ([tt.rows.at(i, ("agg", 0))] if b else [])
                    running(own, i, b, lambda g: cc[b][:, g, 2 * D:3 * D], prev, 0, lambda g: us[b][:, g, :], cont,
                            tcol(i, b), mark, both, final=lambda ins: tt.rows.raise_by(ins, ("agg", b)))
                if first:
                    V.tensor_copy(brd[:, 0:D], x3[0][:, G - 1, :]).then_inc(s_saved, 1)
                    V.tensor_copy(brd[:, D:2 * D], cc[0][:, G - 1, D:2 * D]).then_inc(s_saved, 1)
                for half in range(2):
                    for b in B2K:
                        dve.wait_ge(*tt.second.at(i, (f"u{half}", b)))
                        if not first and half == 0:
                            dve.wait_ge(tt.written[b], 16 * G * i)
                        did(tt.taken, (f"u{half}", b), V.tensor_tensor(
                            acc[b][:, half * HB:half * HB + HB, :], x3[b][:, half * HB:half * HB + HB, :],
                            tp[b][:, 0:HB * D].rearrange("p (g d) -> p g d", d=D), ALU.add))
                for b in B2K:
                    dve.wait_ge(*tt.taken.at(i, ("u1", b)))
                    tt.o_ready.raise_now(dve, ("o", b))

            for b in B2K:
                dve.wait_ge(s_dense[b], 16 * DSTEPS)
            steps(dve, STEPS, last_pass)
            dve.wait_ge(s_span, 3)
            dve.wait_ge(s_saved, 2)
            V.tensor_copy(brd[:, 2 * D:3 * D], tp[0][:, D:2 * D]).then_inc(s_border, 1)
            dve.wait_ge(s_bpe, 1)
            V.tensor_copy(bz[:, 0:P], tp[0][:, 0:P]).then_inc(s_border, 1)
            dve.wait_ge(s_bpe, 2)
            V.tensor_scalar(bz[:, P:2 * P], mm[0][:, 0:P], bcol[:, 2:3], 0.0, ALU.add, ALU.max).then_inc(s_border, 1)
            dve.wait_ge(s_border, 3)
            dve.sem_inc(s_border, 1)
            dve.wait_ge(s_bpe, 3)
            V.tensor_tensor(fix[:, 0:D], brd[:, 0:D], tp[1][:, 0:D], ALU.add).then_inc(s_border, 1)


_INS = ["x", "src", "dst", "edge_attr_32", "edge_weight", "L1_gnn_W", "L1_gnn_b", "L2_gnn_W1", "L2_gnn_b1",
        "L2_gnn_W2", "L2_gnn_b2", "L3_gnn_mW1", "L3_gnn_mb1", "L3_gnn_mW2", "L3_gnn_mb2", "L3_gnn_uW1",
        "L3_gnn_ub1", "L3_gnn_uW2", "L3_gnn_ub2"]


def kernel(**inputs):
    import numpy as np
    import concourse.bacc as bacc
    from concourse.bass_utils import run_bass_kernel_spmd

    nc = bacc.Bacc("TRN2", target_bir_lowering=False, num_devices=1)
    arrays, args = {}, []
    for name in _INS:
        a = np.asarray(inputs[name])
        a = np.ascontiguousarray(a.T if name in ("L2_gnn_W1", "L2_gnn_W2") else a)
        arrays[f"in_{name}"] = a
        args.append(nc.dram_tensor(f"in_{name}", a.shape, mybir.dt.from_np(a.dtype), kind="ExternalInput").ap())
    args.append(nc.dram_tensor("out_x", (N, D), F32, kind="ExternalOutput").ap())
    gnn(nc, *args)
    r = run_bass_kernel_spmd(nc, [arrays], core_ids=[0])
    return r.results[0]["out_x"]
```

```python
from contextlib import ExitStack

import concourse.bass as bass
from concourse import mybir

P = 128
N = 100000
E = 50000
D = 64
DE = 32
DH = 128
EC = -(-E // P)
T = EC + 1
ELAST = E - (P - 1) * EC
G = 14
U = T // G
STEPS = U // 2
NU = -(-N // (P * G))
DSTEPS = NU // 4
W = G * D
HB = G // 2
HC = 208
ROWS = P * T
BIG = float(1 << 20)
EPS = 1e-5
assert G == 14 and T % (2 * G) == 0 and NU % 4 == 0 and W % P == 0

F32 = mybir.dt.float32
I32 = mybir.dt.int32
BF16 = mybir.dt.bfloat16
ALU = mybir.AluOpType
ACT = mybir.ActivationFunctionType
X = mybir.AxisListType.X


class Signal:

    def __init__(self, sem, keys):
        self.sem, self.keys, self.next = sem, list(keys), 0

    def at(self, i, key):
        return self.sem, i * len(self.keys) + self.keys.index(key) + 1

    def raise_by(self, instruction, key):
        assert self.keys[self.next % len(self.keys)] == key, (key, self.keys, self.next)
        self.next += 1
        instruction.then_inc(self.sem, 1)

    def raise_now(self, engine, key):
        assert self.keys[self.next % len(self.keys)] == key, (key, self.keys, self.next)
        self.next += 1
        engine.sem_inc(self.sem, 1)


class Settled:

    def __init__(self, engine, passed):
        self.engine, self.passed = engine, passed

    def wait_ge(self, sem, value):
        self.engine.wait_ge(sem, value)
        if not isinstance(value, int):
            self.engine.sem_inc(self.passed, 1)


class Own:

    def __init__(self, engine, sem):
        self.engine, self.sem, self.per, self.k, self.i = engine, sem, 0, 0, 0

    def step(self, i):
        assert not self.per or self.k == self.per
        self.per, self.i, self.k = self.k, i, 0

    def did(self, instruction):
        instruction.then_inc(self.sem, 1)
        self.k += 1
        return self.sem, self.i * self.per + self.k

    def wait(self, *marks):
        for sem, value in marks:
            self.engine.wait_ge(sem, value)


def steps(engine, n, body, last_apart=False):
    body(0, True)
    with engine.Fori(1, n - last_apart) as i:
        body(i, False)
    if last_apart:
        body(n - 1, False)


def gnn(nc, x, src, dst, edge_attr, edge_weight, W1g, b1g, W2a, b2a, W2b, b2b, mW1, mb1, mW2, mb2, uW1, ub1,
        uW2, ub2, out):
    ctx = ExitStack()
    with ctx:
        def sb(name, shape, dt=F32):
            return ctx.enter_context(nc.sbuf_tensor(name, shape, dt))

        def sem(name):
            return ctx.enter_context(nc.semaphore(name))

        def dram(name, shape):
            return nc.dram_tensor(name, shape, F32, kind="Internal").ap()

        tables = [dram(f"table{k}", [ROWS + P, D]) for k in range(2)]
        hop = dram("hop", [N + 2 * P, D])
        x1 = dram("x1", [N + 2 * P, D])
        suffix = dram("suffix", [ROWS, D])
        node_map = dram("node_map", [N, 2])
        xs1, xs2 = (dram(f"xs{k}", [P, T * D]) for k in (1, 2))
        ms1, hs2 = dram("ms1", [P, T * D]), dram("hs2", [P, T * D])

        def rows(t):
            return t[0:ROWS, :].rearrange("(p c) d -> p (c d)", p=P)

        zeros = sb("zeros", [P, G * DE])
        ident = sb("ident", [P, P])
        upper = sb("upper", [P, P])
        ones = sb("ones", [P, P])
        rows3 = sb("rows3", [P, P], BF16)
        eps = sb("eps", [P, 1])
        one = sb("one", [P, 1])
        wg = sb("wg", [P, P])
        w2a = sb("w2a", [P, P])
        w2b = sb("w2b", [P, P])
        m1 = sb("m1", [P, DH])
        m1e = sb("m1e", [P, 4, DH])
        m2 = sb("m2", [P, D])
        u1 = sb("u1", [P, DH])
        u1s = sb("u1s", [P, 2, DH])
        u2 = sb("u2", [P, D])
        bias = sb("bias", [P, 4, 512], BF16)
        bcol = sb("bcol", [P, 3])
        BG, B2, BM, BU = range(4)

        dst_i, src_i = (sb(n, [P, T], I32) for n in ("dst_i", "src_i"))
        dst_f = sb("dst_f", [P, T])
        wt = sb("wt", [P, T])
        same = sb("same", [P, T])
        more = sb("more", [P, T])
        last = sb("last", [P, T])
        cont = sb("cont", [P, T])
        flag = sb("flag", [P, T])
        tmp = sb("tmp", [P, T])
        cnt = sb("cnt", [P, T])
        map_idx = sb("map_idx", [P, T], I32)
        out_idx = sb("out_idx", [P, T], I32)
        dstc_i = sb("dstc_i", [P, T], I32)
        ptr_i = sb("ptr_i", [P, T], I32)
        rowno = sb("rowno", [P, T])
        map_rows = sb("map_rows", [P, T, 2])
        src_map = map_rows
        dis_s = sb("dis_s", [P, T])
        dis_d = sb("dis_d", [P, T])
        kn_i = sb("kn_i", [P, 1], I32)
        small = sb("small", [P, 24])
        head_i, tail_i, brd_i = (sb(n, [P, 1], I32) for n in ("head_i", "tail_i", "brd_i"))
        diag = sb("diag", [P, 2, P])
        kf = sb("kf", [P, 2, P])
        mh, mt1, mt2 = (sb(n, [P, P]) for n in ("mh", "mt1", "mt2"))

        def pair(name, shape, dt=F32):
            return [sb(f"{name}{b}", shape, dt) for b in range(2)]

        unit = [P, G, D]
        xin, hin, xw, h, vt, zz, ga = (pair(n, unit) for n in ("xin", "hin", "xw", "h", "vt", "zz", "ga"))
        acc = pair("acc", unit)
        us = pair("us", unit)
        wide = pair("wide", [P, 4, G, D])
        a3, a4, gx, xd = ([wide[b][:, k] for b in range(2)] for k in range(4))
        equal = [t[:, :, :, :].rearrange("p k g d -> p (k g d)").rearrange("p (g m) -> p g m", g=G) for t in wide]
        lower = sb("lower", [P, 2, 2 * P])
        kslot, krow = pair("kslot", [P, G]), pair("krow", [G, P])
        dups = pair("dups", [P, G])
        kidx = sb("kidx", [P, T], I32)
        key = sb("key", [P, T])
        spare = sb("spare", [P, T])
        x3 = pair("x3", unit)
        xc, sq = pair("xc", unit), pair("sq", unit)
        st = [sb(f"st{q}", [P, 4, G]) for q in range(4)]
        cc = pair("cc", [P, G, 3 * D])
        pick = cc[0][0:G, :, :].rearrange("p g d -> p (g d)")[:, 0:G * P].rearrange("p (g m) -> p g m", g=G)
        ef = pair("ef", [P, G, DE])
        eft = pair("eft", [P, 512])
        isl, isl2, osl = (pair(n, [P, G], I32) for n in ("isl", "isl2", "osl"))
        msl = pair("msl", [P, G, 2])
        hsum = sb("hsum", [P, D])
        fix = sb("fix", [P, 2 * D])
        brd = sb("brd", [P, 3 * D])
        bz = sb("bz", [P, 2 * P])

        ccu = [[t[:, :, :].rearrange("p g d -> p (g d)")[:, j * W:j * W + W].rearrange("p (g d) -> p g d", d=D)
                for j in range(3)] for t in cc]
        lane_x, lane_y, lane_h, lane_o = ([t[0], t[1], wide[0][:, j], wide[1][:, j]]
                                          for j, t in enumerate((xin, xw, h, acc)))
        lane_c, lane_s, lane_v = ([t[0], t[1], ccu[0][j], ccu[1][j]] for j, t in enumerate((xc, sq, vt)))
        lane_z = [zz[0], zz[1], us[0], us[1]]
        bias_f = cc[0][:, :, :].rearrange("p g d -> p (g d)")[:, 0:4 * 512].rearrange("p (k c) -> p k c", k=4)
        bias_part = cc[1][:, :, :].rearrange("p g d -> p (g d)")[:, 0:2 * 512].bitcast(BF16).rearrange("p (k c) -> p k c", k=4)
        nxt_f, prv_f = (xc[b][:, :, :].rearrange("p g d -> p (g d)")[:, 0:T] for b in range(2))
        nxt_i, prv_i = (sq[b][:, :, :].rearrange("p g d -> p (g d)")[:, 0:T].bitcast(I32) for b in range(2))

        tp = [ctx.enter_context(nc.psum_tensor(f"tp{b}", [P, 1024], F32)) for b in range(2)]
        mm = [ctx.enter_context(nc.psum_tensor(f"mm{b}", [P, 1024], F32)) for b in range(2)]
        lane_p = [*tp, *mm]

        def flat(t, n=W):
            return (t if isinstance(t, bass.AP) else t[:, :, :]).rearrange("p g d -> p (g d)")[:, 0:n]

        def full(t):
            return t if isinstance(t, bass.AP) else t[:, :, :]

        def cols(ap, c, n=G):
            return ap[:, bass.ds(c, n)].unsqueeze(2).broadcast_to([P, n, D])

        def stat(q, k):
            return st[q][:, k, :].unsqueeze(2).broadcast_to([P, G, D])

        s_const = sem("constants_ready")
        s_zero = sem("zeros_ready")
        s_pad = sem("padding_written")
        s_edges = sem("edges_loaded")
        s_weights = sem("weights_loaded")
        s_cleared = sem("map_and_zero_rows_cleared")
        s_rowno = sem("row_numbers_ready")
        s_prep = sem("dve_prep_done")
        s_diag = sem("diagonals_ready")
        s_kfp = sem("key_rows_in_psum")
        s_mats = sem("span_matrices_ready")
        s_cc = sem("count_carries_in_psum")
        s_mapin = sem("map_rows_ready")
        s_maps = [sem(f"map_scattered{b}") for b in range(2)]
        s_slot = sem("pool_slot_copied")
        s_mapg = [sem(f"map_gathered{b}") for b in range(2)]
        s_mapv = sem("source_map_ready")
        s_ptr = sem("pointers_ready")
        s_deg = sem("degrees_ready")
        s_root = sem("degree_roots_ready")
        s_dense = [sem(f"dense_rows_stored{q}") for q in range(4)]
        s_phase = sem("dve_phase_done")
        s_head = sem("head_sums_gathered")
        s_span = sem("span_sums_in_psum")
        s_fix = sem("span_sums_ready")
        s_fixed = sem("table_complete")
        s_final = sem("final_scattered")
        s_bias = sem("bias_parts_ready")
        s_pick = sem("pick_ready")
        s_hop_init = sem("hop_cleared")
        s_x1_init = sem("x1_started")
        HALF = [range(0, 8), range(8, G)]
        s_own = sem("dve_prep_own")
        s_fixpart = sem("first_node_sums_ready")
        s_saved = sem("last_nodes_saved")
        WEIGHTS = 12 + 4 + 4 * 3 + 4

        B2K = [0, 1]

        def per_unit(*names):
            return [(n, b) for n in names for b in B2K]

        class Phase:

            def __init__(self, name, lns, rows_,
                         turned=None, copied=None, product=None, hidden=None, second=None,
                         taken=None, message=None, slot=None, krow=None, picked=None,
                         compared=None, merged=None, sums=None, ga_free=None, gx_free=None,
                         in_free=None, xin_free=None, state_ready=None, acc_ready=None,
                         out_ready=None, o_ready=None):
                def signal(kind, keys):
                    return Signal(sem(f"{name}_{kind}"), keys) if keys else None

                ln = [(n, q) for n, qs in lns for q in qs]
                self.dve = sem(name + "_dve_own")
                self.centred, self.squared = signal("centred", ln), signal("squared", ln)
                self.variance, self.deviation = signal("variance", ln), signal("deviation", ln)
                self.rows = signal("rows_ready", rows_)
                self.turned = signal("turned", turned)
                self.copied = signal("copied", copied)
                self.product = signal("product", product)
                self.hidden = signal("hidden", hidden)
                self.second = signal("second", second)
                self.taken = signal("taken", taken)
                self.message = signal("message", message)
                self.slot = signal("slot", slot)
                self.krow = signal("krow", krow)
                self.picked = signal("picked", picked)
                self.compared = signal("compared", compared)
                self.merged = signal("merged", merged)
                self.sums = signal("sums", sums)
                self.ga_free = signal("ga_free", ga_free)
                self.gx_free = signal("gx_free", gx_free)
                self.in_free = signal("in_free", in_free)
                self.xin_free = signal("xin_free", xin_free)
                self.state_ready = signal("state_ready", state_ready)
                self.acc_ready = signal("acc_ready", acc_ready)
                self.out_ready = signal("out_ready", out_ready)
                self.o_ready = signal("o_ready", o_ready)

        LANES = range(4)
        PAIRS = ((0, 1), (2, 3))

        def staggered(*names):
            return [(n, q) for n in names for q in LANES]

        dn = Phase("dense", [("l1", LANES), ("l2", LANES), ("l3", LANES)], staggered("h1", "h2", "h3"),
                   turned=staggered("h1", "h2", "h3"), copied=staggered("h1", "h2", "h3"),
                   product=[(n, q) for names, lanes in
                            [(("h1",), p) for p in PAIRS] + [(("h2",), p) for p in PAIRS] + [(("even", "odd"), p) for p in PAIRS]
                            for n in names for q in lanes],
                   hidden=[(n, q) for names, lanes in
                           [(("h2",), p) for p in PAIRS] + [(("even", "odd"), p) for p in PAIRS]
                           for n in names for q in lanes],
                   second=staggered("h2", "h3"), taken=staggered("x2", "x3", "out"))
        dn_load = [sem(f"dense_loaded{q}") for q in LANES]

        hops = []
        for k in range(2):
            f = Phase(f"hop{k}", [("l", B2K)] if k == 0 else [], per_unit("m"),
                      slot=per_unit("k"), turned=per_unit("k"), krow=per_unit("k"),
                      picked=[("k", b, j) for b in B2K for j in B2K], compared=[("k", b, j) for b in B2K for j in B2K],
                      merged=per_unit("m"), sums=per_unit("m"))
            f.got = [sem(f"hop{k}_gathered{b}") for b in B2K]
            f.added = sem(f"hop{k}_added")
            hops.append(f)

        sp_ = []
        for k in range(2):
            v = per_unit("v") if k == 1 else None
            f = Phase(f"s{k}", [("l", B2K)], v, turned=v, copied=v, product=v, taken=v,
                      ga_free=per_unit("g"), in_free=per_unit("x") if k == 1 else None,
                      state_ready=per_unit("x"), acc_ready=per_unit("a"))
            f.got = [sem(f"s{k}_gathered{b}") for b in B2K]
            f.load = [sem(f"s{k}_loaded{b}") for b in B2K] if k == 1 else None
            f.stored = [sem(f"s{k}_sums_stored{b}") for b in B2K]
            f.kept = [sem(f"s{k}_state_stored{b}") for b in B2K]
            sp_.append(f)

        T_TURNED = per_unit("ef", "us", "vd", "ud", "m0", "m1", "u0", "u1")
        T_MLP = per_unit("us", "ud", "m0", "m1", "u0", "u1")
        tt = Phase("t", [("d1", B2K), ("d2", B2K), ("s3", B2K), ("d3", B2K)],
                   per_unit("us", "vd", "ud", "h3", "agg"),
                   turned=T_TURNED, copied=T_TURNED,
                   product=per_unit("us", "vd", "ud", "m0", "m1", "u0", "u1"),
                   hidden=T_MLP, second=T_MLP, message=per_unit("m0", "m1"),
                   taken=per_unit("us", "vd", "ud", "u0", "u1"),
                   in_free=per_unit("x"), gx_free=per_unit("g"), ga_free=per_unit("g"), o_ready=per_unit("o"))
        tt.load = [sem(f"t_loaded{b}") for b in range(2)]
        tt.got_a = [sem(f"t_sums_gathered{b}") for b in range(2)]
        tt.got_x = [sem(f"t_nodes_gathered{b}") for b in range(2)]
        tt.kept = [sem(f"t_suffix_stored{b}") for b in range(2)]
        tt.written = [sem(f"t_rows_written{b}") for b in range(2)]
        s_border = sem("border_dve_steps")
        s_bpe = sem("border_products")

        block = ctx.enter_context(nc.Block())

        def drow(i, b):
            if isinstance(i, int):
                return min((4 * i + b) * P * G, N - P * G)
            return (4 * i + b) * (P * G)

        def ecol(i, b):
            return (2 * i + b) * G

        def tcol(i, b):
            return (U - 1 - b) * G - 2 * G * i

        @block.sync
        def _(sp):
            after = Settled(sp, sem("sp_waits_passed"))
            n = (P - 1) * EC
            after.wait_ge(s_pad, 7)
            for t, s in ((dst_i, dst), (src_i, src), (wt, edge_weight)):
                sp.dma_start(t[0:P - 1, 0:EC], s[0:n].rearrange("(p c) -> p c", c=EC)).then_inc(s_edges, 16)
                sp.dma_start(t[P - 1:P, 0:ELAST], s[n:E].rearrange("(p c) -> p c", p=1)).then_inc(s_edges, 16)
            sp.dma_start(nxt_i[0:P - 1, 0:EC], dst[1:n + 1].rearrange("(p c) -> p c", c=EC)).then_inc(s_edges, 16)
            sp.dma_start(nxt_i[P - 1:P, 0:ELAST - 1], dst[n + 1:E].rearrange("(p c) -> p c", p=1)).then_inc(s_edges, 16)
            sp.dma_start(prv_i[0:1, 1:EC], dst[0:EC - 1].rearrange("(p c) -> p c", p=1)).then_inc(s_edges, 16)
            sp.dma_start(prv_i[1:P - 1, 0:EC], dst[EC - 1:n - 1].rearrange("(p c) -> p c", c=EC)).then_inc(s_edges, 16)
            sp.dma_start(prv_i[P - 1:P, 0:ELAST], dst[n - 1:E - 1].rearrange("(p c) -> p c", p=1)).then_inc(s_edges, 16)
            with nc.allow_non_contiguous_dma(reason="126 single keys"):
                sp.dma_start(kn_i[0:P - 2, :], dst[EC:n].rearrange("(p c) -> p c", c=EC)[:, EC - 1:EC]).then_inc(s_edges, 16)
            after.wait_ge(s_zero, 1)
            cleared = node_map.rearrange("(p a) b -> p (a b)", p=125)
            for j in range(4):
                w = 2 * N // 125 // 4
                sp.dma_start(cleared[:, j * w:j * w + w], zeros[0:125, 0:w]).then_inc(s_cleared, 16)
            cleared = hop.rearrange("a b -> (a b)").rearrange("(p k w) -> p k w", p=P, k=HC)
            w = (N + 2 * P) * D // P // HC
            sp.dma_start(cleared, zeros[:, 0:w].unsqueeze(1).broadcast_to([P, HC, w])).then_inc(s_hop_init, 16)
            for j in range(4):
                at = slice(j * N // 4, (j + 1) * N // 4)
                sp.dma_start(x1[at, :], x[at, :]).then_inc(s_x1_init, 16)
            sp.dma_start(x1[N:N + 2 * P, :].rearrange("(p a) d -> p (a d)", p=P), zeros[:, 0:2 * D]).then_inc(s_x1_init, 16)
            for t in tables:
                sp.dma_start(t[ROWS:ROWS + P, :], zeros[:, 0:D]).then_inc(s_cleared, 16)
            after.wait_ge(s_const, 1)
            lo, hi = slice(0, D), slice(D, P)
            for o, s in ((wg[lo, 0:D], W1g), (wg[hi, D:P], W1g), (w2a[lo, 0:D], W2a), (w2a[hi, D:P], W2a),
                         (w2b[lo, 0:D], W2b), (w2b[hi, D:P], W2b), (m1[:, :], mW1[0:P, :]), (m2[:, :], mW2),
                         (u1[:, :], uW1), (u1s[lo, 0, :], uW1[0:D, :]), (u1s[hi, 1, :], uW1[0:D, :]),
                         (u2[:, :], uW2)):
                sp.dma_start(o, s).then_inc(s_weights, 16)
            for j in range(4):
                sp.dma_start(m1e[DE * j:DE * j + DE, j, :], mW1[P:P + DE, :]).then_inc(s_weights, 16)
            for j, v in enumerate((b1g, b2b, mb2, ub2)):
                for p in range(3):
                    sp.dma_start(bias_f[p:p + 1, j, :].rearrange("p (r d) -> p r d", d=D),
                                 v.rearrange("(p r d) -> p r d", p=1, r=1).broadcast_to([1, 512 // D, D])).then_inc(s_weights, 16)
            with nc.allow_non_contiguous_dma(reason="bias columns"):
                for o, v in ((bcol[lo, 0:1], b2a), (bcol[hi, 0:1], b2a), (bcol[:, 1:2], mb1), (bcol[:, 2:3], ub1)):
                    sp.dma_start(o, v.rearrange("(d p) -> d p", p=1)).then_inc(s_weights, 16)

            def node_rows(t, i, q):
                return t[bass.ds(drow(i, q), P * G), :].rearrange("(p g) d -> p g d", g=G)

            def dense_load(i, q):
                sp.dma_start(full(lane_x[q]), node_rows(x1, i, q)).then_inc(dn_load[q], 16)

            def dense(i, more_steps=True):
                for q in LANES:
                    if more_steps:
                        after.wait_ge(*dn.taken.at(i, ("x2", q)))
                        dense_load(i + 1, q)
                for q in LANES:
                    after.wait_ge(*dn.taken.at(i, ("out", q)))
                    if not more_steps and q == 3:
                        after.wait_ge(s_dense[2], 16 * DSTEPS)
                    sp.dma_start(node_rows(out, i, q), full(lane_o[q])).then_inc(s_dense[q], 16)

            after.wait_ge(hops[1].added, 16 * G * U)
            for q in LANES:
                dense_load(0, q)
            dense(0)
            with sp.Fori(1, DSTEPS - 2) as i:
                dense(i)
            dense(DSTEPS - 2)
            dense(DSTEPS - 1, False)

            for k, f in enumerate(sp_):
                def load(i, b):
                    for t, s in ((xin, xs1), (hin, ms1)):
                        sp.dma_start(flat(t[b]), s[:, bass.ds(ecol(i, b) * D, W)]).then_inc(f.load[b], 16)

                def body(i, more_steps=True):
                    for b in B2K:
                        if more_steps and k == 1:
                            after.wait_ge(*f.in_free.at(i, ("x", b)))
                            load(i + 1, b)
                    for b in B2K:
                        at = bass.ds(ecol(i, b) * D, W)
                        after.wait_ge(*f.state_ready.at(i, ("x", b)))
                        state, rest = ((ga, xs1), (h, ms1)) if k == 0 else ((xw, xs2), (h, hs2))
                        for t, s in (state, rest):
                            sp.dma_start(s[:, at], flat(t[b])).then_inc(f.kept[b], 16)
                        after.wait_ge(*f.acc_ready.at(i, ("a", b)))
                        sp.dma_start(rows(tables[k])[:, at], flat(acc[b])).then_inc(f.stored[b], 16)

                if k == 1:
                    for b in B2K:
                        after.wait_ge(sp_[0].kept[b], 16 * STEPS * 2)
                        load(0, b)
                body(0)
                with sp.Fori(1, STEPS - 1) as i:
                    body(i)
                body(STEPS - 1, False)

            def t_load(i, b):
                at = bass.ds(tcol(i, b) * D, W)
                for t, s in ((xin, xs2), (hin, hs2), (a3, rows(tables[0])), (a4, rows(tables[1]))):
                    sp.dma_start(flat(t[b]), s[:, at]).then_inc(tt.load[b], 16)
                n = (P - 1) * EC
                c = tcol(i, b)
                first = isinstance(i, int) and i == 0 and b == 0
                w = G - 1 if first else G
                sp.dma_start(ef[b][0:P - 1, 0:w, :],
                             edge_attr[0:n, :].rearrange("(p c) d -> p (c d)", c=EC)[:, bass.ds(c * DE, w * DE)]
                             .rearrange("p (c d) -> p c d", d=DE)).then_inc(tt.load[b], 16)
                tail(i, b, c)

            def tail(i, b, c):
                n = (P - 1) * EC
                left = ELAST - c if isinstance(c, int) else G
                w = max(0, min(G, left))
                if w:
                    sp.dma_start(ef[b][P - 1:P, 0:w, :],
                                 edge_attr[n:E, :].rearrange("(p c) d -> p (c d)", p=1)[:, bass.ds(c * DE, w * DE)]
                                 .rearrange("p (c d) -> p c d", d=DE)).then_inc(tt.load[b], 16)
                else:
                    sp.dma_start(ef[b][P - 1:P, :, :],
                                 zeros[P - 1:P, 0:G * DE].rearrange("p (c d) -> p c d", d=DE)).then_inc(tt.load[b], 16)

            def t_body(i, more_steps=True):
                for b in B2K:
                    if more_steps:
                        after.wait_ge(*tt.in_free.at(i, ("x", b)))
                        t_load(i + 1, b)
                for b in B2K:
                    after.wait_ge(*tt.rows.at(i, ("agg", b)))
                    sp.dma_start(rows(suffix)[:, bass.ds(tcol(i, b) * D, W)].rearrange("p (g d) -> p g d", d=D),
                                 cc[b][:, :, 2 * D:3 * D]).then_inc(tt.kept[b], 16)

            after.wait_ge(s_phase, 3)
            after.wait_ge(s_fixed, 2 * 32)
            for b in B2K:
                after.wait_ge(sp_[1].kept[b], 16 * STEPS * 2)
            for b in B2K:
                t_load(0, b)
            apart = 2
            for i in range(apart):
                t_body(i)
            with sp.Fori(apart, STEPS - 1) as i:
                t_body(i)
            t_body(STEPS - 1, False)
            for q in LANES:
                after.wait_ge(s_dense[q], 16 * DSTEPS)
            for b in B2K:
                after.wait_ge(tt.kept[b], 16 * STEPS)
                after.wait_ge(tt.written[b], 16 * G * STEPS)
            after.wait_ge(s_final, 16)

        @block.gpsimd
        def _(pool):
            after = Settled(pool, sem("pool_waits_passed"))
            nc.gpsimd.memset(zeros[:, :], 0.0).then_inc(s_zero, 1)
            for t, v in ((dst_i, N), (nxt_i, N), (prv_i, -1), (src_i, 0), (kn_i, N)):
                nc.gpsimd.memset(t[:, :], v).then_inc(s_pad, 1)
            nc.gpsimd.memset(wt[:, :], 0.0).then_inc(s_pad, 1)
            nc.gpsimd.memset(ef[0][:, :, :], 0.0).then_inc(s_pad, 1)
            nc.gpsimd.memset(ones[:, :], 1.0).then_inc(s_rowno, 1)
            nc.gpsimd.iota(rowno[:, :], pattern=[[1, T]], base=0, channel_multiplier=T,
                           allow_small_or_imprecise_dtypes=True).then_inc(s_rowno, 1)
            after.wait_ge(s_rowno, 1)
            nc.gpsimd.affine_select(out=ident[:, :], in_=ones[:, :], pattern=[[-1, P]], base=0, channel_multiplier=1,
                                    compare_op=ALU.is_equal, fill=0.0).then_inc(s_rowno, 1)
            nc.gpsimd.affine_select(out=upper[:, :], in_=ones[:, :], pattern=[[1, P]], base=0, channel_multiplier=-1,
                                    compare_op=ALU.is_gt, fill=0.0).then_inc(s_rowno, 1)
            nc.gpsimd.affine_select(out=rows3[:, :], in_=ones[:, :], pattern=[[0, P]], base=3, channel_multiplier=-1,
                                    compare_op=ALU.is_gt, fill=0.0).then_inc(s_rowno, 1)
            for j in range(2):
                nc.gpsimd.affine_select(out=lower[:, j, 0:P], in_=ones[:, :], pattern=[[-1, P]], base=j * P,
                                        channel_multiplier=1, compare_op=ALU.is_gt, fill=0.0).then_inc(s_rowno, 1)
                nc.gpsimd.affine_select(out=lower[:, j, P:2 * P], in_=ones[:, :], pattern=[[-1, P]], base=(j - 1) * P,
                                        channel_multiplier=1, compare_op=ALU.is_gt, fill=0.0).then_inc(s_rowno, 1)
            nc.gpsimd.iota(spare[:, :], pattern=[[0, T // 2], [P, 2]], base=N, channel_multiplier=1,
                           allow_small_or_imprecise_dtypes=True).then_inc(s_rowno, 1)
            nodes_max = pool.to_reg(N - 1)
            rows_max = pool.to_reg(ROWS + P - 1)

            def slot_copy(o, i_):
                return nc.gpsimd.tensor_copy(o, i_).then_inc(s_slot, 1)

            def gather(o, table, idx, limit, s, columns=range(G)):
                for g in columns:
                    nc.gpsimd.indirect_dma_start(
                        o[:, g, :], None, table, bass.IndirectOffsetOnAxis(idx[:, g:g + 1], 0),
                        bounds_check=limit, oob_is_err=False).then_inc(s, 16)

            after.wait_ge(s_bias, 1)
            nc.gpsimd.memset(pick[:, :, :], 1.0).then_inc(s_pick, 1)
            after.wait_ge(s_pick, 1)
            nc.gpsimd.affine_select(out=pick[:, :, :], in_=pick[:, :, :], pattern=[[-1, G], [0, P]], base=0,
                                    channel_multiplier=1, compare_op=ALU.is_equal, fill=0.0).then_inc(s_pick, 1)
            after.wait_ge(s_prep, 1)
            base = 0
            spare_max = pool.to_reg(N + 2 * P - 1)
            for k, f in enumerate(hops):
                table, sums = (x, hop) if k == 0 else (hop, x1)
                after.wait_ge(*((s_hop_init, 16) if k == 0 else (s_x1_init, 5 * 16)))
                for b in B2K:
                    slot_copy(isl[b][:, :], dstc_i[:, b * G:b * G + G])
                    after.wait_ge(s_slot, base + b + 1)
                    gather(ga[b], table, isl[b], nodes_max, f.got[b])
                base += 2

                def body(i, more_steps=True):
                    for b in B2K:
                        after.wait_ge(*f.sums.at(i, ("m", b)))
                        slot_copy(osl[b][:, :], kidx[:, bass.ds(ecol(i, b), G)])
                        if more_steps:
                            slot_copy(isl[b][:, :], dstc_i[:, bass.ds(ecol(i + 1, b), G)])
                        after.wait_ge(s_slot, base + 4 * i + 2 * b + 2 if more_steps else base + 4 * i + b + 1)
                        for q in range(HB):
                            if not (isinstance(i, int) and i == 0 and b == 0 and q == 0):
                                after.wait_ge(f.added, 32 * ((2 * i + b) * HB + q))
                            for g in (2 * q, 2 * q + 1):
                                nc.gpsimd.indirect_dma_start(
                                    sums, bass.IndirectOffsetOnAxis(osl[b][:, g:g + 1], 0), acc[b][:, g, :], None,
                                    bounds_check=spare_max, oob_is_err=True, compute_op=ALU.add).then_inc(f.added, 16)
                            if more_steps:
                                gather(ga[b], table, isl[b], nodes_max, f.got[b], (2 * q, 2 * q + 1))

                body(0)
                with pool.Fori(1, STEPS - 1) as i:
                    body(i)
                body(STEPS - 1, False)
                base += 4 * STEPS - 2
                after.wait_ge(f.added, 16 * G * U)

            after.wait_ge(s_mapin, 1)
            after.wait_ge(s_cleared, 6 * 16)

            def map_scatter(i, first):
                for b in B2K:
                    if not first:
                        after.wait_ge(s_maps[b], 16 * G * i)
                    slot_copy(isl[b][:, :], map_idx[:, bass.ds(ecol(i, b), G)])
                    slot_copy(msl[b][:, :, :], map_rows[:, bass.ds(ecol(i, b), G), :])
                    after.wait_ge(s_slot, base + 4 * i + 2 * b + 2)
                    for g in range(G):
                        nc.gpsimd.indirect_dma_start(
                            node_map, bass.IndirectOffsetOnAxis(isl[b][:, g:g + 1], 0), msl[b][:, g, :], None,
                            bounds_check=nodes_max, oob_is_err=False).then_inc(s_maps[b], 16)

            steps(pool, STEPS, map_scatter)
            base += 4 * STEPS
            for b in B2K:
                after.wait_ge(s_maps[b], 16 * G * STEPS)

            def map_gather(i, first):
                for b in B2K:
                    if not first:
                        after.wait_ge(s_mapg[b], 16 * G * i)
                        nc.gpsimd.tensor_copy(src_map[:, bass.ds(ecol(i - 1, b), G), :], msl[b][:, :, :]).then_inc(s_mapv, 1)
                        after.wait_ge(s_mapv, 2 * (i - 1) + b + 1)
                    slot_copy(isl[b][:, :], src_i[:, bass.ds(ecol(i, b), G)])
                    after.wait_ge(s_slot, base + 2 * i + b + 1)
                    for g in range(G):
                        nc.gpsimd.indirect_dma_start(
                            msl[b][:, g, :], None, node_map, bass.IndirectOffsetOnAxis(isl[b][:, g:g + 1], 0),
                            bounds_check=nodes_max, oob_is_err=False).then_inc(s_mapg[b], 16)

            steps(pool, STEPS, map_gather)
            base += 2 * STEPS
            for b in B2K:
                after.wait_ge(s_mapg[b], 16 * G * STEPS)
                nc.gpsimd.tensor_copy(src_map[:, ecol(STEPS - 1, b):ecol(STEPS - 1, b) + G, :], msl[b][:, :, :]).then_inc(s_mapv, 1)

            for k, f in enumerate(sp_):
                if k == 0:
                    table, index, limit = x1, src_i, nodes_max
                else:
                    table, index, limit = tables[k - 1], ptr_i, rows_max
                    after.wait_ge(s_ptr, 1)
                    for b in B2K:
                        after.wait_ge(sp_[0].kept[b], 2 * 16 * STEPS)

                def body(i, first):
                    for b in B2K:
                        if not first:
                            after.wait_ge(*f.ga_free.at(i - 1, ("g", b)))
                            if k == 0:
                                after.wait_ge(f.kept[b], 2 * 16 * i)
                        slot_copy(isl[b][:, :], index[:, bass.ds(ecol(i, b), G)])
                        after.wait_ge(s_slot, base + 2 * i + b + 1)
                        gather(ga[b], table, isl[b], limit, f.got[b])

                steps(pool, STEPS, body)
                base += 2 * STEPS
                for b in B2K:
                    after.wait_ge(f.stored[b], 16 * STEPS)
                if k == 0:
                    after.wait_ge(s_prep, 1)
                nc.gpsimd.indirect_dma_start(hsum[:, :], None, tables[k], bass.IndirectOffsetOnAxis(head_i[:, :], 0),
                                             bounds_check=rows_max, oob_is_err=False).then_inc(s_head, 16)
                after.wait_ge(s_fix, k + 1)
                nc.gpsimd.indirect_dma_start(tables[k], bass.IndirectOffsetOnAxis(head_i[:, :], 0), fix[:, 0:D], None,
                                             bounds_check=rows_max, oob_is_err=False).then_inc(s_fixed, 16)
                pool.dma_start(rows(tables[k])[:, EC * D:T * D], fix[:, D:2 * D]).then_inc(s_fixed, 16)
                after.wait_ge(s_fixed, 32 * (k + 1))

            def t_gather(i, first):
                for b in B2K:
                    if not first:
                        after.wait_ge(*tt.ga_free.at(i - 1, ("g", b)))
                        after.wait_ge(*tt.gx_free.at(i - 1, ("g", b)))
                    slot_copy(isl[b][:, :], ptr_i[:, bass.ds(tcol(i, b), G)])
                    slot_copy(isl2[b][:, :], dstc_i[:, bass.ds(tcol(i, b), G)])
                    if first:
                        after.wait_ge(s_slot, base + 2 * b + 2)
                    else:
                        after.wait_ge(s_slot, base + 6 * (i - 1) + 4 + 2 * b + 2)
                    gather(gx[b], x1, isl2[b], nodes_max, tt.got_x[b])
                    gather(ga[b], tables[1], isl[b], rows_max, tt.got_a[b])

            def t_scatter(i, first=False, more_steps=True):
                for b in B2K:
                    after.wait_ge(*tt.o_ready.at(i, ("o", b)))
                    if not first:
                        after.wait_ge(tt.written[b], 16 * G * i)
                    slot_copy(osl[b][:, :], out_idx[:, bass.ds(tcol(i, b), G)])
                    after.wait_ge(s_slot, base + 6 * i + 4 + (4 if more_steps else 0) + b + 1)
                    for g in range(G):
                        nc.gpsimd.indirect_dma_start(
                            out, bass.IndirectOffsetOnAxis(osl[b][:, g:g + 1], 0), acc[b][:, g, :], None,
                            bounds_check=nodes_max, oob_is_err=False).then_inc(tt.written[b], 16)

            for q in LANES:
                after.wait_ge(s_dense[q], 16 * DSTEPS)
            t_gather(0, True)
            t_gather(1, False)
            t_scatter(0, True)
            with pool.Fori(1, STEPS - 1) as i:
                t_gather(i + 1, False)
                t_scatter(i)
            t_scatter(STEPS - 1, more_steps=False)
            for b in B2K:
                after.wait_ge(tt.kept[b], 16 * STEPS)
            nc.gpsimd.indirect_dma_start(hsum[:, :], None, suffix, bass.IndirectOffsetOnAxis(tail_i[:, :], 0),
                                         bounds_check=rows_max, oob_is_err=False).then_inc(s_head, 16)
            after.wait_ge(s_border, 5)
            nc.gpsimd.indirect_dma_start(out, bass.IndirectOffsetOnAxis(brd_i[:, :], 0), fix[:, 0:D], None,
                                         bounds_check=nodes_max, oob_is_err=False).then_inc(s_final, 16)


        @block.tensor
        def _(pe):
            def turn(o, blocks, signal, key):
                for j, blk in enumerate(blocks):
                    w = blk.shape[1]
                    t = nc.tensor.transpose(o[0:w, j * P:j * P + P], blk, ident[:, :])
                signal.raise_by(t, key)

            def product(o, weights, src_, b, extra=None, signal=None, key=None):
                for c in range(0, W, 512):
                    n = min(512, W - c)
                    t = nc.tensor.matmul(o[:, c:c + n], weights, flat(src_)[:, c:c + n], start=True, stop=extra is None)
                    if extra is not None:
                        for j in range(c // P, (c + n) // P):
                            g = extra + j
                            t = nc.tensor.matmul(o[:, j * P:j * P + P], m1e[:, g % 4, :],
                                                 eft[b][:, (g // 4) * P:(g // 4) * P + P],
                                                 start=False, stop=j == (c + n) // P - 1)
                signal.raise_by(t, key)

            def by_row(o, sources, weights, k, signal, key):
                w = weights.shape[1]
                for n_src, src_ in enumerate(sources):
                    for c in range(0, HB * w, 512):
                        n = min(512, HB * w - c)
                        at = 512 * n_src + c
                        nc.tensor.matmul(o[:, at:at + n], rows3[:, :], bias[:, k, 0:n], start=True, stop=False)
                        for j in range(c // w, (c + n) // w):
                            t = nc.tensor.matmul(o[:, at - c + j * w:at - c + j * w + w], src_[:, j * P:j * P + P], weights,
                                                 start=False, stop=j == (c + n) // w - 1)
                signal.raise_by(t, key)

            pe.wait_ge(s_diag, 2)
            nc.tensor.matmul(tp[0][:, 0:P], ones[:, :], diag[:, 0, :], start=True, stop=True)
            nc.tensor.matmul(tp[0][:, P:2 * P], ones[:, :], diag[:, 1, :], start=True, stop=True).then_inc(s_kfp, 1)
            pe.wait_ge(s_mats, 1)
            nc.tensor.matmul(tp[1][:, 0:1], mh[:, :], small[:, 5:6], start=True, stop=True)
            nc.tensor.matmul(tp[1][:, 1:2], mt1[:, :], small[:, 5:6], start=True, stop=False)
            nc.tensor.matmul(tp[1][:, 1:2], mt2[:, :], small[:, 4:5], start=False, stop=True).then_inc(s_cc, 1)
            pe.wait_ge(s_weights, WEIGHTS * 16)
            pe.wait_ge(s_prep, 1)
            pe.wait_ge(s_pick, 2)

            def span(k, tails, heads):
                nc.tensor.matmul(tp[0][:, 0:D], mh[:, :], tails, start=True, stop=True)
                nc.tensor.matmul(tp[0][:, D:2 * D], mt1[:, :], tails, start=True, stop=False)
                nc.tensor.matmul(tp[0][:, D:2 * D], mt2[:, :], heads, start=False, stop=True).then_inc(s_span, 1)

            for k, f in enumerate(hops):
                def body(i, first):
                    for b in B2K:
                        pe.wait_ge(*f.slot.at(i, ("k", b)))
                        f.turned.raise_by(nc.tensor.transpose(tp[b][0:G, W:W + P], kslot[b][:, :], ident[:, :]), ("k", b))
                    for b in B2K:
                        pe.wait_ge(*f.krow.at(i, ("k", b)))
                        for j, columns in enumerate(HALF):
                            if b == 1:
                                pe.wait_ge(*f.compared.at(i, ("k", 0, j)))
                            elif not first:
                                pe.wait_ge(*f.compared.at(i - 1, ("k", 1, j)))
                            for g in columns:
                                t = nc.tensor.matmul(mm[j][:, (g - columns[0]) * P:(g - columns[0] + 1) * P], pick[:, g, :],
                                                     krow[b][:, :], start=True, stop=True)
                            f.picked.raise_by(t, ("k", b, j))
                    for b in B2K:
                        pe.wait_ge(*f.compared.at(i, ("k", b, 1)))
                        pe.wait_ge(*f.rows.at(i, ("m", b)))
                        if not first:
                            pe.wait_ge(*f.sums.at(i - 1, ("m", b)))
                        for g in range(G):
                            for n in range(2):
                                o = g - g % 2 + n
                                t = nc.tensor.matmul(tp[b][:, g * D:g * D + D], equal[b][:, o, (g % 2) * P:(g % 2) * P + P],
                                                     us[b][:, o, :], start=n == 0, stop=n == 1)
                        f.merged.raise_by(t, ("m", b))

                steps(pe, STEPS, body)

            def dense(i, first):
                def job(lanes, n):
                    for q in lanes:
                        pe.wait_ge(*dn.rows.at(i, (n, q)))
                        if n == "h1" and not first:
                            pe.wait_ge(*dn.taken.at(i - 1, ("out", q)))
                        turn(lane_p[q], [flat(lane_h[q])[:, j * P:j * P + P] for j in range(HB)], dn.turned, (n, q))
                    if n == "h1":
                        for q in lanes:
                            pe.wait_ge(*dn.copied.at(i, (n, q)))
                            by_row(lane_p[q], [flat(lane_v[q])], wg[:, :], BG, dn.product, (n, q))
                    if n == "h2":
                        for q in lanes:
                            pe.wait_ge(*dn.copied.at(i, (n, q)))
                            product(lane_p[q], w2a[:, :], lane_v[q], q, None, dn.product, (n, q))
                        for q in lanes:
                            pe.wait_ge(*dn.hidden.at(i, (n, q)))
                            by_row(lane_p[q], [flat(lane_z[q])], w2b[:, :], B2, dn.second, (n, q))
                    if n == "h3":
                        for q in lanes:
                            pe.wait_ge(*dn.copied.at(i, (n, q)))
                            product(lane_p[q], u1s[:, 0, :], lane_v[q], q, None, dn.product, ("even", q))
                        for q in lanes:
                            pe.wait_ge(*dn.hidden.at(i, ("even", q)))
                            product(lane_p[q], u1s[:, 1, :], lane_v[q], q, None, dn.product, ("odd", q))
                        for q in lanes:
                            pe.wait_ge(*dn.hidden.at(i, ("odd", q)))
                            by_row(lane_p[q], [flat(lane_z[q]), flat(lane_v[q])], u2[:, :], BU, dn.second, (n, q))

                for n in ("h1", "h2", "h3"):
                    for lanes in PAIRS:
                        job(lanes, n)

            steps(pe, DSTEPS, dense)

            for k, f in enumerate(sp_):
                def body(i, first):
                    for b in B2K:
                        pe.wait_ge(*f.rows.at(i, ("v", b)))
                        turn(tp[b], [flat(us[b])[:, j * P:j * P + P] for j in range(HB)], f.turned, ("v", b))
                    for b in B2K:
                        if not first:
                            pe.wait_ge(*f.taken.at(i - 1, ("v", b)))
                        pe.wait_ge(*f.copied.at(i, ("v", b)))
                        by_row(mm[b], [flat(vt[b])], wg[:, :], BG, f.product, ("v", b))

                if k == 1:
                    steps(pe, STEPS, body)
                pe.wait_ge(*f.acc_ready.at(STEPS - 1, ("a", 1)))
                pe.wait_ge(s_head, 16 * (k + 1))
                span(k, acc[1][:, EC - 1 - T + G, :], hsum[:, :])

            def turn_job(i, n, blocks_of, *waits):
                for b in B2K:
                    for w in waits:
                        pe.wait_ge(*w(b))
                    turn(tp[b], blocks_of(b), tt.turned, (n, b))

            def blocks7(t):
                return lambda b: [flat(t[b])[:, j * P:j * P + P] for j in range(HB)]

            def last_pass(i, first):
                if not first:
                    for b in B2K:
                        pe.wait_ge(*tt.taken.at(i - 1, ("u1", b)))
                for b in B2K:
                    pe.wait_ge(*tt.rows.at(i, ("us", b)))
                    e = ef[b][:, :, :].rearrange("p g d -> p (g d)")
                    turn(tp[b], [e[:, c:min(c + P, G * DE)] for c in range(0, G * DE, P)], tt.turned, ("ef", b))
                turn_job(i, "us", blocks7(us), lambda b: tt.copied.at(i, ("ef", b)))
                for b in B2K:
                    pe.wait_ge(*tt.copied.at(i, ("us", b)))
                    product(mm[b], w2a[:, :], vt[b], b, None, tt.product, ("us", b))
                for b in B2K:
                    pe.wait_ge(*tt.hidden.at(i, ("us", b)))
                    by_row(tp[b], [flat(zz[b])], w2b[:, :], B2, tt.second, ("us", b))
                turn_job(i, "vd", blocks7(xw), lambda b: tt.rows.at(i, ("vd", b)), lambda b: tt.taken.at(i, ("us", b)))
                for b in B2K:
                    pe.wait_ge(*tt.copied.at(i, ("vd", b)))
                    by_row(mm[b], [flat(vt[b])], wg[:, :], BG, tt.product, ("vd", b))
                turn_job(i, "ud", blocks7(h), lambda b: tt.rows.at(i, ("ud", b)))
                for b in B2K:
                    pe.wait_ge(*tt.copied.at(i, ("ud", b)))
                    pe.wait_ge(*tt.taken.at(i, ("vd", b)))
                    product(mm[b], w2a[:, :], vt[b], b, None, tt.product, ("ud", b))
                for b in B2K:
                    pe.wait_ge(*tt.hidden.at(i, ("ud", b)))
                    by_row(tp[b], [flat(zz[b])], w2b[:, :], B2, tt.second, ("ud", b))
                for part, c0, weights1, weights2, k in (("m", 0, m1, m2, BM), ("u", D, u1, u2, BU)):
                    for half in range(2):
                        n = f"{part}{half}"
                        before = {"m0": lambda b: tt.taken.at(i, ("ud", b)), "m1": lambda b: tt.message.at(i, ("m0", b)),
                                  "u0": lambda b: tt.message.at(i, ("m1", b)), "u1": lambda b: tt.taken.at(i, ("u0", b))}[n]
                        turn_job(i, n, lambda b: [cc[b][:, half * HB + j, c0:c0 + P] for j in range(HB)],
                                 lambda b: tt.rows.at(i, ("h3" if part == "m" else "agg", b)), before)
                        for b in B2K:
                            pe.wait_ge(*tt.copied.at(i, (n, b)))
                            product(mm[b], weights1[:, :], vt[b], b, half * HB if part == "m" else None, tt.product, (n, b))
                        for b in B2K:
                            pe.wait_ge(*tt.hidden.at(i, (n, b)))
                            by_row(tp[b], [flat(zz[b])], weights2[:, :], k, tt.second, (n, b))

            steps(pe, STEPS, last_pass)
            pe.wait_ge(s_head, 16 * 3)
            pe.wait_ge(*tt.taken.at(STEPS - 1, ("u1", 0)))
            span(2, hsum[:, :], cc[1][:, 0, 2 * D:3 * D])
            pe.wait_ge(s_border, 1)
            nc.tensor.transpose(tp[0][:, 0:P], brd[:, D:3 * D], ident[:, :]).then_inc(s_bpe, 1)
            pe.wait_ge(s_border, 2)
            nc.tensor.matmul(mm[0][:, 0:P], u1[:, :], bz[:, 0:P], start=True, stop=True).then_inc(s_bpe, 1)
            pe.wait_ge(s_border, 4)
            nc.tensor.matmul(tp[1][:, 0:D], rows3[:, :], bias[:, BU, 0:D], start=True, stop=False)
            nc.tensor.matmul(tp[1][:, 0:D], bz[:, P:2 * P], u2[:, :], start=False, stop=True).then_inc(s_bpe, 1)

        @block.scalar
        def _(act):
            def ln_squares(f, i, lanes, n):
                for q in lanes:
                    act.wait_ge(*f.centred.at(i, (n, q)))
                    f.squared.raise_by(nc.scalar.activation(full(lane_s[q]), full(lane_c[q]), ACT.Square), (n, q))

            def ln_stds(f, i, lanes, n):
                for q in lanes:
                    act.wait_ge(*f.variance.at(i, (n, q)))
                    f.deviation.raise_by(nc.scalar.activation(st[q][:, 2, :], st[q][:, 1, :], ACT.Sqrt, bias=eps[:, 0:1],
                                                        scale=1.0 / D), (n, q))

            def copy(f, i, n, after=None):
                for b in B2K:
                    act.wait_ge(*f.turned.at(i, (n, b)))
                    f.copied.raise_by(nc.scalar.copy(flat(vt[b]), tp[b][:, 0:W]), (n, b))

            def relu(f, i, n, k):
                for b in B2K:
                    act.wait_ge(*f.product.at(i, (n, b)))
                    f.hidden.raise_by(nc.scalar.activation(flat(zz[b]), mm[b][:, 0:W], ACT.Relu, bias=bcol[:, k:k + 1]),
                                      (n, b))

            act.wait_ge(s_weights, WEIGHTS * 16)
            act.wait_ge(s_const, 1)

            def dense(i, first):
                def copies(lanes, n):
                    for q in lanes:
                        act.wait_ge(*dn.turned.at(i, (n, q)))
                        dn.copied.raise_by(nc.scalar.copy(flat(lane_v[q]), lane_p[q][:, 0:W]), (n, q))

                def relus(lanes, n, k, o):
                    for q in lanes:
                        act.wait_ge(*dn.product.at(i, (n, q)))
                        dn.hidden.raise_by(nc.scalar.activation(flat(o[q]), lane_p[q][:, 0:W], ACT.Relu,
                                                                bias=bcol[:, k:k + 1]), (n, q))

                one_, two = PAIRS
                ln_squares(dn, i, one_, "l1")
                ln_stds(dn, i, one_, "l1")
                ln_squares(dn, i, two, "l1")
                copies(one_, "h1")
                ln_stds(dn, i, two, "l1")
                ln_squares(dn, i, one_, "l2")
                copies(two, "h1")
                ln_stds(dn, i, one_, "l2")
                ln_squares(dn, i, two, "l2")
                copies(one_, "h2")
                ln_stds(dn, i, two, "l2")
                relus(one_, "h2", 0, lane_z)
                ln_squares(dn, i, one_, "l3")
                copies(two, "h2")
                ln_stds(dn, i, one_, "l3")
                relus(two, "h2", 0, lane_z)
                ln_squares(dn, i, two, "l3")
                copies(one_, "h3")
                ln_stds(dn, i, two, "l3")
                relus(one_, "even", 2, lane_z)
                relus(one_, "odd", 2, lane_v)
                copies(two, "h3")
                relus(two, "even", 2, lane_z)
                relus(two, "odd", 2, lane_v)

            for k, f in enumerate(hops):
                def body(i, first):
                    for b in B2K:
                        if not first:
                            act.wait_ge(*f.turned.at(i - 1, ("k", b)))
                        if first and k == 1:
                            act.wait_ge(*hops[0].turned.at(STEPS - 1, ("k", b)))
                        f.slot.raise_by(nc.scalar.copy(kslot[b][:, :], key[:, bass.ds(ecol(i, b), G)]), ("k", b))
                    for b in B2K:
                        act.wait_ge(*f.turned.at(i, ("k", b)))
                        if not first:
                            act.wait_ge(*f.picked.at(i - 1, ("k", b, 1)))
                        if first and k == 1:
                            act.wait_ge(*hops[0].picked.at(STEPS - 1, ("k", b, 1)))
                        f.krow.raise_by(nc.scalar.copy(krow[b][:, :], tp[b][0:G, W:W + P]), ("k", b))
                    if k == 0:
                        ln_squares(f, i, B2K, "l")
                        ln_stds(f, i, B2K, "l")
                    for b in B2K:
                        act.wait_ge(*f.merged.at(i, ("m", b)))
                        if not first:
                            act.wait_ge(f.added, 16 * G * (2 * i - 1 + b))
                        if first and k == 1:
                            act.wait_ge(hops[0].added, 16 * G * U)
                        f.sums.raise_by(nc.scalar.copy(flat(acc[b]), tp[b][:, 0:W]), ("m", b))

                act.wait_ge(s_prep, 1)
                steps(act, STEPS, body)

            steps(act, DSTEPS, dense)

            act.wait_ge(s_deg, 2)
            nc.scalar.activation(dis_s[:, :], tmp[:, :], ACT.Sqrt, bias=one[:, 0:1]).then_inc(s_root, 1)
            nc.scalar.activation(dis_d[:, :], cnt[:, :], ACT.Sqrt, bias=one[:, 0:1]).then_inc(s_root, 1)

            for k, f in enumerate(sp_):
                def body(i, first):
                    if k == 1:
                        copy(f, i, "v")
                    ln_squares(f, i, B2K, "l")
                    ln_stds(f, i, B2K, "l")

                steps(act, STEPS, body)

            def last_pass(i, first):
                for b in B2K:
                    act.wait_ge(*tt.turned.at(i, ("ef", b)))
                    if not first:
                        act.wait_ge(*tt.product.at(i - 1, ("m1", b)))
                    nc.scalar.copy(eft[b][:, 0:3 * P], tp[b][:, 0:3 * P])
                    tt.copied.raise_by(nc.scalar.copy(eft[b][0:D, 3 * P:4 * P], tp[b][0:D, 3 * P:4 * P]), ("ef", b))
                copy(tt, i, "us")
                ln_squares(tt, i, B2K, "d1")
                ln_stds(tt, i, B2K, "d1")
                relu(tt, i, "us", 0)
                copy(tt, i, "vd")
                ln_squares(tt, i, B2K, "d2")
                ln_stds(tt, i, B2K, "d2")
                copy(tt, i, "ud")
                ln_squares(tt, i, B2K, "s3")
                ln_stds(tt, i, B2K, "s3")
                relu(tt, i, "ud", 0)
                ln_squares(tt, i, B2K, "d3")
                ln_stds(tt, i, B2K, "d3")
                for half in range(2):
                    copy(tt, i, f"m{half}")
                    relu(tt, i, f"m{half}", 1)
                    for b in B2K:
                        act.wait_ge(*tt.second.at(i, (f"m{half}", b)))
                        o = us[b][:, half * HB:half * HB + HB, :].rearrange("p g d -> p (g d)")
                        tt.message.raise_by(nc.scalar.copy(o, tp[b][:, 0:HB * D]), (f"m{half}", b))
                for half in range(2):
                    copy(tt, i, f"u{half}")
                    relu(tt, i, f"u{half}", 2)

            steps(act, STEPS, last_pass)

        @block.vector
        def _(dve):
            V = nc.vector
            dve_passed = sem("dve_waits_passed")

            prep = [0]

            def link(ins):
                prep[0] += 1
                ins.then_inc(s_own, 1)
                dve.wait_ge(s_own, prep[0])

            for t in (wg, w2a, w2b, bias_f, u1s, m1e, *eft):
                link(V.memset(t if isinstance(t, bass.AP) else t[:, :] if len(t.shape) == 2 else t[:, :, :], 0.0))
            link(V.memset(eps[:, :], EPS))
            V.memset(one[:, :], 1.0).then_inc(s_const, 1)
            dve.wait_ge(s_const, 1)
            dve.wait_ge(s_edges, 12 * 16)
            dve.wait_ge(s_rowno, 10)
            K, F, KN, TLEN, HLEN, TCNT, CARRY, BCNT, FNK, S0, S1 = (small[:, j:j + 1] for j in range(11))
            link(V.tensor_copy(dst_f[:, :], dst_i[:, :]))
            link(V.tensor_copy(nxt_f[:, :], nxt_i[:, :]))
            link(V.tensor_copy(prv_f[:, :], prv_i[:, :]))
            link(V.tensor_copy(K, dst_f[:, EC - 1:EC]))
            link(V.tensor_copy(F, dst_f[:, 0:1]))
            link(V.tensor_copy(KN, kn_i[:, :]))
            link(V.tensor_copy(dst_f[:, EC:T], K))
            link(V.tensor_tensor(flag[:, :], prv_f[:, :], dst_f[:, :], ALU.is_equal))
            link(V.tensor_copy(same[:, :], flag[:, :]))
            link(V.memset(same[:, 0:1], 0.0))
            link(V.tensor_tensor(more[:, :], nxt_f[:, :], dst_f[:, :], ALU.is_equal))
            link(V.memset(more[:, EC:T], 0.0))
            link(V.tensor_scalar(last[:, :], more[:, :], -1.0, 1.0, ALU.mult, ALU.add))
            link(V.tensor_copy(cont[:, :], more[:, :]))
            link(V.memset(cont[:, EC - 1:EC], 0.0))
            link(V.scalar_tensor_tensor(tmp[:, :], more[:, :], BIG, dst_f[:, :], ALU.mult, ALU.add))
            link(V.memset(tmp[:, EC:T], BIG))
            link(V.tensor_copy(map_idx[:, :], tmp[:, :]))
            link(V.tensor_scalar(tmp[:, :], dst_f[:, :], K, None, ALU.is_equal))
            link(V.tensor_reduce(TLEN, tmp[:, 0:EC], X, ALU.add))
            link(V.tensor_tensor(tmp[:, :], tmp[:, :], flag[:, :], ALU.max))
            link(V.scalar_tensor_tensor(tmp[:, :], tmp[:, :], BIG, dst_f[:, :], ALU.mult, ALU.add))
            link(V.tensor_copy(out_idx[:, :], tmp[:, :]))
            link(V.tensor_scalar(tmp[:, :], dst_f[:, :], float(N - 1), None, ALU.min))
            link(V.tensor_copy(dstc_i[:, :], tmp[:, :]))
            link(V.tensor_scalar(flag[:, :], dst_f[:, :], F, None, ALU.is_equal))
            link(V.memset(flag[:, EC:T], 0.0))
            link(V.tensor_reduce(HLEN, flag[:, 0:EC], X, ALU.add))
            link(V.scalar_tensor_tensor(S0, HLEN, -1.0, rowno[:, 0:1], ALU.add, ALU.add))
            link(V.tensor_copy(head_i[:, :], S0))
            link(V.scalar_tensor_tensor(S0, TLEN, -1.0, rowno[:, EC:T], ALU.mult, ALU.add))
            link(V.tensor_copy(tail_i[:, :], S0))
            link(V.tensor_tensor(S0, K, KN, ALU.is_equal))
            link(V.scalar_tensor_tensor(S1, S0, BIG, K, ALU.mult, ALU.add))
            link(V.tensor_copy(brd_i[:, :], S1))
            link(V.memset(tmp[:, :], 1.0))
            link(V.tensor_tensor_scan(cnt[:, :], same[:, :], tmp[:, :], 0.0, ALU.mult, ALU.add))
            link(V.tensor_copy(TCNT, cnt[:, EC - 1:EC]))
            link(V.tensor_copy(key[:, :], src_i[:, :]))
            link(V.scalar_tensor_tensor(tmp[:, :], dst_f[:, :], float(N), spare[:, :], ALU.is_equal, ALU.mult))
            link(V.tensor_copy(tmp[:, EC:T], spare[:, EC:T]))
            link(V.tensor_tensor(key[:, :], key[:, :], tmp[:, :], ALU.add))
            for j, border in ((0, K), (1, F)):
                V.tensor_scalar(diag[:, j, :], ident[:, :], border, None, ALU.mult).then_inc(s_diag, 1)
            dve.wait_ge(s_kfp, 1)
            link(V.tensor_copy(kf[:, :, :].rearrange("p a b -> p (a b)"), tp[0][:, 0:2 * P]))
            link(V.tensor_tensor(FNK, F, K, ALU.not_equal))
            link(V.scalar_tensor_tensor(mh[:, :], kf[:, 1, :], K, upper[:, :], ALU.is_equal, ALU.mult))
            link(V.tensor_scalar(mt1[:, :], kf[:, 0, :], K, None, ALU.is_equal))
            link(V.tensor_scalar(mt2[:, :], kf[:, 0, :], F, FNK, ALU.is_equal, ALU.mult))
            dve.sem_inc(s_mats, 1)
            dve.wait_ge(s_weights, WEIGHTS * 16)
            for p in range(3):
                link(V.tensor_copy(bias_part, bias_f))
                if p == 0:
                    link(V.tensor_scalar(bias[:, :, :], bias_part, ident[:, 0:1], None, ALU.mult))
                else:
                    link(V.scalar_tensor_tensor(bias[:, :, :], bias_part, ident[:, p:p + 1], bias[:, :, :], ALU.mult, ALU.add))
                if p < 2:
                    link(V.tensor_tensor(bias_f, bias_f, bias_part, ALU.subtract))
            dve.sem_inc(s_bias, 1)
            dve.wait_ge(s_cc, 1)
            link(V.tensor_copy(small[:, 6:8], tp[1][:, 0:2]))
            link(V.scalar_tensor_tensor(cnt[:, :], flag[:, :], CARRY, cnt[:, :], ALU.mult, ALU.add))
            link(V.tensor_copy(cnt[:, EC:T], BCNT))
            link(V.tensor_copy(map_rows[:, :, 0], rowno[:, :]))
            V.tensor_copy(map_rows[:, :, 1], cnt[:, :]).then_inc(s_mapin, 1)
            dve.sem_inc(s_prep, 1)

            def layer_norm(own, f, i, n, lanes, xs, hs, ready, scale=None, free=None, final=None):
                marks = {}
                for q in lanes:
                    own.wait(*ready[q])
                    marks[q] = own.did(V.tensor_reduce(st[q][:, 0, :], xs[q], X, ALU.add))
                for q in lanes:
                    own.wait(marks[q])
                    f.centred.raise_by(V.scalar_tensor_tensor(full(lane_c[q]), stat(q, 0), -1.0 / D, xs[q],
                                                              ALU.mult, ALU.add), (n, q))
                    if free is not None:
                        free(q)
                for q in lanes:
                    dve.wait_ge(*f.squared.at(i, (n, q)))
                    f.variance.raise_by(V.tensor_reduce(st[q][:, 1, :], full(lane_s[q]), X, ALU.add), (n, q))
                for q in lanes:
                    dve.wait_ge(*f.deviation.at(i, (n, q)))
                    marks[q] = own.did(V.reciprocal(st[q][:, 3, :], st[q][:, 2, :]))
                if scale is not None:
                    for q in lanes:
                        own.wait(marks[q])
                        dve.sem_inc(dve_passed)
                        marks[q] = own.did(V.tensor_tensor(st[q][:, 3, :], st[q][:, 3, :], scale(q), ALU.mult))
                done = {}
                for q in lanes:
                    own.wait(marks[q])
                    ins = V.scalar_tensor_tensor(hs[q], full(lane_c[q]), 0.0, stat(q, 3), ALU.max, ALU.mult)
                    done[q] = final(q, ins) if final else own.did(ins)
                return done


            for k, f in enumerate(hops):
                own = Own(dve, f.dve)

                def body(i, first):
                    own.step(i)
                    def msg_ready(q, ins):
                        f.rows.raise_by(ins, ("m", q))

                    if not first:
                        for b in B2K:
                            dve.wait_ge(*f.merged.at(i - 1, ("m", b)))
                    elif k == 1:
                        for b in B2K:
                            dve.wait_ge(*hops[0].merged.at(STEPS - 1, ("m", b)))
                    count = {}
                    for b in B2K:
                        for j, columns in enumerate(HALF):
                            dve.wait_ge(*f.picked.at(i, ("k", b, j)))
                            for g in columns:
                                o = g - g % 2 - columns[0]
                                keys, mine = mm[j][:, o * P:o * P + 2 * P], kslot[b][:, g:g + 1]
                                if k == 0:
                                    w = P * (1 + g % 2)
                                    count[b] = own.did(V.scalar_tensor_tensor(
                                        equal[b][:, g, 0:w], keys[:, 0:w], mine, lower[:, g % 2, 0:w], ALU.is_equal,
                                        ALU.mult, accum_out=dups[b][:, g:g + 1]))
                                    own.wait(count[b])
                                ins = V.tensor_scalar(equal[b][:, g, :], keys, mine, None, ALU.is_equal)
                                if g == columns[-1]:
                                    f.compared.raise_by(ins, ("k", b, j))
                    if k == 0:
                        for b in B2K:
                            mine = key[:, bass.ds(ecol(i, b), G)]
                            d0 = own.did(V.tensor_scalar(dups[b][:, :], dups[b][:, :], 1.0, None, ALU.min))
                            d1 = own.did(V.scalar_tensor_tensor(st[b][:, 0, :], mine, -1.0, spare[:, 0:G], ALU.mult, ALU.add))
                            own.wait(d0, d1)
                            own.wait(own.did(V.tensor_tensor(st[b][:, 0, :], st[b][:, 0, :], dups[b][:, :], ALU.mult)))
                            own.wait(own.did(V.tensor_tensor(kidx[:, bass.ds(ecol(i, b), G)], st[b][:, 0, :], mine, ALU.add)))
                        layer_norm(own, f, i, "l", B2K, [full(ga[b]) for b in B2K], [full(us[b]) for b in B2K],
                                   [[(f.got[b], 16 * G * (i + 1))] for b in B2K],
                                   scale=lambda q: wt[:, bass.ds(ecol(i, q), G)], final=msg_ready)
                    else:
                        for b in B2K:
                            dve.wait_ge(f.got[b], 16 * G * (i + 1))
                            msg_ready(b, V.tensor_tensor(full(us[b]), full(ga[b]), cols(wt, ecol(i, b)), ALU.mult))

                steps(dve, STEPS, body)


            own = Own(dve, dn.dve)

            def dense(i, first):
                own.step(i)

                def rows_ready(n):
                    return lambda q, ins: dn.rows.raise_by(ins, (n, q))

                xs, ys, hs = ([full(t) for t in lanes] for lanes in (lane_x, lane_y, lane_h))
                loaded = [[(dn_load[q], 16 * (i + 1))] for q in LANES]
                for lanes in PAIRS:
                    layer_norm(own, dn, i, "l1", lanes, xs, hs, loaded, final=rows_ready("h1"))
                for lanes in PAIRS:
                    for q in lanes:
                        dve.wait_ge(*dn.product.at(i, ("h1", q)))
                        dn.taken.raise_by(V.tensor_tensor(flat(lane_y[q]), flat(lane_x[q]), lane_p[q][:, 0:W], ALU.add), ("x2", q))
                    layer_norm(own, dn, i, "l2", lanes, ys, hs, [[dn.taken.at(i, ("x2", q))] for q in LANES],
                               final=rows_ready("h2"))
                for lanes in PAIRS:
                    for q in lanes:
                        dve.wait_ge(*dn.second.at(i, ("h2", q)))
                        dn.taken.raise_by(V.tensor_tensor(flat(lane_y[q]), flat(lane_y[q]), lane_p[q][:, 0:W], ALU.add), ("x3", q))
                    layer_norm(own, dn, i, "l3", lanes, ys, hs, [[dn.taken.at(i, ("x3", q))] for q in LANES],
                               final=rows_ready("h3"))
                for lanes in PAIRS:
                    for q in lanes:
                        dve.wait_ge(*dn.second.at(i, ("h3", q)))
                        if not first:
                            dve.wait_ge(s_dense[q], 16 * i)
                        dn.taken.raise_by(V.tensor_tensor(
                            full(lane_o[q]).rearrange("p (g s) d -> p s g d", s=2),
                            ys[q].rearrange("p (g s) d -> p s g d", s=2),
                            lane_p[q][:, :].rearrange("p (s c) -> p s c", s=2)[:, :, 0:HB * D]
                            .rearrange("p s (g d) -> p s g d", d=D), ALU.add), ("out", q))

            steps(dve, DSTEPS, dense)

            base = prep[0]
            dve.wait_ge(s_mapv, 2 * STEPS)
            link(V.tensor_scalar(flag[:, :], src_map[:, :, 1], 0.0, None, ALU.is_equal))
            link(V.tensor_copy(tmp[:, :], rowno[:, 0:1].broadcast_to([P, T])))
            link(V.tensor_scalar(tmp[:, :], tmp[:, :], 1.0 / T, float(ROWS), ALU.mult, ALU.add))
            link(V.tensor_tensor(tmp[:, :], tmp[:, :], flag[:, :], ALU.mult))
            link(V.tensor_tensor(tmp[:, :], tmp[:, :], src_map[:, :, 0], ALU.add))
            link(V.tensor_copy(ptr_i[:, :], tmp[:, :]))
            dve.sem_inc(s_ptr, 1)
            V.tensor_copy(tmp[:, :], src_map[:, :, 1]).then_inc(s_deg, 1)
            dve.wait_ge(s_deg, 1)
            dve.sem_inc(s_deg, 1)
            dve.wait_ge(s_root, 2)
            link(V.reciprocal(dis_s[:, :], dis_s[:, :]))
            link(V.reciprocal(dis_d[:, :], dis_d[:, :]))
            dve.sem_inc(s_phase, 1)

            def running(own, i, b, o, prev, first_at, msg, factor, col, ready, order, final=None):
                mark = None
                for n, g in enumerate(order):
                    if mark is None:
                        own.wait(*ready)
                    else:
                        own.wait(mark)
                    if prev is None:
                        ins = V.tensor_copy(o(g), msg(g))
                    else:
                        ins = V.scalar_tensor_tensor(o(g), prev, factor[:, bass.ds(col + g, 1)], msg(g), ALU.mult, ALU.add)
                    prev = o(g)
                    if final is not None and n == G - 1:
                        final(ins)
                    else:
                        mark = own.did(ins)

            for k, f in enumerate(sp_):
                own = Own(dve, f.dve)

                def body(i, first):
                    own.step(i)
                    ready = {}
                    if not first:
                        dve.wait_ge(*f.acc_ready.at(i - 1, ("a", 1)))
                        for b in B2K:
                            dve.wait_ge(f.kept[b], 16 * 2 * i)
                    got = {b: (f.got[b], 16 * G * (i + 1)) for b in B2K}
                    if k == 0:
                        ready = layer_norm(own, f, i, "l", B2K, [full(ga[b]) for b in B2K], [full(h[b]) for b in B2K],
                                           [[got[b]] for b in B2K], scale=lambda q: dis_s[:, bass.ds(ecol(i, q), G)])
                        for b in B2K:
                            own.wait(ready[b])
                            f.ga_free.raise_now(dve, ("g", b))
                    else:
                        for b in B2K:
                            own.wait(got[b], (f.load[b], 32 * (i + 1)))
                            ready[b] = own.did(V.tensor_tensor(full(us[b]), full(hin[b]), full(ga[b]), ALU.add))
                        for b in B2K:
                            own.wait(ready[b])
                            f.ga_free.raise_now(dve, ("g", b))
                            f.rows.raise_by(V.tensor_tensor(full(us[b]), full(us[b]), cols(dis_s, ecol(i, b)), ALU.mult), ("v", b))
                        for b in B2K:
                            dve.wait_ge(*f.product.at(i, ("v", b)))
                            f.taken.raise_by(V.tensor_tensor(flat(xw[b]), flat(xin[b]), mm[b][:, 0:W], ALU.add), ("v", b))
                        for b in B2K:
                            dve.wait_ge(*f.taken.at(i, ("v", b)))
                            f.in_free.raise_now(dve, ("x", b))
                        ready = layer_norm(own, f, i, "l", B2K, [full(xw[b]) for b in B2K], [full(h[b]) for b in B2K],
                                           [[] for b in B2K])
                    for b in B2K:
                        own.wait(ready[b])
                        f.state_ready.raise_now(dve, ("x", b))
                    for b in B2K:
                        if not first:
                            dve.wait_ge(f.stored[b], 16 * i)
                        prev = None if first and b == 0 else acc[1 - b][:, G - 1, :]
                        carry = [] if b == 0 else [f.acc_ready.at(i, ("a", 0))]
                        if b == 0 and not first:
                            carry = [f.acc_ready.at(i - 1, ("a", 1))]
                        running(own, i, b, lambda g: acc[b][:, g, :], prev, 0, lambda g: h[b][:, g, :], same, ecol(i, b),
                                [ready[b]] + carry, range(G),
                                final=lambda ins: f.acc_ready.raise_by(ins, ("a", b)))

                if k == 0:
                    for q in LANES:
                        dve.wait_ge(s_dense[q], 16 * DSTEPS)
                if k == 1:
                    for b in B2K:
                        dve.wait_ge(sp_[0].stored[b], 16 * STEPS)
                        dve.wait_ge(sp_[0].kept[b], 16 * 2 * STEPS)
                steps(dve, STEPS, body)
                dve.wait_ge(s_span, k + 1)
                V.tensor_tensor(fix[:, 0:D], tp[0][:, 0:D], hsum[:, :], ALU.add).then_inc(s_fixpart, 1)
                dve.wait_ge(s_fixpart, k + 1)
                V.tensor_copy(fix[:, D:2 * D], tp[0][:, D:2 * D]).then_inc(s_fix, 1)
                dve.wait_ge(s_fix, k + 1)
                dve.sem_inc(s_phase, 1)

            own = Own(dve, tt.dve)

            def last_pass(i, first):
                own.step(i)
                both = range(G - 1, -1, -1)

                def did(signal, key, ins):
                    signal.raise_by(ins, key)
                    return signal.at(i, key)

                loaded = {b: (tt.load[b], 16 * 6 * (i + 1)) for b in B2K}
                got_a = {b: (tt.got_a[b], 16 * G * (i + 1)) for b in B2K}
                got_x = {b: (tt.got_x[b], 16 * G * (i + 1)) for b in B2K}
                ddis = lambda b: dis_d[:, bass.ds(tcol(i, b), G)]
                for b in B2K:
                    own.wait(loaded[b], got_a[b])
                    did(tt.rows, ("us", b), V.tensor_tensor(full(us[b]), full(hin[b]), full(ga[b]), ALU.add))
                xm = {}
                for b in B2K:
                    own.wait(tt.rows.at(i, ("us", b)))
                    tt.ga_free.raise_now(dve, ("g", b))
                hd = layer_norm(own, tt, i, "d1", B2K, [full(gx[b]) for b in B2K], [full(xw[b]) for b in B2K],
                                [[got_x[b]] for b in B2K], scale=ddis)
                for b in B2K:
                    own.wait(hd[b])
                    hd[b] = own.did(V.tensor_tensor(full(xw[b]), full(xw[b]), full(a3[b]), ALU.add))
                for b in B2K:
                    own.wait(hd[b])
                    did(tt.rows, ("vd", b), V.tensor_tensor(full(xw[b]), full(xw[b]), cols(dis_d, tcol(i, b)), ALU.mult))
                xs = {}
                for b in B2K:
                    dve.wait_ge(*tt.second.at(i, ("us", b)))
                    xs[b] = did(tt.taken, ("us", b),
                                V.tensor_tensor(flat(us[b]), flat(xin[b]), tp[b][:, 0:W], ALU.add))
                for b in B2K:
                    dve.wait_ge(*tt.product.at(i, ("vd", b)))
                    xm[b] = did(tt.taken, ("vd", b), V.tensor_tensor(flat(xd[b]), flat(gx[b]), mm[b][:, 0:W], ALU.add))
                for b in B2K:
                    own.wait(xm[b])
                    tt.gx_free.raise_now(dve, ("g", b))
                hd = layer_norm(own, tt, i, "d2", B2K, [full(xd[b]) for b in B2K], [full(h[b]) for b in B2K],
                                [[xm[b]] for b in B2K])
                for b in B2K:
                    own.wait(hd[b])
                    did(tt.rows, ("ud", b), V.tensor_tensor(full(h[b]), full(h[b]), full(a4[b]), ALU.add))
                for b in B2K:
                    own.wait(tt.rows.at(i, ("ud", b)))
                    tt.in_free.raise_now(dve, ("x", b))
                h3s = layer_norm(own, tt, i, "s3", B2K, [full(us[b]) for b in B2K],
                                 [cc[b][:, :, 0:D] for b in B2K], [[xs[b]] for b in B2K])
                for b in B2K:
                    dve.wait_ge(*tt.second.at(i, ("ud", b)))
                    xm[b] = did(tt.taken, ("ud", b), V.tensor_tensor(flat(xd[b]), flat(xd[b]), tp[b][:, 0:W], ALU.add))
                for b in B2K:
                    own.wait(xm[b])
                    xm[b] = own.did(V.tensor_tensor(full(xd[b]), full(xd[b]), cols(last, tcol(i, b)), ALU.mult))
                ends = {}
                for b in B2K:
                    prev = None if first and b == 0 else x3[1 - b][:, 0, :]
                    mark = []
                    if b == 1:
                        mark = [ends[0]]
                    running(own, i, b, lambda g: x3[b][:, g, :], prev, 0, lambda g: xd[b][:, g, :], more, tcol(i, b),
                            [xm[b]] + mark, both)
                    ends[b] = (own.sem, own.i * own.per + own.k)
                layer_norm(own, tt, i, "d3", B2K, [full(x3[b]) for b in B2K], [cc[b][:, :, D:2 * D] for b in B2K],
                           [[ends[b]] for b in B2K], final=lambda q, ins: did(tt.rows, ("h3", q), ins))
                for b in B2K:
                    if not first:
                        dve.wait_ge(tt.kept[b], 16 * i)
                    prev = None if first and b == 0 else cc[1 - b][:, 0, 2 * D:3 * D]
                    mark = [tt.message.at(i, ("m1", b))] + ([tt.rows.at(i, ("agg", 0))] if b else [])
                    running(own, i, b, lambda g: cc[b][:, g, 2 * D:3 * D], prev, 0, lambda g: us[b][:, g, :], cont,
                            tcol(i, b), mark, both, final=lambda ins: tt.rows.raise_by(ins, ("agg", b)))
                if first:
                    V.tensor_copy(brd[:, 0:D], x3[0][:, G - 1, :]).then_inc(s_saved, 1)
                    V.tensor_copy(brd[:, D:2 * D], cc[0][:, G - 1, D:2 * D]).then_inc(s_saved, 1)
                for half in range(2):
                    for b in B2K:
                        dve.wait_ge(*tt.second.at(i, (f"u{half}", b)))
                        if not first and half == 0:
                            dve.wait_ge(tt.written[b], 16 * G * i)
                        did(tt.taken, (f"u{half}", b), V.tensor_tensor(
                            acc[b][:, half * HB:half * HB + HB, :], x3[b][:, half * HB:half * HB + HB, :],
                            tp[b][:, 0:HB * D].rearrange("p (g d) -> p g d", d=D), ALU.add))
                for b in B2K:
                    dve.wait_ge(*tt.taken.at(i, ("u1", b)))
                    tt.o_ready.raise_now(dve, ("o", b))

            steps(dve, STEPS, last_pass)
            dve.wait_ge(s_span, 3)
            dve.wait_ge(s_saved, 2)
            V.tensor_copy(brd[:, 2 * D:3 * D], tp[0][:, D:2 * D]).then_inc(s_border, 1)
            dve.wait_ge(s_bpe, 1)
            V.tensor_copy(bz[:, 0:P], tp[0][:, 0:P]).then_inc(s_border, 1)
            dve.wait_ge(s_bpe, 2)
            V.tensor_scalar(bz[:, P:2 * P], mm[0][:, 0:P], bcol[:, 2:3], 0.0, ALU.add, ALU.max).then_inc(s_border, 1)
            dve.wait_ge(s_border, 3)
            dve.sem_inc(s_border, 1)
            dve.wait_ge(s_bpe, 3)
            V.tensor_tensor(fix[:, 0:D], brd[:, 0:D], tp[1][:, 0:D], ALU.add).then_inc(s_border, 1)


_INS = ["x", "src", "dst", "edge_attr_32", "edge_weight", "L1_gnn_W", "L1_gnn_b", "L2_gnn_W1", "L2_gnn_b1",
        "L2_gnn_W2", "L2_gnn_b2", "L3_gnn_mW1", "L3_gnn_mb1", "L3_gnn_mW2", "L3_gnn_mb2", "L3_gnn_uW1",
        "L3_gnn_ub1", "L3_gnn_uW2", "L3_gnn_ub2"]


def kernel(**inputs):
    import numpy as np
    import concourse.bacc as bacc
    from concourse.bass_utils import run_bass_kernel_spmd

    nc = bacc.Bacc("TRN2", target_bir_lowering=False, num_devices=1)
    arrays, args = {}, []
    for name in _INS:
        a = np.asarray(inputs[name])
        a = np.ascontiguousarray(a.T if name in ("L2_gnn_W1", "L2_gnn_W2") else a)
        arrays[f"in_{name}"] = a
        args.append(nc.dram_tensor(f"in_{name}", a.shape, mybir.dt.from_np(a.dtype), kind="ExternalInput").ap())
    args.append(nc.dram_tensor("out_x", (N, D), F32, kind="ExternalOutput").ap())
    gnn(nc, *args)
    r = run_bass_kernel_spmd(nc, [arrays], core_ids=[0])
    return r.results[0]["out_x"]
```

```python
from contextlib import ExitStack

import concourse.bass as bass
from concourse import mybir

P = 128
N = 100000
E = 50000
D = 64
DE = 32
DH = 128
EC = -(-E // P)
T = EC + 1
ELAST = E - (P - 1) * EC
G = 14
U = T // G
STEPS = U // 2
NU = -(-N // (P * G))
DSTEPS = NU // 4
W = G * D
HB = G // 2
HC = 208
ROWS = P * T
PIECES = 25
SC = 1000
SG = 17
SCALE = 1.0 / (1 << 16)
BIG = float(1 << 20)
EPS = 1e-5
assert G == 14 and T % (2 * G) == 0 and NU % 4 == 0 and W % P == 0
assert EC % SG == 0 and E % SC == 0 and E < 1 << 16

F32 = mybir.dt.float32
I32 = mybir.dt.int32
BF16 = mybir.dt.bfloat16
ALU = mybir.AluOpType
ACT = mybir.ActivationFunctionType
X = mybir.AxisListType.X


class Signal:

    def __init__(self, sem, keys, early=(), n=0):
        self.sem, self.keys, self.n, self.raised = sem, list(keys), n, 0
        self.early = [k for k in keys if k in early or k[0] in early]
        self.late = [k for k in keys if k not in self.early]

    def at(self, i, key):
        if key in self.early:
            if isinstance(i, int) and i == 0:
                return self.sem, self.early.index(key) + 1
            i = i - 1
        at = self.keys.index(key) + 1
        if self.early and isinstance(i, int) and i == self.n - 1:
            at = self.late.index(key) + 1
        return self.sem, i * len(self.keys) + (len(self.early) + at)

    def check(self, key):
        order = [*self.early, *self.keys, *self.keys, *self.late] if self.early else self.keys
        assert order[self.raised % len(order)] == key, (key, order, self.raised)
        self.raised += 1

    def raise_by(self, instruction, key):
        self.check(key)
        instruction.then_inc(self.sem, 1)

    def raise_now(self, engine, key):
        self.check(key)
        engine.sem_inc(self.sem, 1)


class Settled:

    def __init__(self, engine, passed):
        self.engine, self.passed = engine, passed

    def wait_ge(self, sem, value):
        self.engine.wait_ge(sem, value)
        if not isinstance(value, int):
            self.engine.sem_inc(self.passed, 1)


class Own:

    def __init__(self, engine, sem):
        self.engine, self.sem, self.before, self.per, self.k, self.i = engine, sem, 0, 0, 0, 0

    def start(self):
        self.before, self.k = self.k, 0

    def step(self, i):
        assert not self.per or self.k == self.per
        self.per, self.i, self.k = self.k, i, 0

    def did(self, instruction):
        instruction.then_inc(self.sem, 1)
        self.k += 1
        return self.mark()

    def mark(self):
        return self.sem, self.i * self.per + (self.before + self.k)

    def wait(self, *marks):
        for sem, value in marks:
            self.engine.wait_ge(sem, value)


def steps(engine, n, body, last_apart=False):
    body(0, True)
    with engine.Fori(1, n - last_apart) as i:
        body(i, False)
    if last_apart:
        body(n - 1, False)


def gnn(nc, x, src, dst, edge_attr, edge_weight, W1g, b1g, W2a, b2a, W2b, b2b, mW1, mb1, mW2, mb2, uW1, ub1,
        uW2, ub2, out):
    ctx = ExitStack()
    with ctx:
        def sb(name, shape, dt=F32):
            return ctx.enter_context(nc.sbuf_tensor(name, shape, dt))

        def sem(name):
            return ctx.enter_context(nc.semaphore(name))

        def dram(name, shape):
            return nc.dram_tensor(name, shape, F32, kind="Internal").ap()

        tables = [dram(f"table{k}", [ROWS + P, D]) for k in range(2)]
        hop = dram("hop", [N + 2 * P, D])
        x1 = dram("x1", [N + 2 * P, D])
        suffix = dram("suffix", [ROWS, D])
        node_map = dram("node_map", [N, 2])
        xs1, xs2 = (dram(f"xs{k}", [P, T * D]) for k in (1, 2))
        dst_s, src_s = (nc.dram_tensor(n, [E, 1], I32, kind="Internal").ap() for n in ("dst_sorted", "src_sorted"))
        weight_s, attr_s = dram("weight_sorted", [E, 1]), dram("attr_sorted", [E, DE])
        ms1, hs2 = dram("ms1", [P, T * D]), dram("hs2", [P, T * D])

        def rows(t):
            return t[0:ROWS, :].rearrange("(p c) d -> p (c d)", p=P)

        zeros = sb("zeros", [P, G * DE])
        ident = sb("ident", [P, P])
        upper = sb("upper", [P, P])
        ones = sb("ones", [P, P])
        rows3 = sb("rows3", [P, P], BF16)
        eps = sb("eps", [P, 1])
        one = sb("one", [P, 1])
        wg = sb("wg", [P, P])
        w2a = sb("w2a", [P, P])
        w2b = sb("w2b", [P, P])
        m1 = sb("m1", [P, DH])
        m1e = sb("m1e", [P, 4, DH])
        m2 = sb("m2", [P, D])
        u1 = sb("u1", [P, DH])
        u1s = sb("u1s", [P, 2, DH])
        u2 = sb("u2", [P, D])
        bias = sb("bias", [P, 4, 512], BF16)
        bcol = sb("bcol", [P, 3])
        BG, B2, BM, BU = range(4)

        dst_i, src_i = (sb(n, [P, T], I32) for n in ("dst_i", "src_i"))
        dst_f = sb("dst_f", [P, T])
        wt = sb("wt", [P, T])
        same = sb("same", [P, T])
        more = sb("more", [P, T])
        last = sb("last", [P, T])
        cont = sb("cont", [P, T])
        flag = sb("flag", [P, T])
        tmp = sb("tmp", [P, T])
        cnt = sb("cnt", [P, T])
        map_idx = sb("map_idx", [P, T], I32)
        out_idx = sb("out_idx", [P, T], I32)
        dstc_i = sb("dstc_i", [P, T], I32)
        ptr_i = sb("ptr_i", [P, T], I32)
        rowno = sb("rowno", [P, T])
        map_rows = sb("map_rows", [P, T, 2])
        src_map = map_rows
        dis_s = sb("dis_s", [P, T])
        dis_d = sb("dis_d", [P, T])
        kn_i = sb("kn_i", [P, 1], I32)
        small = sb("small", [P, 24])
        head_i, tail_i, brd_i = (sb(n, [P, 1], I32) for n in ("head_i", "tail_i", "brd_i"))
        diag = sb("diag", [P, 2, P])
        kf = sb("kf", [P, 2, P])
        mh, mt1, mt2 = (sb(n, [P, P]) for n in ("mh", "mt1", "mt2"))

        def pair(name, shape, dt=F32):
            return [sb(f"{name}{b}", shape, dt) for b in range(2)]

        unit = [P, G, D]
        xin, hin, xw, h, vt, zz, ga = (pair(n, unit) for n in ("xin", "hin", "xw", "h", "vt", "zz", "ga"))
        acc = pair("acc", unit)
        us = pair("us", unit)
        wide = pair("wide", [P, 4, G, D])
        a3, a4, gx, xd = ([wide[b][:, k] for b in range(2)] for k in range(4))
        equal = [t[:, :, :, :].rearrange("p k g d -> p (k g d)").rearrange("p (g m) -> p g m", g=G) for t in wide]
        lower = sb("lower", [P, 2, 2 * P])
        kslot, krow = pair("kslot", [P, G]), pair("krow", [G, P])
        dups = pair("dups", [P, G])
        kidx = sb("kidx", [P, T], I32)
        key = sb("key", [P, T])
        spare = sb("spare", [P, T])
        x3 = pair("x3", unit)
        xc, sq = pair("xc", unit), pair("sq", unit)
        st = [sb(f"st{q}", [P, 4, G]) for q in range(4)]
        cc = pair("cc", [P, G, 3 * D])
        pick = cc[0][0:G, :, :].rearrange("p g d -> p (g d)")[:, 0:G * P].rearrange("p (g m) -> p g m", g=G)
        ef = pair("ef", [P, G, DE])
        eft = pair("eft", [P, 512])
        isl, isl2, osl = (pair(n, [P, G], I32) for n in ("isl", "isl2", "osl"))
        msl = pair("msl", [P, G, 2])
        hsum = sb("hsum", [P, D])
        fix = sb("fix", [P, 2 * D])
        brd = sb("brd", [P, 3 * D])
        bz = sb("bz", [P, 2 * P])

        room = [t[:, :, :, :].rearrange("p k g d -> p (k g d)") for t in wide]
        chunk_i, chunk_f, gap = room[0][:, 0:SC].bitcast(I32), room[0][:, SC:2 * SC], room[0][:, 2 * SC:3 * SC + EC - 1]
        found, number = room[1][:, 0:SC], room[1][:, SC:SC + T]
        unsorted_i = sb("unsorted_i", [P, 1], I32)
        rank_slot, number_slot, dst_slot, src_slot = (sb(n, [P, SG], I32) for n in
                                                      ("rank_slot", "number_slot", "dst_slot", "src_slot"))
        weight_slot = sb("weight_slot", [P, SG])
        attr_slot = vt[0][:, :, :].rearrange("p g d -> p (g d)")[:, 0:SG * DE].rearrange("p (g d) -> p g d", d=DE)

        ccu = [[t[:, :, :].rearrange("p g d -> p (g d)")[:, j * W:j * W + W].rearrange("p (g d) -> p g d", d=D)
                for j in range(3)] for t in cc]
        lane_x, lane_y, lane_h, lane_o = ([t[0], t[1], wide[0][:, j], wide[1][:, j]]
                                          for j, t in enumerate((xin, xw, h, acc)))
        lane_c, lane_s, lane_v = ([t[0], t[1], ccu[0][j], ccu[1][j]] for j, t in enumerate((xc, sq, vt)))
        lane_z = [zz[0], zz[1], us[0], us[1]]
        bias_f = cc[0][:, :, :].rearrange("p g d -> p (g d)")[:, 0:4 * 512].rearrange("p (k c) -> p k c", k=4)
        bias_part = cc[1][:, :, :].rearrange("p g d -> p (g d)")[:, 0:2 * 512].bitcast(BF16).rearrange("p (k c) -> p k c", k=4)
        nxt_f, prv_f = (xc[b][:, :, :].rearrange("p g d -> p (g d)")[:, 0:T] for b in range(2))
        nxt_i, prv_i = (sq[b][:, :, :].rearrange("p g d -> p (g d)")[:, 0:T].bitcast(I32) for b in range(2))

        tp = [ctx.enter_context(nc.psum_tensor(f"tp{b}", [P, 1024], F32)) for b in range(2)]
        mm = [ctx.enter_context(nc.psum_tensor(f"mm{b}", [P, 1024], F32)) for b in range(2)]
        lane_p = [*tp, *mm]

        def flat(t, n=W):
            return (t if isinstance(t, bass.AP) else t[:, :, :]).rearrange("p g d -> p (g d)")[:, 0:n]

        def full(t):
            return t if isinstance(t, bass.AP) else t[:, :, :]

        def cols(ap, c, n=G):
            return ap[:, bass.ds(c, n)].unsqueeze(2).broadcast_to([P, n, D])

        def stat(q, k):
            return st[q][:, k, :].unsqueeze(2).broadcast_to([P, G, D])

        s_passed = sem("waits_passed")
        s_const = sem("constants_ready")
        s_pad = sem("padding_written")
        s_edges = sem("edges_loaded")
        s_order = sem("order_known")
        s_attr = sem("edge_features_in_place")
        s_chunk = sem("key_chunk_loaded")
        s_chunk_free = sem("key_chunk_used")
        s_counted = sem("columns_counted")
        s_rank_own = sem("ranks_own")
        s_rank = sem("ranks_ready")
        s_sort_slot = sem("sort_slot_filled")
        s_attr_got = sem("sort_features_gathered")
        s_sorted = sem("sorted_rows_written")
        s_reloaded = sem("sorted_edges_loaded")
        s_weights = sem("weights_loaded")
        s_cleared = sem("map_and_zero_rows_cleared")
        s_rowno = sem("row_numbers_ready")
        s_prep = sem("dve_prep_done")
        s_asked = sem("prep_operands_ready")
        s_answer = sem("prep_products_in_psum")
        s_mapin = sem("map_rows_ready")
        s_maps = [sem(f"map_scattered{b}") for b in range(2)]
        s_slot = sem("pool_slot_copied")
        s_mapg = [sem(f"map_gathered{b}") for b in range(2)]
        s_mapv = sem("source_map_ready")
        s_ptr = sem("pointers_ready")
        s_deg = sem("degrees_ready")
        s_root = sem("degree_roots_ready")
        s_dense = [sem(f"dense_rows_stored{q}") for q in range(4)]
        s_phase = sem("dve_phase_done")
        s_head = sem("head_sums_gathered")
        s_span = sem("span_sums_in_psum")
        s_fix = sem("span_sums_ready")
        s_fixed = sem("table_complete")
        s_final = sem("final_scattered")
        s_bias = sem("bias_parts_ready")
        s_pick = sem("pick_ready")
        s_hop_init = sem("hop_cleared")
        s_x1_init = sem("x1_started")
        HALF = [range(0, 8), range(8, G)]
        s_own = sem("dve_prep_own")
        s_fixpart = sem("first_node_sums_ready")
        WEIGHTS = 12 + 4 + 4 * 3 + 4

        B2K = [0, 1]

        def per_unit(*names):
            return [(n, b) for n in names for b in B2K]

        class Phase:

            def __init__(self, name, lns, rows_,
                         turned=None, copied=None, product=None, hidden=None, second=None,
                         taken=None, message=None, slot=None, krow=None, picked=None,
                         compared=None, merged=None, sums=None, ga_free=None, gx_free=None,
                         in_free=None, state_ready=None, acc_ready=None,
                         o_ready=None, early=(), n=0):
                def signal(kind, keys):
                    return Signal(sem(f"{name}_{kind}"), keys, early, n) if keys else None

                ln = [(n, q) for n, qs in lns for q in qs]
                self.dve = sem(name + "_dve_own")
                self.centred, self.squared = signal("centred", ln), signal("squared", ln)
                self.variance, self.deviation = signal("variance", ln), signal("deviation", ln)
                self.rows = signal("rows_ready", rows_)
                self.turned = signal("turned", turned)
                self.copied = signal("copied", copied)
                self.product = signal("product", product)
                self.hidden = signal("hidden", hidden)
                self.second = signal("second", second)
                self.taken = signal("taken", taken)
                self.message = signal("message", message)
                self.slot = signal("slot", slot)
                self.krow = signal("krow", krow)
                self.picked = signal("picked", picked)
                self.compared = signal("compared", compared)
                self.merged = signal("merged", merged)
                self.sums = signal("sums", sums)
                self.ga_free = signal("ga_free", ga_free)
                self.gx_free = signal("gx_free", gx_free)
                self.in_free = signal("in_free", in_free)
                self.state_ready = signal("state_ready", state_ready)
                self.acc_ready = signal("acc_ready", acc_ready)
                self.o_ready = signal("o_ready", o_ready)

        LANES = range(4)
        PAIRS = ((0, 1), (2, 3))

        A, B = PAIRS

        def of(*parts):
            return [(n, q) for names, pair in parts for n in names.split() for q in pair]

        dn = Phase("dense", [(n, p) for n, p in (("l3", A), ("l3", B), ("l1", A), ("l1", B), ("l2", A), ("l2", B))],
                   of(("h3", A), ("h3", B), ("h1", A), ("h1", B), ("h2", A), ("h2", B)),
                   turned=of(("h2", B), ("h3", A), ("h1", A), ("h3", B), ("h1", B), ("h2", A)),
                   copied=of(("h2", B), ("h3", A), ("h1", A), ("h3", B), ("h1", B), ("h2", A)),
                   product=of(("h2", B), ("even odd", A), ("h1", A), ("even odd", B), ("h1", B), ("h2", A)),
                   hidden=of(("h2", B), ("even odd", A), ("even odd", B), ("h2", A)),
                   second=of(("h2", B), ("h3", A), ("h3", B), ("h2", A)),
                   taken=of(("x3", A), ("x3", B), ("out", A), ("x2", A), ("out", B), ("x2", B)),
                   early=("l1", "l2", "h1", "x2", ("h2", 0), ("h2", 1)), n=DSTEPS)
        dn.rows = Signal(dn.rows.sem, dn.rows.keys, ("h1", "h2"), DSTEPS)
        dn_load = [sem(f"dense_loaded{q}") for q in LANES]

        hops = []
        for k in range(2):
            f = Phase(f"hop{k}", [("l", B2K)] if k == 0 else [], per_unit("m"),
                      slot=per_unit("k"), turned=per_unit("k"), krow=per_unit("k"),
                      picked=[("k", b, j) for b in B2K for j in B2K], compared=[("k", b, j) for b in B2K for j in B2K],
                      merged=per_unit("m"), sums=per_unit("m"))
            f.got = [sem(f"hop{k}_gathered{b}") for b in B2K]
            f.added = sem(f"hop{k}_added")
            hops.append(f)

        sp_ = []
        for k in range(2):
            v = per_unit("v") if k == 1 else None
            f = Phase(f"s{k}", [("l", B2K)], v, turned=v, copied=v, product=v, taken=v,
                      ga_free=per_unit("g"), in_free=per_unit("x") if k == 1 else None,
                      state_ready=per_unit("x"), acc_ready=per_unit("a"))
            f.got = [sem(f"s{k}_gathered{b}") for b in B2K]
            f.load = [sem(f"s{k}_loaded{b}") for b in B2K] if k == 1 else None
            f.stored = [sem(f"s{k}_sums_stored{b}") for b in B2K]
            f.kept = [sem(f"s{k}_state_stored{b}") for b in B2K]
            sp_.append(f)

        T_EARLY = ("ef", "us", "vd", "ud", "d1", "d2", "s3", "d3", "h3", "x", "g")
        T_TURNED = per_unit("m0", "m1", "vd", "ef", "us", "ud", "u0", "u1")
        T_MLP = per_unit("m0", "m1", "us", "ud", "u0", "u1")
        tt = Phase("t", [("d1", B2K), ("d2", B2K), ("s3", B2K), ("d3", B2K)],
                   per_unit("vd", "agg", "us", "ud", "h3"),
                   turned=T_TURNED, copied=T_TURNED,
                   product=per_unit("m0", "m1", "vd", "us", "ud", "u0", "u1"),
                   hidden=T_MLP, second=T_MLP, message=per_unit("m0", "m1"),
                   taken=per_unit("vd", "us", "ud", "u0", "u1"), acc_ready=per_unit("a"),
                   in_free=per_unit("x"), gx_free=per_unit("g"), ga_free=per_unit("g"), o_ready=per_unit("o"),
                   early=T_EARLY, n=STEPS)
        tt.load = [sem(f"t_loaded{b}") for b in range(2)]
        tt.got_a = [sem(f"t_sums_gathered{b}") for b in range(2)]
        tt.got_x = [sem(f"t_nodes_gathered{b}") for b in range(2)]
        tt.kept = [sem(f"t_suffix_stored{b}") for b in range(2)]
        tt.written = [sem(f"t_rows_written{b}") for b in range(2)]
        s_border = sem("border_dve_steps")
        s_bpe = sem("border_products")

        block = ctx.enter_context(nc.Block())

        def drow(i, b):
            if isinstance(i, int):
                return min((4 * i + b) * P * G, N - P * G)
            return (4 * i + b) * (P * G)

        def ecol(i, b):
            return (2 * i + b) * G

        def tcol(i, b):
            return (U - 1 - b) * G - 2 * G * i

        @block.sync
        def _(sp):
            after = Settled(sp, s_passed)
            n = (P - 1) * EC

            def load_edges(dst, src, edge_weight, loaded):
                for t, s in ((dst_i, dst), (src_i, src), (wt, edge_weight)):
                    sp.dma_start(t[0:P - 1, 0:EC], s[0:n].rearrange("(p c) -> p c", c=EC)).then_inc(loaded, 16)
                    sp.dma_start(t[P - 1:P, 0:ELAST], s[n:E].rearrange("(p c) -> p c", p=1)).then_inc(loaded, 16)
                sp.dma_start(nxt_i[0:P - 1, 0:EC], dst[1:n + 1].rearrange("(p c) -> p c", c=EC)).then_inc(loaded, 16)
                sp.dma_start(nxt_i[P - 1:P, 0:ELAST - 1], dst[n + 1:E].rearrange("(p c) -> p c", p=1)).then_inc(loaded, 16)
                sp.dma_start(prv_i[0:1, 1:EC], dst[0:EC - 1].rearrange("(p c) -> p c", p=1)).then_inc(loaded, 16)
                sp.dma_start(prv_i[1:P - 1, 0:EC], dst[EC - 1:n - 1].rearrange("(p c) -> p c", c=EC)).then_inc(loaded, 16)
                sp.dma_start(prv_i[P - 1:P, 0:ELAST], dst[n - 1:E - 1].rearrange("(p c) -> p c", p=1)).then_inc(loaded, 16)
                with nc.allow_non_contiguous_dma(reason="126 single keys"):
                    sp.dma_start(kn_i[0:P - 2, :], dst[EC:n].rearrange("(p c) -> p c", c=EC)[:, EC - 1:EC]).then_inc(loaded, 16)

            after.wait_ge(s_pad, 8)
            load_edges(dst, src, edge_weight, s_edges)
            after.wait_ge(s_const, 1)
            lo, hi = slice(0, D), slice(D, P)
            for o, s in ((wg[lo, 0:D], W1g), (wg[hi, D:P], W1g), (w2a[lo, 0:D], W2a), (w2a[hi, D:P], W2a),
                         (w2b[lo, 0:D], W2b), (w2b[hi, D:P], W2b), (m1[:, :], mW1[0:P, :]), (m2[:, :], mW2),
                         (u1[:, :], uW1), (u1s[lo, 0, :], uW1[0:D, :]), (u1s[hi, 1, :], uW1[0:D, :]),
                         (u2[:, :], uW2)):
                sp.dma_start(o, s).then_inc(s_weights, 16)
            for j in range(4):
                sp.dma_start(m1e[DE * j:DE * j + DE, j, :], mW1[P:P + DE, :]).then_inc(s_weights, 16)
            for j, v in enumerate((b1g, b2b, mb2, ub2)):
                for p in range(3):
                    sp.dma_start(bias_f[p:p + 1, j, :].rearrange("p (r d) -> p r d", d=D),
                                 v.rearrange("(p r d) -> p r d", p=1, r=1).broadcast_to([1, 512 // D, D])).then_inc(s_weights, 16)
            with nc.allow_non_contiguous_dma(reason="bias columns"):
                for o, v in ((bcol[lo, 0:1], b2a), (bcol[hi, 0:1], b2a), (bcol[:, 1:2], mb1), (bcol[:, 2:3], ub1)):
                    sp.dma_start(o, v.rearrange("(d p) -> d p", p=1)).then_inc(s_weights, 16)

            cleared = hop.rearrange("a b -> (a b)").rearrange("(p k w) -> p k w", p=P, k=HC)
            w = (N + 2 * P) * D // P // HC
            sp.dma_start(cleared, zeros[:, 0:w].unsqueeze(1).broadcast_to([P, HC, w])).then_inc(s_hop_init, 16)
            cleared = node_map.rearrange("(p a) b -> p (a b)", p=125)
            for j in range(4):
                w = 2 * N // 125 // 4
                sp.dma_start(cleared[:, j * w:j * w + w], zeros[0:125, 0:w]).then_inc(s_cleared, 16)
            sp.dma_start(x1[N:N + 2 * P, :].rearrange("(p a) d -> p (a d)", p=P), zeros[:, 0:2 * D]).then_inc(s_x1_init, 16)
            for t in tables:
                sp.dma_start(t[ROWS:ROWS + P, :], zeros[:, 0:D]).then_inc(s_cleared, 16)
            after.wait_ge(s_order, 1)
            unsorted = sp.value_load(unsorted_i[0:1, 0:1])
            with sp.If(unsorted > 0):
                with sp.Fori(0, E // SC) as j:
                    after.wait_ge(s_chunk_free, j + 1)
                    sp.dma_start(chunk_i, dst.rearrange("(a n) -> a n", a=1)[:, bass.ds(j * SC, SC)]
                                 .broadcast_to([P, SC])).then_inc(s_chunk, 16)
                after.wait_ge(s_sorted, 4 * 16 * EC)
                sp.sem_inc(s_attr, 16)
                load_edges(*(t.rearrange("a b -> (a b)") for t in (dst_s, src_s, weight_s)), s_reloaded)

            for j in range(PIECES):
                after.wait_ge(hops[0].added, 16 * G * (j + 1))
                at = slice(j * N // PIECES, (j + 1) * N // PIECES)
                sp.dma_start(x1[at, :], x[at, :]).then_inc(s_x1_init, 16)

            after.wait_ge(hops[1].added, 16 * G)
            with sp.If(unsorted < 1):
                sp.dma_start(attr_s, edge_attr).then_inc(s_attr, 16)

            def node_rows(t, i, q):
                return t[bass.ds(drow(i, q), P * G), :].rearrange("(p g) d -> p g d", g=G)

            def dense_load(i, q):
                sp.dma_start(full(lane_x[q]), node_rows(x1, i, q)).then_inc(dn_load[q], 16)

            def dense(i, more_steps=True):
                for q in LANES:
                    if more_steps:
                        after.wait_ge(*dn.taken.at(i, ("x2", q)))
                        dense_load(i + 1, q)
                for q in LANES:
                    after.wait_ge(*dn.taken.at(i, ("out", q)))
                    if not more_steps and q == 3:
                        after.wait_ge(s_dense[2], 16 * DSTEPS)
                    sp.dma_start(node_rows(out, i, q), full(lane_o[q])).then_inc(s_dense[q], 16)

            after.wait_ge(hops[1].added, 16 * G * U)
            for q in LANES:
                dense_load(0, q)
            dense(0)
            with sp.Fori(1, DSTEPS - 2) as i:
                dense(i)
            dense(DSTEPS - 2)
            dense(DSTEPS - 1, False)

            for k, f in enumerate(sp_):
                def load(i, b):
                    for t, s in ((xin, xs1), (hin, ms1)):
                        sp.dma_start(flat(t[b]), s[:, bass.ds(ecol(i, b) * D, W)]).then_inc(f.load[b], 16)

                def body(i, more_steps=True):
                    for b in B2K:
                        if more_steps and k == 1:
                            after.wait_ge(*f.in_free.at(i, ("x", b)))
                            load(i + 1, b)
                    for b in B2K:
                        at = bass.ds(ecol(i, b) * D, W)
                        after.wait_ge(*f.state_ready.at(i, ("x", b)))
                        state, rest = ((ga, xs1), (h, ms1)) if k == 0 else ((xw, xs2), (h, hs2))
                        for t, s in (state, rest):
                            sp.dma_start(s[:, at], flat(t[b])).then_inc(f.kept[b], 16)
                        after.wait_ge(*f.acc_ready.at(i, ("a", b)))
                        sp.dma_start(rows(tables[k])[:, at], flat(acc[b])).then_inc(f.stored[b], 16)

                if k == 1:
                    for b in B2K:
                        after.wait_ge(sp_[0].kept[b], 16 * STEPS * 2)
                        load(0, b)
                body(0)
                with sp.Fori(1, STEPS - 1) as i:
                    body(i)
                body(STEPS - 1, False)

            def t_load(i, b):
                at = bass.ds(tcol(i, b) * D, W)
                for t, s in ((xin, xs2), (hin, hs2), (a3, rows(tables[0])), (a4, rows(tables[1]))):
                    sp.dma_start(flat(t[b]), s[:, at]).then_inc(tt.load[b], 16)
                n = (P - 1) * EC
                c = tcol(i, b)
                first = isinstance(i, int) and i == 0 and b == 0
                w = G - 1 if first else G
                sp.dma_start(ef[b][0:P - 1, 0:w, :],
                             attr_s[0:n, :].rearrange("(p c) d -> p (c d)", c=EC)[:, bass.ds(c * DE, w * DE)]
                             .rearrange("p (c d) -> p c d", d=DE)).then_inc(tt.load[b], 16)
                tail(i, b, c)

            def tail(i, b, c):
                n = (P - 1) * EC
                left = ELAST - c if isinstance(c, int) else G
                w = max(0, min(G, left))
                if w:
                    sp.dma_start(ef[b][P - 1:P, 0:w, :],
                                 attr_s[n:E, :].rearrange("(p c) d -> p (c d)", p=1)[:, bass.ds(c * DE, w * DE)]
                                 .rearrange("p (c d) -> p c d", d=DE)).then_inc(tt.load[b], 16)
                else:
                    sp.dma_start(ef[b][P - 1:P, :, :],
                                 zeros[P - 1:P, 0:G * DE].rearrange("p (c d) -> p c d", d=DE)).then_inc(tt.load[b], 16)

            def t_body(i, more_steps=True):
                for b in B2K:
                    after.wait_ge(*tt.rows.at(i, ("agg", b)))
                    sp.dma_start(rows(suffix)[:, bass.ds(tcol(i, b) * D, W)].rearrange("p (g d) -> p g d", d=D),
                                 cc[b][:, :, 2 * D:3 * D]).then_inc(tt.kept[b], 16)
                for b in B2K:
                    if more_steps:
                        after.wait_ge(*tt.in_free.at(i + 1, ("x", b)))
                        t_load(i + 2, b)

            after.wait_ge(s_phase, 3)
            after.wait_ge(s_fixed, 2 * 32)
            after.wait_ge(s_attr, 16)
            for b in B2K:
                after.wait_ge(sp_[1].kept[b], 16 * STEPS * 2)
            for b in B2K:
                t_load(0, b)
            for b in B2K:
                after.wait_ge(*tt.in_free.at(0, ("x", b)))
                t_load(1, b)
            t_body(0)
            with sp.Fori(1, STEPS - 2) as i:
                t_body(i)
            t_body(STEPS - 2, False)
            t_body(STEPS - 1, False)
            for q in LANES:
                after.wait_ge(s_dense[q], 16 * DSTEPS)
            for b in B2K:
                after.wait_ge(tt.kept[b], 16 * STEPS)
                after.wait_ge(tt.written[b], 16 * G * STEPS)
            after.wait_ge(s_final, 16)

        @block.gpsimd
        def _(pool):
            after = Settled(pool, s_passed)
            nc.gpsimd.memset(zeros[:, :], 0.0).then_inc(s_pad, 1)
            for t, v in ((dst_i, N), (nxt_i, N), (prv_i, -1), (src_i, 0), (kn_i, N)):
                nc.gpsimd.memset(t[:, :], v).then_inc(s_pad, 1)
            nc.gpsimd.memset(wt[:, :], 0.0).then_inc(s_pad, 1)
            nc.gpsimd.memset(ef[0][:, :, :], 0.0).then_inc(s_pad, 1)
            nc.gpsimd.memset(ones[:, :], 1.0).then_inc(s_rowno, 1)
            nc.gpsimd.iota(rowno[:, :], pattern=[[1, T]], base=0, channel_multiplier=T,
                           allow_small_or_imprecise_dtypes=True).then_inc(s_rowno, 1)
            after.wait_ge(s_rowno, 1)
            nc.gpsimd.affine_select(out=ident[:, :], in_=ones[:, :], pattern=[[-1, P]], base=0, channel_multiplier=1,
                                    compare_op=ALU.is_equal, fill=0.0).then_inc(s_rowno, 1)
            nc.gpsimd.affine_select(out=upper[:, :], in_=ones[:, :], pattern=[[1, P]], base=0, channel_multiplier=-1,
                                    compare_op=ALU.is_gt, fill=0.0).then_inc(s_rowno, 1)
            nc.gpsimd.affine_select(out=rows3[:, :], in_=ones[:, :], pattern=[[0, P]], base=3, channel_multiplier=-1,
                                    compare_op=ALU.is_gt, fill=0.0).then_inc(s_rowno, 1)
            for j in range(2):
                nc.gpsimd.affine_select(out=lower[:, j, 0:P], in_=ones[:, :], pattern=[[-1, P]], base=j * P,
                                        channel_multiplier=1, compare_op=ALU.is_gt, fill=0.0).then_inc(s_rowno, 1)
                nc.gpsimd.affine_select(out=lower[:, j, P:2 * P], in_=ones[:, :], pattern=[[-1, P]], base=(j - 1) * P,
                                        channel_multiplier=1, compare_op=ALU.is_gt, fill=0.0).then_inc(s_rowno, 1)
            nc.gpsimd.iota(spare[:, :], pattern=[[0, T // 2], [P, 2]], base=N, channel_multiplier=1,
                           allow_small_or_imprecise_dtypes=True).then_inc(s_rowno, 1)
            nodes_max = pool.to_reg(N - 1)
            rows_max = pool.to_reg(ROWS + P - 1)

            after.wait_ge(s_order, 1)
            with pool.If(pool.value_load(unsorted_i[0:1, 0:1]) > 0):
                nc.gpsimd.iota(gap, pattern=[[-1, SC + EC - 1]], base=EC - 1, channel_multiplier=EC,
                               allow_small_or_imprecise_dtypes=True).then_inc(s_sort_slot, 1)
                nc.gpsimd.iota(number, pattern=[[1, T]], base=0, channel_multiplier=EC,
                               allow_small_or_imprecise_dtypes=True).then_inc(s_sort_slot, 1)
                nc.gpsimd.memset(attr_slot, 0.0).then_inc(s_sort_slot, 1)
                after.wait_ge(s_sort_slot, 3)
                after.wait_ge(s_rank, 1)
                edges_max = pool.to_reg(E - 1)
                with pool.Fori(0, EC // SG) as i:
                    for o, t in ((rank_slot, kidx), (number_slot, map_idx), (dst_slot, dst_i), (src_slot, src_i),
                                 (weight_slot, wt)):
                        nc.gpsimd.tensor_copy(o[:, :], t[:, bass.ds(i * SG, SG)]).then_inc(s_sort_slot, 1)
                    after.wait_ge(s_sort_slot, 3 + 5 * i + 5)
                    for g in range(SG):
                        nc.gpsimd.indirect_dma_start(
                            attr_slot[:, g, :], None, edge_attr, bass.IndirectOffsetOnAxis(number_slot[:, g:g + 1], 0),
                            bounds_check=edges_max, oob_is_err=False).then_inc(s_attr_got, 16)
                    after.wait_ge(s_attr_got, 16 * SG * i + 16 * SG)
                    for o, t in ((dst_s, dst_slot), (src_s, src_slot), (weight_s, weight_slot), (attr_s, attr_slot)):
                        for g in range(SG):
                            nc.gpsimd.indirect_dma_start(
                                o, bass.IndirectOffsetOnAxis(rank_slot[:, g:g + 1], 0),
                                t[:, g, :] if t is attr_slot else t[:, g:g + 1], None,
                                bounds_check=edges_max, oob_is_err=False).then_inc(s_sorted, 16)
                    after.wait_ge(s_sorted, 4 * 16 * SG * i + 4 * 16 * SG)

            def slot_copy(o, i_):
                return nc.gpsimd.tensor_copy(o, i_).then_inc(s_slot, 1)

            def gather(o, table, idx, limit, s, columns=range(G)):
                for g in columns:
                    nc.gpsimd.indirect_dma_start(
                        o[:, g, :], None, table, bass.IndirectOffsetOnAxis(idx[:, g:g + 1], 0),
                        bounds_check=limit, oob_is_err=False).then_inc(s, 16)

            after.wait_ge(s_bias, 1)
            nc.gpsimd.memset(pick[:, :, :], 1.0).then_inc(s_pick, 1)
            after.wait_ge(s_pick, 1)
            nc.gpsimd.affine_select(out=pick[:, :, :], in_=pick[:, :, :], pattern=[[-1, G], [0, P]], base=0,
                                    channel_multiplier=1, compare_op=ALU.is_equal, fill=0.0).then_inc(s_pick, 1)
            after.wait_ge(s_prep, 1)
            base = 0
            spare_max = pool.to_reg(N + 2 * P - 1)
            for k, f in enumerate(hops):
                table, sums = (x, hop) if k == 0 else (hop, x1)
                for b in B2K:
                    slot_copy(isl[b][:, :], dstc_i[:, b * G:b * G + G])
                    after.wait_ge(s_slot, base + b + 1)
                    gather(ga[b], table, isl[b], nodes_max, f.got[b])
                base += 2
                after.wait_ge(*((s_hop_init, 16) if k == 0 else (s_x1_init, (PIECES + 1) * 16)))

                def body(i, more_steps=True):
                    for b in B2K:
                        after.wait_ge(*f.sums.at(i, ("m", b)))
                        slot_copy(osl[b][:, :], kidx[:, bass.ds(ecol(i, b), G)])
                        if more_steps:
                            slot_copy(isl[b][:, :], dstc_i[:, bass.ds(ecol(i + 1, b), G)])
                        after.wait_ge(s_slot, base + 4 * i + 2 * b + 2 if more_steps else base + 4 * i + b + 1)
                        for q in range(HB):
                            if not (isinstance(i, int) and i == 0 and b == 0 and q == 0):
                                after.wait_ge(f.added, 32 * ((2 * i + b) * HB + q))
                            for g in (2 * q, 2 * q + 1):
                                nc.gpsimd.indirect_dma_start(
                                    sums, bass.IndirectOffsetOnAxis(osl[b][:, g:g + 1], 0), acc[b][:, g, :], None,
                                    bounds_check=spare_max, oob_is_err=True, compute_op=ALU.add).then_inc(f.added, 16)
                            if more_steps:
                                gather(ga[b], table, isl[b], nodes_max, f.got[b], (2 * q, 2 * q + 1))

                body(0)
                with pool.Fori(1, STEPS - 1) as i:
                    body(i)
                body(STEPS - 1, False)
                base += 4 * STEPS - 2
                after.wait_ge(f.added, 16 * G * U)

            after.wait_ge(s_mapin, 1)
            after.wait_ge(s_cleared, 6 * 16)

            def map_scatter(i, first):
                for b in B2K:
                    if not first:
                        after.wait_ge(s_maps[b], 16 * G * i)
                    slot_copy(isl[b][:, :], map_idx[:, bass.ds(ecol(i, b), G)])
                    slot_copy(msl[b][:, :, :], map_rows[:, bass.ds(ecol(i, b), G), :])
                    after.wait_ge(s_slot, base + 4 * i + 2 * b + 2)
                    for g in range(G):
                        nc.gpsimd.indirect_dma_start(
                            node_map, bass.IndirectOffsetOnAxis(isl[b][:, g:g + 1], 0), msl[b][:, g, :], None,
                            bounds_check=nodes_max, oob_is_err=False).then_inc(s_maps[b], 16)

            steps(pool, STEPS, map_scatter)
            base += 4 * STEPS
            for b in B2K:
                after.wait_ge(s_maps[b], 16 * G * STEPS)

            def map_gather(i, first):
                for b in B2K:
                    if not first:
                        after.wait_ge(s_mapg[b], 16 * G * i)
                        nc.gpsimd.tensor_copy(src_map[:, bass.ds(ecol(i - 1, b), G), :], msl[b][:, :, :]).then_inc(s_mapv, 1)
                        after.wait_ge(s_mapv, 2 * (i - 1) + b + 1)
                    slot_copy(isl[b][:, :], src_i[:, bass.ds(ecol(i, b), G)])
                    after.wait_ge(s_slot, base + 2 * i + b + 1)
                    for g in range(G):
                        nc.gpsimd.indirect_dma_start(
                            msl[b][:, g, :], None, node_map, bass.IndirectOffsetOnAxis(isl[b][:, g:g + 1], 0),
                            bounds_check=nodes_max, oob_is_err=False).then_inc(s_mapg[b], 16)

            steps(pool, STEPS, map_gather)
            base += 2 * STEPS
            for b in B2K:
                after.wait_ge(s_mapg[b], 16 * G * STEPS)
                nc.gpsimd.tensor_copy(src_map[:, ecol(STEPS - 1, b):ecol(STEPS - 1, b) + G, :], msl[b][:, :, :]).then_inc(s_mapv, 1)

            for k, f in enumerate(sp_):
                if k == 0:
                    table, index, limit = x1, src_i, nodes_max
                else:
                    table, index, limit = tables[k - 1], ptr_i, rows_max
                    after.wait_ge(s_ptr, 1)
                    for b in B2K:
                        after.wait_ge(sp_[0].kept[b], 2 * 16 * STEPS)

                def body(i, first):
                    for b in B2K:
                        if not first:
                            after.wait_ge(*f.ga_free.at(i - 1, ("g", b)))
                            if k == 0:
                                after.wait_ge(f.kept[b], 2 * 16 * i)
                        slot_copy(isl[b][:, :], index[:, bass.ds(ecol(i, b), G)])
                        after.wait_ge(s_slot, base + 2 * i + b + 1)
                        gather(ga[b], table, isl[b], limit, f.got[b])

                steps(pool, STEPS, body)
                base += 2 * STEPS
                for b in B2K:
                    after.wait_ge(f.stored[b], 16 * STEPS)
                if k == 0:
                    after.wait_ge(s_prep, 1)
                nc.gpsimd.indirect_dma_start(hsum[:, :], None, tables[k], bass.IndirectOffsetOnAxis(head_i[:, :], 0),
                                             bounds_check=rows_max, oob_is_err=False).then_inc(s_head, 16)
                after.wait_ge(s_fix, k + 1)
                nc.gpsimd.indirect_dma_start(tables[k], bass.IndirectOffsetOnAxis(head_i[:, :], 0), fix[:, 0:D], None,
                                             bounds_check=rows_max, oob_is_err=False).then_inc(s_fixed, 16)
                pool.dma_start(rows(tables[k])[:, EC * D:T * D], fix[:, D:2 * D]).then_inc(s_fixed, 16)
                after.wait_ge(s_fixed, 32 * (k + 1))

            def t_gather(i, slots, first=False):
                for b in B2K:
                    if not first:
                        after.wait_ge(*tt.gx_free.at(i - 1, ("g", b)))
                    slot_copy(isl2[b][:, :], dstc_i[:, bass.ds(tcol(i, b), G)])
                    after.wait_ge(s_slot, base + slots + b + 1)
                    gather(gx[b], x1, isl2[b], nodes_max, tt.got_x[b])
                for b in B2K:
                    if not first:
                        after.wait_ge(*tt.ga_free.at(i - 1, ("g", b)))
                    slot_copy(isl[b][:, :], ptr_i[:, bass.ds(tcol(i, b), G)])
                    after.wait_ge(s_slot, base + slots + 2 + b + 1)
                    gather(ga[b], tables[1], isl[b], rows_max, tt.got_a[b])

            def t_scatter(i, slots, first=False):
                for b in B2K:
                    after.wait_ge(*tt.o_ready.at(i, ("o", b)))
                    if not first:
                        after.wait_ge(tt.written[b], 16 * G * i)
                    slot_copy(osl[b][:, :], out_idx[:, bass.ds(tcol(i, b), G)])
                    after.wait_ge(s_slot, base + slots + b + 1)
                    for g in range(G):
                        nc.gpsimd.indirect_dma_start(
                            out, bass.IndirectOffsetOnAxis(osl[b][:, g:g + 1], 0), acc[b][:, g, :], None,
                            bounds_check=nodes_max, oob_is_err=False).then_inc(tt.written[b], 16)

            for q in LANES:
                after.wait_ge(s_dense[q], 16 * DSTEPS)
            t_gather(0, 0, True)
            t_gather(1, 4)
            t_gather(2, 8)
            t_scatter(0, 12, True)
            t_gather(3, 14)
            with pool.Fori(2, STEPS - 2) as i:
                t_scatter(i - 1, 6 * i + 6)
                t_gather(i + 2, 6 * i + 8)
            for i in (STEPS - 3, STEPS - 2, STEPS - 1):
                t_scatter(i, 4 * STEPS + 2 * i)
            for b in B2K:
                after.wait_ge(tt.kept[b], 16 * STEPS)
            nc.gpsimd.indirect_dma_start(hsum[:, :], None, suffix, bass.IndirectOffsetOnAxis(tail_i[:, :], 0),
                                         bounds_check=rows_max, oob_is_err=False).then_inc(s_head, 16)
            after.wait_ge(s_border, 5)
            nc.gpsimd.indirect_dma_start(out, bass.IndirectOffsetOnAxis(brd_i[:, :], 0), fix[:, 0:D], None,
                                         bounds_check=nodes_max, oob_is_err=False).then_inc(s_final, 16)


        @block.tensor
        def _(pe):
            def turn(o, blocks, signal, key):
                for j, blk in enumerate(blocks):
                    w = blk.shape[1]
                    t = nc.tensor.transpose(o[0:w, j * P:j * P + P], blk, ident[:, :])
                signal.raise_by(t, key)

            def product(o, weights, src_, b, extra=None, signal=None, key=None):
                for c in range(0, W, 512):
                    n = min(512, W - c)
                    t = nc.tensor.matmul(o[:, c:c + n], weights, flat(src_)[:, c:c + n], start=True, stop=extra is None)
                    if extra is not None:
                        for j in range(c // P, (c + n) // P):
                            g = extra + j
                            t = nc.tensor.matmul(o[:, j * P:j * P + P], m1e[:, g % 4, :],
                                                 eft[b][:, (g // 4) * P:(g // 4) * P + P],
                                                 start=False, stop=j == (c + n) // P - 1)
                signal.raise_by(t, key)

            def by_row(o, sources, weights, k, signal, key):
                w = weights.shape[1]
                for n_src, src_ in enumerate(sources):
                    for c in range(0, HB * w, 512):
                        n = min(512, HB * w - c)
                        at = 512 * n_src + c
                        nc.tensor.matmul(o[:, at:at + n], rows3[:, :], bias[:, k, 0:n], start=True, stop=False)
                        for j in range(c // w, (c + n) // w):
                            t = nc.tensor.matmul(o[:, at - c + j * w:at - c + j * w + w], src_[:, j * P:j * P + P], weights,
                                                 start=False, stop=j == (c + n) // w - 1)
                signal.raise_by(t, key)

            pe.wait_ge(s_asked, 1)
            pe.wait_ge(s_rowno, 1)
            nc.tensor.matmul(mm[0][:, 0:1], ones[:, :], small[:, 11:12], start=True, stop=True).then_inc(s_answer, 1)
            pe.wait_ge(s_asked, 3)
            nc.tensor.matmul(tp[0][:, 0:P], ones[:, :], diag[:, 0, :], start=True, stop=True)
            nc.tensor.matmul(tp[0][:, P:2 * P], ones[:, :], diag[:, 1, :], start=True, stop=True).then_inc(s_answer, 1)
            pe.wait_ge(s_asked, 4)
            nc.tensor.matmul(tp[1][:, 0:1], mh[:, :], small[:, 5:6], start=True, stop=True)
            nc.tensor.matmul(tp[1][:, 1:2], mt1[:, :], small[:, 5:6], start=True, stop=False)
            nc.tensor.matmul(tp[1][:, 1:2], mt2[:, :], small[:, 4:5], start=False, stop=True).then_inc(s_answer, 1)
            pe.wait_ge(s_weights, WEIGHTS * 16)
            pe.wait_ge(s_prep, 1)
            pe.wait_ge(s_pick, 2)

            def span(k, tails, heads):
                nc.tensor.matmul(tp[0][:, 0:D], mh[:, :], tails, start=True, stop=True)
                nc.tensor.matmul(tp[0][:, D:2 * D], mt1[:, :], tails, start=True, stop=False)
                nc.tensor.matmul(tp[0][:, D:2 * D], mt2[:, :], heads, start=False, stop=True).then_inc(s_span, 1)

            for k, f in enumerate(hops):
                def body(i, first):
                    for b in B2K:
                        pe.wait_ge(*f.slot.at(i, ("k", b)))
                        f.turned.raise_by(nc.tensor.transpose(tp[b][0:G, W:W + P], kslot[b][:, :], ident[:, :]), ("k", b))
                    for b in B2K:
                        pe.wait_ge(*f.krow.at(i, ("k", b)))
                        for j, columns in enumerate(HALF):
                            if b == 1:
                                pe.wait_ge(*f.compared.at(i, ("k", 0, j)))
                            elif not first:
                                pe.wait_ge(*f.compared.at(i - 1, ("k", 1, j)))
                            for g in columns:
                                t = nc.tensor.matmul(mm[j][:, (g - columns[0]) * P:(g - columns[0] + 1) * P], pick[:, g, :],
                                                     krow[b][:, :], start=True, stop=True)
                            f.picked.raise_by(t, ("k", b, j))
                    for b in B2K:
                        pe.wait_ge(*f.compared.at(i, ("k", b, 1)))
                        pe.wait_ge(*f.rows.at(i, ("m", b)))
                        if not first:
                            pe.wait_ge(*f.sums.at(i - 1, ("m", b)))
                        for g in range(G):
                            for n in range(2):
                                o = g - g % 2 + n
                                t = nc.tensor.matmul(tp[b][:, g * D:g * D + D], equal[b][:, o, (g % 2) * P:(g % 2) * P + P],
                                                     us[b][:, o, :], start=n == 0, stop=n == 1)
                        f.merged.raise_by(t, ("m", b))

                steps(pe, STEPS, body)

            def dense_job(i, lanes, n):
                for q in lanes:
                    pe.wait_ge(*dn.rows.at(i, (n, q)))
                    if n == "h1" and not (isinstance(i, int) and i == 0):
                        pe.wait_ge(*dn.taken.at(i - 1, ("out", q)))
                    turn(lane_p[q], [flat(lane_h[q])[:, j * P:j * P + P] for j in range(HB)], dn.turned, (n, q))
                if n == "h1":
                    for q in lanes:
                        pe.wait_ge(*dn.copied.at(i, (n, q)))
                        by_row(lane_p[q], [flat(lane_v[q])], wg[:, :], BG, dn.product, (n, q))
                if n == "h2":
                    for q in lanes:
                        pe.wait_ge(*dn.copied.at(i, (n, q)))
                        product(lane_p[q], w2a[:, :], lane_v[q], q, None, dn.product, (n, q))
                    for q in lanes:
                        pe.wait_ge(*dn.hidden.at(i, (n, q)))
                        by_row(lane_p[q], [flat(lane_z[q])], w2b[:, :], B2, dn.second, (n, q))
                if n == "h3":
                    for q in lanes:
                        pe.wait_ge(*dn.copied.at(i, (n, q)))
                        product(lane_p[q], u1s[:, 0, :], lane_v[q], q, None, dn.product, ("even", q))
                    for q in lanes:
                        pe.wait_ge(*dn.hidden.at(i, ("even", q)))
                        product(lane_p[q], u1s[:, 1, :], lane_v[q], q, None, dn.product, ("odd", q))
                    for q in lanes:
                        pe.wait_ge(*dn.hidden.at(i, ("odd", q)))
                        by_row(lane_p[q], [flat(lane_z[q]), flat(lane_v[q])], u2[:, :], BU, dn.second, (n, q))

            def dense(i, more_steps=True):
                if i is None:
                    dense_job(0, A, "h1")
                    dense_job(0, B, "h1")
                    dense_job(0, A, "h2")
                    return
                dense_job(i, B, "h2")
                dense_job(i, A, "h3")
                if more_steps:
                    dense_job(i + 1, A, "h1")
                dense_job(i, B, "h3")
                if more_steps:
                    dense_job(i + 1, B, "h1")
                    dense_job(i + 1, A, "h2")

            dense(None)
            dense(0)
            with pe.Fori(1, DSTEPS - 1) as i:
                dense(i)
            dense(DSTEPS - 1, more_steps=False)

            for k, f in enumerate(sp_):
                def body(i, first):
                    for b in B2K:
                        pe.wait_ge(*f.rows.at(i, ("v", b)))
                        turn(tp[b], [flat(us[b])[:, j * P:j * P + P] for j in range(HB)], f.turned, ("v", b))
                    for b in B2K:
                        if not first:
                            pe.wait_ge(*f.taken.at(i - 1, ("v", b)))
                        pe.wait_ge(*f.copied.at(i, ("v", b)))
                        by_row(mm[b], [flat(vt[b])], wg[:, :], BG, f.product, ("v", b))

                if k == 1:
                    steps(pe, STEPS, body)
                pe.wait_ge(*f.acc_ready.at(STEPS - 1, ("a", 1)))
                pe.wait_ge(s_head, 16 * (k + 1))
                span(k, acc[1][:, EC - 1 - T + G, :], hsum[:, :])

            def turn_job(i, n, blocks_of, *waits):
                for b in B2K:
                    for w in waits:
                        pe.wait_ge(*w(b))
                    turn(tp[b], blocks_of(b), tt.turned, (n, b))

            def blocks7(t):
                return lambda b: [flat(t[b])[:, j * P:j * P + P] for j in range(HB)]

            def mlp_halves(i, part, c0, weights1, weights2, k, free):
                for half in range(2):
                    n = f"{part}{half}"
                    turn_job(i, n, lambda b: [cc[b][:, half * HB + j, c0:c0 + P] for j in range(HB)],
                             lambda b: tt.rows.at(i, ("h3" if part == "m" else "agg", b)), free[half])
                    for b in B2K:
                        pe.wait_ge(*tt.copied.at(i, (n, b)))
                        product(mm[b], weights1[:, :], vt[b], b, half * HB if part == "m" else None, tt.product, (n, b))
                    for b in B2K:
                        pe.wait_ge(*tt.hidden.at(i, (n, b)))
                        by_row(tp[b], [flat(zz[b])], weights2[:, :], k, tt.second, (n, b))

            def last_pass(i, first=False, more_steps=True):
                if i is not None:
                    mlp_halves(i, "m", 0, m1, m2, BM,
                               [(lambda b: tt.taken.at(i, ("ud", b))) if first else (lambda b: tt.taken.at(i - 1, ("u1", b))),
                                lambda b: tt.message.at(i, ("m0", b))])
                if more_steps:
                    j = 0 if i is None else i + 1
                    turn_job(j, "vd", blocks7(xw), lambda b: tt.rows.at(j, ("vd", b)),
                             *([] if i is None else [lambda b: tt.message.at(i, ("m1", b))]))
                    for b in B2K:
                        pe.wait_ge(*tt.copied.at(j, ("vd", b)))
                        by_row(mm[b], [flat(vt[b])], wg[:, :], BG, tt.product, ("vd", b))
                    for b in B2K:
                        pe.wait_ge(*tt.rows.at(j, ("us", b)))
                        e = ef[b][:, :, :].rearrange("p g d -> p (g d)")
                        turn(tp[b], [e[:, c:min(c + P, G * DE)] for c in range(0, G * DE, P)], tt.turned, ("ef", b))
                    turn_job(j, "us", blocks7(us), lambda b: tt.copied.at(j, ("ef", b)))
                    for b in B2K:
                        pe.wait_ge(*tt.copied.at(j, ("us", b)))
                        pe.wait_ge(*tt.taken.at(j, ("vd", b)))
                        product(mm[b], w2a[:, :], vt[b], b, None, tt.product, ("us", b))
                    for b in B2K:
                        pe.wait_ge(*tt.hidden.at(j, ("us", b)))
                        by_row(tp[b], [flat(zz[b])], w2b[:, :], B2, tt.second, ("us", b))
                    turn_job(j, "ud", blocks7(h), lambda b: tt.rows.at(j, ("ud", b)), lambda b: tt.taken.at(j, ("us", b)))
                    for b in B2K:
                        pe.wait_ge(*tt.copied.at(j, ("ud", b)))
                        product(mm[b], w2a[:, :], vt[b], b, None, tt.product, ("ud", b))
                    for b in B2K:
                        pe.wait_ge(*tt.hidden.at(j, ("ud", b)))
                        by_row(tp[b], [flat(zz[b])], w2b[:, :], B2, tt.second, ("ud", b))
                if i is not None:
                    mlp_halves(i, "u", D, u1, u2, BU,
                               [(lambda b: tt.taken.at(i + 1, ("ud", b))) if more_steps
                                else (lambda b: tt.message.at(i, ("m1", b))),
                                lambda b: tt.taken.at(i, ("u0", b))])

            last_pass(None)
            last_pass(0, first=True)
            with pe.Fori(1, STEPS - 1) as i:
                last_pass(i)
            last_pass(STEPS - 1, more_steps=False)
            pe.wait_ge(s_head, 16 * 3)
            pe.wait_ge(*tt.taken.at(STEPS - 1, ("u1", 0)))
            span(2, hsum[:, :], cc[1][:, 0, 2 * D:3 * D])
            pe.wait_ge(s_border, 1)
            nc.tensor.transpose(tp[0][:, 0:P], brd[:, D:3 * D], ident[:, :]).then_inc(s_bpe, 1)
            pe.wait_ge(s_border, 2)
            nc.tensor.matmul(mm[0][:, 0:P], u1[:, :], bz[:, 0:P], start=True, stop=True).then_inc(s_bpe, 1)
            pe.wait_ge(s_border, 4)
            nc.tensor.matmul(tp[1][:, 0:D], rows3[:, :], bias[:, BU, 0:D], start=True, stop=False)
            nc.tensor.matmul(tp[1][:, 0:D], bz[:, P:2 * P], u2[:, :], start=False, stop=True).then_inc(s_bpe, 1)

        @block.scalar
        def _(act):
            def ln_squares(f, i, lanes, n):
                for q in lanes:
                    act.wait_ge(*f.centred.at(i, (n, q)))
                    f.squared.raise_by(nc.scalar.activation(full(lane_s[q]), full(lane_c[q]), ACT.Square), (n, q))

            def ln_stds(f, i, lanes, n):
                for q in lanes:
                    act.wait_ge(*f.variance.at(i, (n, q)))
                    f.deviation.raise_by(nc.scalar.activation(st[q][:, 2, :], st[q][:, 1, :], ACT.Sqrt, bias=eps[:, 0:1],
                                                        scale=1.0 / D), (n, q))

            def copy(f, i, n, after=None):
                for b in B2K:
                    act.wait_ge(*f.turned.at(i, (n, b)))
                    f.copied.raise_by(nc.scalar.copy(flat(vt[b]), tp[b][:, 0:W]), (n, b))

            def relu(f, i, n, k):
                for b in B2K:
                    act.wait_ge(*f.product.at(i, (n, b)))
                    f.hidden.raise_by(nc.scalar.activation(flat(zz[b]), mm[b][:, 0:W], ACT.Relu, bias=bcol[:, k:k + 1]),
                                      (n, b))

            act.wait_ge(s_weights, WEIGHTS * 16)
            act.wait_ge(s_const, 1)

            def copies(i, lanes, n):
                for q in lanes:
                    act.wait_ge(*dn.turned.at(i, (n, q)))
                    dn.copied.raise_by(nc.scalar.copy(flat(lane_v[q]), lane_p[q][:, 0:W]), (n, q))

            def relus(i, lanes, n, k, o):
                for q in lanes:
                    act.wait_ge(*dn.product.at(i, (n, q)))
                    dn.hidden.raise_by(nc.scalar.activation(flat(o[q]), lane_p[q][:, 0:W], ACT.Relu,
                                                            bias=bcol[:, k:k + 1]), (n, q))

            def dense(i, more_steps=True):
                if i is None:
                    for lanes in PAIRS:
                        ln_squares(dn, 0, lanes, "l1")
                        ln_stds(dn, 0, lanes, "l1")
                    for lanes in PAIRS:
                        copies(0, lanes, "h1")
                    ln_squares(dn, 0, A, "l2")
                    ln_stds(dn, 0, A, "l2")
                    copies(0, A, "h2")
                    ln_squares(dn, 0, B, "l2")
                    relus(0, A, "h2", 0, lane_z)
                    ln_stds(dn, 0, B, "l2")
                    return
                copies(i, B, "h2")
                ln_squares(dn, i, A, "l3")
                relus(i, B, "h2", 0, lane_z)
                ln_stds(dn, i, A, "l3")
                copies(i, A, "h3")
                ln_squares(dn, i, B, "l3")
                relus(i, A, "even", 2, lane_z)
                ln_stds(dn, i, B, "l3")
                relus(i, A, "odd", 2, lane_v)
                if more_steps:
                    ln_squares(dn, i + 1, A, "l1")
                    ln_stds(dn, i + 1, A, "l1")
                    copies(i + 1, A, "h1")
                copies(i, B, "h3")
                if more_steps:
                    ln_squares(dn, i + 1, B, "l1")
                relus(i, B, "even", 2, lane_z)
                if more_steps:
                    ln_stds(dn, i + 1, B, "l1")
                relus(i, B, "odd", 2, lane_v)
                if more_steps:
                    ln_squares(dn, i + 1, A, "l2")
                    ln_stds(dn, i + 1, A, "l2")
                    copies(i + 1, B, "h1")
                    copies(i + 1, A, "h2")
                    ln_squares(dn, i + 1, B, "l2")
                    relus(i + 1, A, "h2", 0, lane_z)
                    ln_stds(dn, i + 1, B, "l2")

            for k, f in enumerate(hops):
                def body(i, first):
                    for b in B2K:
                        if not first:
                            act.wait_ge(*f.turned.at(i - 1, ("k", b)))
                        if first and k == 1:
                            act.wait_ge(*hops[0].turned.at(STEPS - 1, ("k", b)))
                        f.slot.raise_by(nc.scalar.copy(kslot[b][:, :], key[:, bass.ds(ecol(i, b), G)]), ("k", b))
                    for b in B2K:
                        act.wait_ge(*f.turned.at(i, ("k", b)))
                        if not first:
                            act.wait_ge(*f.picked.at(i - 1, ("k", b, 1)))
                        if first and k == 1:
                            act.wait_ge(*hops[0].picked.at(STEPS - 1, ("k", b, 1)))
                        f.krow.raise_by(nc.scalar.copy(krow[b][:, :], tp[b][0:G, W:W + P]), ("k", b))
                    for b in B2K:
                        if k == 0:
                            ln_squares(f, i, [b], "l")
                            ln_stds(f, i, [b], "l")
                        act.wait_ge(*f.merged.at(i, ("m", b)))
                        if not first:
                            act.wait_ge(f.added, 16 * G * (2 * i - 1 + b))
                        if first and k == 1:
                            act.wait_ge(hops[0].added, 16 * G * U)
                        f.sums.raise_by(nc.scalar.copy(flat(acc[b]), tp[b][:, 0:W]), ("m", b))

                act.wait_ge(s_prep, 1)
                steps(act, STEPS, body)

            dense(None)
            dense(0)
            with act.Fori(1, DSTEPS - 1) as i:
                dense(i)
            dense(DSTEPS - 1, more_steps=False)

            act.wait_ge(s_deg, 2)
            nc.scalar.activation(dis_s[:, :], tmp[:, :], ACT.Sqrt, bias=one[:, 0:1]).then_inc(s_root, 1)
            nc.scalar.activation(dis_d[:, :], cnt[:, :], ACT.Sqrt, bias=one[:, 0:1]).then_inc(s_root, 1)

            for k, f in enumerate(sp_):
                def body(i, first):
                    if k == 1:
                        copy(f, i, "v")
                    for lanes in (([0], [1]) if k == 0 else (B2K,)):
                        ln_squares(f, i, lanes, "l")
                        ln_stds(f, i, lanes, "l")

                steps(act, STEPS, body)

            def last_pass(i, first=False, more_steps=True):
                j = 0 if i is None else i + 1
                if i is not None:
                    for half in range(2):
                        n = f"m{half}"
                        copy(tt, i, n)
                        if more_steps and half == 0:
                            ln_squares(tt, j, B2K, "d1")
                        relu(tt, i, n, 1)
                        if more_steps and half == 0:
                            ln_stds(tt, j, B2K, "d1")
                        for b in B2K:
                            act.wait_ge(*tt.second.at(i, (n, b)))
                            o = us[b][:, half * HB:half * HB + HB, :].rearrange("p g d -> p (g d)")
                            tt.message.raise_by(nc.scalar.copy(o, tp[b][:, 0:HB * D]), (n, b))
                elif more_steps:
                    ln_squares(tt, j, B2K, "d1")
                    ln_stds(tt, j, B2K, "d1")
                if more_steps:
                    copy(tt, j, "vd")
                    for b in B2K:
                        act.wait_ge(*tt.turned.at(j, ("ef", b)))
                        nc.scalar.copy(eft[b][:, 0:3 * P], tp[b][:, 0:3 * P])
                        tt.copied.raise_by(nc.scalar.copy(eft[b][0:D, 3 * P:4 * P], tp[b][0:D, 3 * P:4 * P]), ("ef", b))
                    copy(tt, j, "us")
                    ln_squares(tt, j, B2K, "d2")
                    relu(tt, j, "us", 0)
                    ln_stds(tt, j, B2K, "d2")
                    copy(tt, j, "ud")
                    ln_squares(tt, j, B2K, "s3")
                    relu(tt, j, "ud", 0)
                    ln_stds(tt, j, B2K, "s3")
                if i is not None:
                    for b in B2K:
                        if not first:
                            act.wait_ge(tt.written[b], 16 * G * i)
                        tt.acc_ready.raise_by(nc.scalar.copy(flat(acc[b]), flat(x3[b])), ("a", b))
                    copy(tt, i, "u0")
                    relu(tt, i, "u0", 2)
                    copy(tt, i, "u1")
                if more_steps:
                    ln_squares(tt, j, B2K, "d3")
                if i is not None:
                    relu(tt, i, "u1", 2)
                if more_steps:
                    ln_stds(tt, j, B2K, "d3")

            last_pass(None)
            last_pass(0, first=True)
            with act.Fori(1, STEPS - 1) as i:
                last_pass(i)
            last_pass(STEPS - 1, more_steps=False)

        @block.vector
        def _(dve):
            V = nc.vector

            prep = [0]

            def link(ins):
                prep[0] += 1
                ins.then_inc(s_own, 1)
                dve.wait_ge(s_own, prep[0])

            for t in (wg, w2a, w2b, bias_f, u1s, m1e, *eft):
                link(V.memset(t if isinstance(t, bass.AP) else t[:, :] if len(t.shape) == 2 else t[:, :, :], 0.0))
            link(V.memset(eps[:, :], EPS))
            V.memset(one[:, :], 1.0).then_inc(s_const, 1)
            dve.wait_ge(s_const, 1)
            dve.wait_ge(s_edges, 12 * 16)
            dve.wait_ge(s_rowno, 10)
            link(V.tensor_copy(dst_f[:, :], dst_i[:, :]))
            link(V.tensor_copy(prv_f[:, :], prv_i[:, :]))
            link(V.tensor_tensor(flag[:, :], prv_f[:, :], dst_f[:, :], ALU.is_gt))
            V.tensor_reduce(small[:, 11:12], flag[:, :], X, ALU.add).then_inc(s_asked, 1)
            dve.wait_ge(s_answer, 1)
            link(V.tensor_copy(unsorted_i[:, :], mm[0][:, 0:1]))
            dve.sem_inc(s_order, 1)
            with dve.If(dve.value_load(unsorted_i[0:1, 0:1]) > 0):
                ranked = [0]

                def rank_link(ins):
                    ranked[0] += 1
                    ins.then_inc(s_rank_own, 1)
                    dve.wait_ge(s_rank_own, ranked[0])

                dve.wait_ge(s_sort_slot, 3)
                rank_link(V.tensor_scalar(gap, gap, SCALE, None, ALU.mult))
                rank_link(V.tensor_copy(map_idx[:, :], number))
                rank_link(V.memset(cnt[:, :], 0.0))
                after = Settled(dve, s_passed)
                dve.sem_inc(s_chunk_free, 1)
                with dve.Fori(0, E // SC) as j:
                    after.wait_ge(s_chunk, 16 * j + 16)
                    V.tensor_copy(chunk_f, chunk_i).then_inc(s_chunk_free, 1)
                    after.wait_ge(s_chunk_free, j + 2)
                    with dve.Fori(0, EC // SG) as i:
                        for g in range(SG):
                            V.scalar_tensor_tensor(found, chunk_f, dst_f[:, bass.ds(i * SG + g, 1)],
                                                   gap[:, bass.ds(EC - 1 - g - i * SG, SC)], ALU.subtract, ALU.is_lt,
                                                   accum_out=tmp[:, bass.ds(i * SG + g, 1)]).then_inc(s_counted, 1)
                            after.wait_ge(s_counted, (EC + 1) * j + SG * i + g + 1)
                    V.tensor_tensor(cnt[:, 0:EC], cnt[:, 0:EC], tmp[:, 0:EC], ALU.add).then_inc(s_rank_own, 1)
                    V.tensor_scalar(gap, gap, -SC * SCALE, None, ALU.add).then_inc(s_counted, 1)
                    after.wait_ge(s_rank_own, ranked[0] + 1 + j)
                    after.wait_ge(s_counted, (EC + 1) * j + EC + 1)
                ranked[0] += E // SC
                rank_link(V.tensor_copy(kidx[:, :], cnt[:, :]))
                dve.sem_inc(s_rank, 1)
                dve.wait_ge(s_reloaded, 12 * 16)

            K, F, KN, TLEN, HLEN, TCNT, CARRY, BCNT, FNK, S0, S1 = (small[:, j:j + 1] for j in range(11))
            link(V.tensor_copy(dst_f[:, :], dst_i[:, :]))
            link(V.tensor_copy(nxt_f[:, :], nxt_i[:, :]))
            link(V.tensor_copy(prv_f[:, :], prv_i[:, :]))
            link(V.tensor_copy(K, dst_f[:, EC - 1:EC]))
            link(V.tensor_copy(F, dst_f[:, 0:1]))
            link(V.tensor_copy(KN, kn_i[:, :]))
            link(V.tensor_copy(dst_f[:, EC:T], K))
            link(V.tensor_tensor(flag[:, :], prv_f[:, :], dst_f[:, :], ALU.is_equal))
            link(V.tensor_copy(same[:, :], flag[:, :]))
            link(V.memset(same[:, 0:1], 0.0))
            link(V.tensor_tensor(more[:, :], nxt_f[:, :], dst_f[:, :], ALU.is_equal))
            link(V.memset(more[:, EC:T], 0.0))
            link(V.tensor_scalar(last[:, :], more[:, :], -1.0, 1.0, ALU.mult, ALU.add))
            link(V.tensor_copy(cont[:, :], more[:, :]))
            link(V.memset(cont[:, EC - 1:EC], 0.0))
            link(V.scalar_tensor_tensor(tmp[:, :], more[:, :], BIG, dst_f[:, :], ALU.mult, ALU.add))
            link(V.memset(tmp[:, EC:T], BIG))
            link(V.tensor_copy(map_idx[:, :], tmp[:, :]))
            link(V.tensor_scalar(tmp[:, :], dst_f[:, :], K, None, ALU.is_equal))
            link(V.tensor_reduce(TLEN, tmp[:, 0:EC], X, ALU.add))
            link(V.tensor_tensor(tmp[:, :], tmp[:, :], flag[:, :], ALU.max))
            link(V.scalar_tensor_tensor(tmp[:, :], tmp[:, :], BIG, dst_f[:, :], ALU.mult, ALU.add))
            link(V.tensor_copy(out_idx[:, :], tmp[:, :]))
            link(V.tensor_scalar(tmp[:, :], dst_f[:, :], float(N - 1), None, ALU.min))
            link(V.tensor_copy(dstc_i[:, :], tmp[:, :]))
            link(V.tensor_scalar(flag[:, :], dst_f[:, :], F, None, ALU.is_equal))
            link(V.memset(flag[:, EC:T], 0.0))
            link(V.tensor_reduce(HLEN, flag[:, 0:EC], X, ALU.add))
            link(V.scalar_tensor_tensor(S0, HLEN, -1.0, rowno[:, 0:1], ALU.add, ALU.add))
            link(V.tensor_copy(head_i[:, :], S0))
            link(V.scalar_tensor_tensor(S0, TLEN, -1.0, rowno[:, EC:T], ALU.mult, ALU.add))
            link(V.tensor_copy(tail_i[:, :], S0))
            link(V.tensor_tensor(S0, K, KN, ALU.is_equal))
            link(V.scalar_tensor_tensor(S1, S0, BIG, K, ALU.mult, ALU.add))
            link(V.tensor_copy(brd_i[:, :], S1))
            link(V.memset(tmp[:, :], 1.0))
            link(V.tensor_tensor_scan(cnt[:, :], same[:, :], tmp[:, :], 0.0, ALU.mult, ALU.add))
            link(V.tensor_copy(TCNT, cnt[:, EC - 1:EC]))
            link(V.tensor_copy(key[:, :], src_i[:, :]))
            link(V.scalar_tensor_tensor(tmp[:, :], dst_f[:, :], float(N), spare[:, :], ALU.is_equal, ALU.mult))
            link(V.tensor_copy(tmp[:, EC:T], spare[:, EC:T]))
            link(V.tensor_tensor(key[:, :], key[:, :], tmp[:, :], ALU.add))
            for j, border in ((0, K), (1, F)):
                V.tensor_scalar(diag[:, j, :], ident[:, :], border, None, ALU.mult).then_inc(s_asked, 1)
            dve.wait_ge(s_answer, 2)
            link(V.tensor_copy(kf[:, :, :].rearrange("p a b -> p (a b)"), tp[0][:, 0:2 * P]))
            link(V.tensor_tensor(FNK, F, K, ALU.not_equal))
            link(V.scalar_tensor_tensor(mh[:, :], kf[:, 1, :], K, upper[:, :], ALU.is_equal, ALU.mult))
            link(V.tensor_scalar(mt1[:, :], kf[:, 0, :], K, None, ALU.is_equal))
            link(V.tensor_scalar(mt2[:, :], kf[:, 0, :], F, FNK, ALU.is_equal, ALU.mult))
            dve.sem_inc(s_asked, 1)
            dve.wait_ge(s_weights, WEIGHTS * 16)
            for p in range(3):
                link(V.tensor_copy(bias_part, bias_f))
                if p == 0:
                    link(V.tensor_scalar(bias[:, :, :], bias_part, ident[:, 0:1], None, ALU.mult))
                else:
                    link(V.scalar_tensor_tensor(bias[:, :, :], bias_part, ident[:, p:p + 1], bias[:, :, :], ALU.mult, ALU.add))
                if p < 2:
                    link(V.tensor_tensor(bias_f, bias_f, bias_part, ALU.subtract))
            dve.sem_inc(s_bias, 1)
            dve.wait_ge(s_answer, 3)
            link(V.tensor_copy(small[:, 6:8], tp[1][:, 0:2]))
            link(V.scalar_tensor_tensor(cnt[:, :], flag[:, :], CARRY, cnt[:, :], ALU.mult, ALU.add))
            link(V.tensor_copy(cnt[:, EC:T], BCNT))
            link(V.tensor_copy(map_rows[:, :, 0], rowno[:, :]))
            V.tensor_copy(map_rows[:, :, 1], cnt[:, :]).then_inc(s_mapin, 1)
            dve.sem_inc(s_prep, 1)

            def layer_norm(own, f, i, n, lanes, xs, hs, ready, scale=None, free=None, final=None, before=None):
                marks = {}
                for q in lanes:
                    own.wait(*ready[q])
                    marks[q] = own.did(V.tensor_reduce(st[q][:, 0, :], xs[q], X, ALU.add))
                for q in lanes:
                    own.wait(marks[q])
                    f.centred.raise_by(V.scalar_tensor_tensor(full(lane_c[q]), stat(q, 0), -1.0 / D, xs[q],
                                                              ALU.mult, ALU.add), (n, q))
                    if free is not None:
                        free(q)
                for q in lanes:
                    dve.wait_ge(*f.squared.at(i, (n, q)))
                    f.variance.raise_by(V.tensor_reduce(st[q][:, 1, :], full(lane_s[q]), X, ALU.add), (n, q))
                for q in lanes:
                    dve.wait_ge(*f.deviation.at(i, (n, q)))
                    marks[q] = own.did(V.reciprocal(st[q][:, 3, :], st[q][:, 2, :]))
                if scale is not None:
                    for q in lanes:
                        own.wait(marks[q])
                        dve.sem_inc(s_passed, 1)
                        marks[q] = own.did(V.tensor_tensor(st[q][:, 3, :], st[q][:, 3, :], scale(q), ALU.mult))
                done = {}
                for q in lanes:
                    own.wait(marks[q])
                    if before is not None:
                        before(q)
                    ins = V.scalar_tensor_tensor(hs[q], full(lane_c[q]), 0.0, stat(q, 3), ALU.max, ALU.mult)
                    done[q] = final(q, ins) if final else own.did(ins)
                return done


            for k, f in enumerate(hops):
                own = Own(dve, f.dve)

                def body(i, first):
                    own.step(i)
                    def msg_ready(q, ins):
                        f.rows.raise_by(ins, ("m", q))

                    for b in B2K:
                        if not first:
                            dve.wait_ge(*f.merged.at(i - 1, ("m", b)))
                        elif k == 1:
                            dve.wait_ge(*hops[0].merged.at(STEPS - 1, ("m", b)))
                        for j, columns in enumerate(HALF):
                            dve.wait_ge(*f.picked.at(i, ("k", b, j)))
                            for g in columns:
                                o = g - g % 2 - columns[0]
                                keys, mine = mm[j][:, o * P:o * P + 2 * P], kslot[b][:, g:g + 1]
                                if k == 0:
                                    w = P * (1 + g % 2)
                                    own.wait(own.did(V.scalar_tensor_tensor(
                                        equal[b][:, g, 0:w], keys[:, 0:w], mine, lower[:, g % 2, 0:w], ALU.is_equal,
                                        ALU.mult, accum_out=dups[b][:, g:g + 1])))
                                ins = V.tensor_scalar(equal[b][:, g, :], keys, mine, None, ALU.is_equal)
                                if g == columns[-1]:
                                    f.compared.raise_by(ins, ("k", b, j))
                        if k == 0:
                            mine = key[:, bass.ds(ecol(i, b), G)]
                            d0 = own.did(V.tensor_scalar(dups[b][:, :], dups[b][:, :], 1.0, None, ALU.min))
                            d1 = own.did(V.scalar_tensor_tensor(st[b][:, 0, :], mine, -1.0, spare[:, 0:G], ALU.mult, ALU.add))
                            own.wait(d0, d1)
                            own.wait(own.did(V.tensor_tensor(st[b][:, 0, :], st[b][:, 0, :], dups[b][:, :], ALU.mult)))
                            own.wait(own.did(V.tensor_tensor(kidx[:, bass.ds(ecol(i, b), G)], st[b][:, 0, :], mine, ALU.add)))
                            layer_norm(own, f, i, "l", [b], {b: full(ga[b])}, {b: full(us[b])},
                                       {b: [(f.got[b], 16 * G * (i + 1))]},
                                       scale=lambda q: wt[:, bass.ds(ecol(i, q), G)], final=msg_ready)
                        else:
                            dve.wait_ge(f.got[b], 16 * G * (i + 1))
                            msg_ready(b, V.tensor_tensor(full(us[b]), full(ga[b]), cols(wt, ecol(i, b)), ALU.mult))

                steps(dve, STEPS, body)


            own = Own(dve, dn.dve)

            def dense(i, first=False, more_steps=True):
                if i is not None:
                    own.step(i)

                def rows_ready(n):
                    return lambda q, ins: dn.rows.raise_by(ins, (n, q))

                xs, ys, hs = ([full(t) for t in lanes] for lanes in (lane_x, lane_y, lane_h))

                def norm1(j, lanes):
                    layer_norm(own, dn, j, "l1", lanes, xs, hs, [[(dn_load[q], 16 * (j + 1))] for q in LANES],
                               final=rows_ready("h1"))

                def norm2(j, lanes):
                    for q in lanes:
                        dve.wait_ge(*dn.product.at(j, ("h1", q)))
                        dn.taken.raise_by(V.tensor_tensor(flat(lane_y[q]), flat(lane_x[q]), lane_p[q][:, 0:W], ALU.add), ("x2", q))
                    layer_norm(own, dn, j, "l2", lanes, ys, hs, [[dn.taken.at(j, ("x2", q))] for q in LANES],
                               final=rows_ready("h2"))

                def norm3(i, lanes):
                    for q in lanes:
                        dve.wait_ge(*dn.second.at(i, ("h2", q)))
                        dn.taken.raise_by(V.tensor_tensor(flat(lane_y[q]), flat(lane_y[q]), lane_p[q][:, 0:W], ALU.add), ("x3", q))
                    layer_norm(own, dn, i, "l3", lanes, ys, hs, [[dn.taken.at(i, ("x3", q))] for q in LANES],
                               final=rows_ready("h3"))

                def result(lanes):
                    for q in lanes:
                        dve.wait_ge(*dn.second.at(i, ("h3", q)))
                        if not first:
                            dve.wait_ge(s_dense[q], 16 * i)
                        dn.taken.raise_by(V.tensor_tensor(
                            full(lane_o[q]).rearrange("p (g s) d -> p s g d", s=2),
                            ys[q].rearrange("p (g s) d -> p s g d", s=2),
                            lane_p[q][:, :].rearrange("p (s c) -> p s c", s=2)[:, :, 0:HB * D]
                            .rearrange("p s (g d) -> p s g d", d=D), ALU.add), ("out", q))

                if i is None:
                    for norm in (norm1, norm2):
                        for lanes in PAIRS:
                            norm(0, lanes)
                    own.start()
                    return
                norm3(i, A)
                norm3(i, B)
                if more_steps:
                    norm1(i + 1, A)
                result(A)
                if more_steps:
                    norm1(i + 1, B)
                    norm2(i + 1, A)
                result(B)
                if more_steps:
                    norm2(i + 1, B)

            dense(None)
            dense(0, first=True)
            with dve.Fori(1, DSTEPS - 1) as i:
                dense(i)
            dense(DSTEPS - 1, more_steps=False)

            base = prep[0]
            dve.wait_ge(s_mapv, 2 * STEPS)
            link(V.tensor_scalar(flag[:, :], src_map[:, :, 1], 0.0, None, ALU.is_equal))
            link(V.tensor_copy(tmp[:, :], rowno[:, 0:1].broadcast_to([P, T])))
            link(V.tensor_scalar(tmp[:, :], tmp[:, :], 1.0 / T, float(ROWS), ALU.mult, ALU.add))
            link(V.tensor_tensor(tmp[:, :], tmp[:, :], flag[:, :], ALU.mult))
            link(V.tensor_tensor(tmp[:, :], tmp[:, :], src_map[:, :, 0], ALU.add))
            link(V.tensor_copy(ptr_i[:, :], tmp[:, :]))
            dve.sem_inc(s_ptr, 1)
            V.tensor_copy(tmp[:, :], src_map[:, :, 1]).then_inc(s_deg, 1)
            dve.wait_ge(s_deg, 1)
            dve.sem_inc(s_deg, 1)
            dve.wait_ge(s_root, 2)
            link(V.reciprocal(dis_s[:, :], dis_s[:, :]))
            link(V.reciprocal(dis_d[:, :], dis_d[:, :]))
            dve.sem_inc(s_phase, 1)

            def running(own, i, b, o, prev, first_at, msg, factor, col, ready, order, final=None):
                mark = None
                for n, g in enumerate(order):
                    if mark is None:
                        own.wait(*ready)
                        dve.sem_inc(s_passed, 1)
                    else:
                        own.wait(mark)
                    if prev is None:
                        ins = V.tensor_copy(o(g), msg(g))
                    else:
                        ins = V.scalar_tensor_tensor(o(g), prev, factor[:, bass.ds(col + g, 1)], msg(g), ALU.mult, ALU.add)
                    prev = o(g)
                    if final is not None and n == G - 1:
                        final(ins)
                    else:
                        mark = own.did(ins)

            for k, f in enumerate(sp_):
                own = Own(dve, f.dve)

                def sums(i, b, ready, first):
                    carry = []
                    if b == 1:
                        carry = [f.acc_ready.at(i, ("a", 0))]
                    elif not first:
                        carry = [f.acc_ready.at(i - 1, ("a", 1))]
                    if not first:
                        dve.wait_ge(f.stored[b], 16 * i)
                    prev = None if first and b == 0 else acc[1 - b][:, G - 1, :]
                    running(own, i, b, lambda g: acc[b][:, g, :], prev, 0, lambda g: h[b][:, g, :], same, ecol(i, b),
                            [ready] + carry, range(G), final=lambda ins: f.acc_ready.raise_by(ins, ("a", b)))

                def sources1(i, first):
                    own.step(i)
                    for b in B2K:
                        if not first:
                            dve.wait_ge(*f.acc_ready.at(i - 1, ("a", 1)))
                            dve.wait_ge(f.kept[b], 16 * 2 * i)
                        ready = layer_norm(own, f, i, "l", [b], {b: full(ga[b])}, {b: full(h[b])},
                                           {b: [(f.got[b], 16 * G * (i + 1))]},
                                           scale=lambda q: dis_s[:, bass.ds(ecol(i, q), G)])
                        own.wait(ready[b])
                        f.ga_free.raise_now(dve, ("g", b))
                        f.state_ready.raise_now(dve, ("x", b))
                        sums(i, b, ready[b], first)

                def source_sums(i):
                    ready = {}
                    for b in B2K:
                        own.wait((f.got[b], 16 * G * (i + 1)), (f.load[b], 32 * (i + 1)))
                        ready[b] = own.did(V.tensor_tensor(full(us[b]), full(hin[b]), full(ga[b]), ALU.add))
                    for b in B2K:
                        own.wait(ready[b])
                        f.ga_free.raise_now(dve, ("g", b))
                        dve.sem_inc(s_passed, 1)
                        f.rows.raise_by(V.tensor_tensor(full(us[b]), full(us[b]), cols(dis_s, ecol(i, b)), ALU.mult), ("v", b))

                def sources2(i, first=False, more_steps=True):
                    own.step(i)
                    if not first:
                        dve.wait_ge(*f.acc_ready.at(i - 1, ("a", 1)))
                        for b in B2K:
                            dve.wait_ge(f.kept[b], 16 * 2 * i)
                    for b in B2K:
                        dve.wait_ge(*f.product.at(i, ("v", b)))
                        f.taken.raise_by(V.tensor_tensor(flat(xw[b]), flat(xin[b]), mm[b][:, 0:W], ALU.add), ("v", b))
                    for b in B2K:
                        dve.wait_ge(*f.taken.at(i, ("v", b)))
                        f.in_free.raise_now(dve, ("x", b))
                    ready = layer_norm(own, f, i, "l", B2K, [full(xw[b]) for b in B2K], [full(h[b]) for b in B2K],
                                       [[] for b in B2K])
                    for b in B2K:
                        own.wait(ready[b])
                        f.state_ready.raise_now(dve, ("x", b))
                    if more_steps:
                        source_sums(i + 1)
                    for b in B2K:
                        sums(i, b, ready[b], first)

                if k == 0:
                    for q in LANES:
                        dve.wait_ge(s_dense[q], 16 * DSTEPS)
                    steps(dve, STEPS, sources1)
                if k == 1:
                    for b in B2K:
                        dve.wait_ge(sp_[0].stored[b], 16 * STEPS)
                        dve.wait_ge(sp_[0].kept[b], 16 * 2 * STEPS)
                    source_sums(0)
                    own.start()
                    sources2(0, first=True)
                    with dve.Fori(1, STEPS - 1) as i:
                        sources2(i)
                    sources2(STEPS - 1, more_steps=False)
                dve.wait_ge(s_span, k + 1)
                V.tensor_tensor(fix[:, 0:D], tp[0][:, 0:D], hsum[:, :], ALU.add).then_inc(s_fixpart, 1)
                dve.wait_ge(s_fixpart, k + 1)
                V.tensor_copy(fix[:, D:2 * D], tp[0][:, D:2 * D]).then_inc(s_fix, 1)
                dve.wait_ge(s_fix, k + 1)
                dve.sem_inc(s_phase, 1)

            own = Own(dve, tt.dve)

            descending = range(G - 1, -1, -1)

            def last_pass(i, first=False, more_steps=True):
                if i is not None:
                    own.step(i)
                j = 0 if i is None else i + 1

                def raised(signal, step, key, ins):
                    signal.raise_by(ins, key)
                    return signal.at(step, key)

                def take_update(half):
                    for b in B2K:
                        dve.wait_ge(*tt.second.at(i, (f"u{half}", b)))
                        if half == 0:
                            dve.wait_ge(*tt.acc_ready.at(i, ("a", b)))
                        at = slice(half * HB, half * HB + HB)
                        tt.taken.raise_by(V.tensor_tensor(acc[b][:, at, :], acc[b][:, at, :],
                                                          tp[b][:, 0:HB * D].rearrange("p (g d) -> p g d", d=D), ALU.add),
                                          (f"u{half}", b))

                if more_steps:
                    hd = layer_norm(own, tt, j, "d1", B2K, [full(gx[b]) for b in B2K], [full(xw[b]) for b in B2K],
                                    [[(tt.got_x[b], 16 * G * (j + 1))] for b in B2K],
                                    scale=lambda b: dis_d[:, bass.ds(tcol(j, b), G)])
                    for b in B2K:
                        own.wait(hd[b], (tt.load[b], 16 * 6 * (j + 1)))
                        hd[b] = own.did(V.tensor_tensor(full(xw[b]), full(xw[b]), full(a3[b]), ALU.add))
                    for b in B2K:
                        own.wait(hd[b])
                        dve.sem_inc(s_passed, 1)
                        tt.rows.raise_by(V.tensor_tensor(full(xw[b]), full(xw[b]), cols(dis_d, tcol(j, b)), ALU.mult), ("vd", b))
                if i is not None:
                    for b in B2K:
                        if not first:
                            dve.wait_ge(tt.kept[b], 16 * i)
                        prev = None if first and b == 0 else cc[1 - b][:, 0, 2 * D:3 * D]
                        mark = [tt.message.at(i, ("m1", b))] + ([tt.rows.at(i, ("agg", 0))] if b else [])
                        running(own, i, b, lambda g: cc[b][:, g, 2 * D:3 * D], prev, 0, lambda g: us[b][:, g, :], cont,
                                tcol(i, b), mark, descending, final=lambda ins: tt.rows.raise_by(ins, ("agg", b)))
                if more_steps:
                    if i is not None:
                        for b in B2K:
                            own.wait(tt.rows.at(i, ("agg", b)))
                    for b in B2K:
                        own.wait((tt.got_a[b], 16 * G * (j + 1)))
                        tt.rows.raise_by(V.tensor_tensor(full(us[b]), full(hin[b]), full(ga[b]), ALU.add), ("us", b))
                    for b in B2K:
                        own.wait(tt.rows.at(j, ("us", b)))
                        tt.ga_free.raise_now(dve, ("g", b))
                    xm, xs = {}, {}
                    for b in B2K:
                        dve.wait_ge(*tt.product.at(j, ("vd", b)))
                        xm[b] = raised(tt.taken, j, ("vd", b), V.tensor_tensor(flat(xd[b]), flat(gx[b]), mm[b][:, 0:W], ALU.add))
                    for b in B2K:
                        own.wait(xm[b])
                        tt.gx_free.raise_now(dve, ("g", b))
                    hd = layer_norm(own, tt, j, "d2", B2K, [full(xd[b]) for b in B2K], [full(h[b]) for b in B2K],
                                    [[xm[b]] for b in B2K])
                    for b in B2K:
                        own.wait(hd[b])
                        tt.rows.raise_by(V.tensor_tensor(full(h[b]), full(h[b]), full(a4[b]), ALU.add), ("ud", b))
                    for b in B2K:
                        dve.wait_ge(*tt.second.at(j, ("us", b)))
                        xs[b] = raised(tt.taken, j, ("us", b),
                                       V.tensor_tensor(flat(us[b]), flat(xin[b]), tp[b][:, 0:W], ALU.add))
                    for b in B2K:
                        own.wait(xs[b], tt.rows.at(j, ("ud", b)))
                        tt.in_free.raise_now(dve, ("x", b))
                    layer_norm(own, tt, j, "s3", B2K, [full(us[b]) for b in B2K],
                               [cc[b][:, :, 0:D] for b in B2K], [[xs[b]] for b in B2K])
                    for b in B2K:
                        dve.wait_ge(*tt.second.at(j, ("ud", b)))
                        xm[b] = raised(tt.taken, j, ("ud", b), V.tensor_tensor(flat(xd[b]), flat(xd[b]), tp[b][:, 0:W], ALU.add))
                    for b in B2K:
                        own.wait(xm[b])
                        dve.sem_inc(s_passed, 1)
                        xm[b] = own.did(V.tensor_tensor(full(xd[b]), full(xd[b]), cols(last, tcol(j, b)), ALU.mult))
                    ends = {}
                    for b in B2K:
                        prev = None if i is None and b == 0 else x3[1 - b][:, 0, :]
                        mark = [] if i is None else [tt.acc_ready.at(i, ("a", b))]
                        if b == 1:
                            mark.append(ends[0])
                        running(own, j, b, lambda g: x3[b][:, g, :], prev, 0, lambda g: xd[b][:, g, :], more, tcol(j, b),
                                [xm[b]] + mark, descending)
                        ends[b] = own.mark()
                        if b == 0 and i is not None:
                            take_update(0)

                if not more_steps:
                    take_update(0)
                if more_steps:
                    def h3_free(q):
                        if i is not None:
                            dve.wait_ge(*tt.turned.at(i, ("u1", q)))

                    layer_norm(own, tt, j, "d3", B2K, [full(x3[b]) for b in B2K], [cc[b][:, :, D:2 * D] for b in B2K],
                               [[ends[b]] for b in B2K], final=lambda q, ins: tt.rows.raise_by(ins, ("h3", q)),
                               before=h3_free)
                if i is None:
                    link(V.tensor_copy(brd[:, 0:D], x3[0][:, G - 1, :]))
                    dve.wait_ge(*tt.rows.at(0, ("h3", 0)))
                    link(V.tensor_copy(brd[:, D:2 * D], cc[0][:, G - 1, D:2 * D]))
                    own.start()
                else:
                    take_update(1)
                    for b in B2K:
                        dve.wait_ge(*tt.taken.at(i, ("u1", b)))
                        tt.o_ready.raise_now(dve, ("o", b))

            last_pass(None)
            last_pass(0, first=True)
            with dve.Fori(1, STEPS - 1) as i:
                last_pass(i)
            last_pass(STEPS - 1, more_steps=False)
            dve.wait_ge(s_span, 3)
            V.tensor_copy(brd[:, 2 * D:3 * D], tp[0][:, D:2 * D]).then_inc(s_border, 1)
            dve.wait_ge(s_bpe, 1)
            V.tensor_copy(bz[:, 0:P], tp[0][:, 0:P]).then_inc(s_border, 1)
            dve.wait_ge(s_bpe, 2)
            V.tensor_scalar(bz[:, P:2 * P], mm[0][:, 0:P], bcol[:, 2:3], 0.0, ALU.add, ALU.max).then_inc(s_border, 1)
            dve.wait_ge(s_border, 3)
            dve.sem_inc(s_border, 1)
            dve.wait_ge(s_bpe, 3)
            V.tensor_tensor(fix[:, 0:D], brd[:, 0:D], tp[1][:, 0:D], ALU.add).then_inc(s_border, 1)


_INS = ["x", "src", "dst", "edge_attr_32", "edge_weight", "L1_gnn_W", "L1_gnn_b", "L2_gnn_W1", "L2_gnn_b1",
        "L2_gnn_W2", "L2_gnn_b2", "L3_gnn_mW1", "L3_gnn_mb1", "L3_gnn_mW2", "L3_gnn_mb2", "L3_gnn_uW1",
        "L3_gnn_ub1", "L3_gnn_uW2", "L3_gnn_ub2"]


def kernel(**inputs):
    import numpy as np
    import concourse.bacc as bacc
    from concourse.bass_utils import run_bass_kernel_spmd

    nc = bacc.Bacc("TRN2", target_bir_lowering=False, num_devices=1)
    arrays, args = {}, []
    for name in _INS:
        a = np.asarray(inputs[name])
        a = np.ascontiguousarray(a.T if name in ("L2_gnn_W1", "L2_gnn_W2") else a)
        arrays[f"in_{name}"] = a
        args.append(nc.dram_tensor(f"in_{name}", a.shape, mybir.dt.from_np(a.dtype), kind="ExternalInput").ap())
    args.append(nc.dram_tensor("out_x", (N, D), F32, kind="ExternalOutput").ap())
    gnn(nc, *args)
    r = run_bass_kernel_spmd(nc, [arrays], core_ids=[0])
    return r.results[0]["out_x"]
```
